# Optimizing a Trainium2 kernel written in Bass

```python
import numpy as np
import jax
import jax.numpy as jnp

def _softmax(x, axis=-1):
    return jax.nn.softmax(x, axis=axis)

def _gelu(x):
    return jax.nn.gelu(x, approximate=True)

def _silu(x):
    return jax.nn.silu(x)

def _sigmoid(x):
    return jax.nn.sigmoid(x)

def _layernorm(x, axis=-1, eps=1e-05):
    m = jnp.mean(x, axis=axis, keepdims=True)
    v = jnp.var(x, axis=axis, keepdims=True)
    return (x - m) / jnp.sqrt(v + eps)

def _scatter_add(tgt, idx, src, axis=0):
    return tgt.at[idx].add(src)

def _segment_sum(src, seg, n):
    return jax.ops.segment_sum(src, seg, n)
kernel_name = 'mk_gnn_resnorm_d4_gnn_r8_596971'

def setup_inputs(seed: int=0):
    np.random.seed(seed)
    _w = jnp.asarray

    def _rec_inputs():
        import jax
        import jax.numpy as jnp
        _gk = jax.random.key(seed)
        x = -0.000202 + 1 * jax.random.normal(jax.random.fold_in(_gk, 1), (6250, 128), jnp.float32)
        _s = jax.random.randint(jax.random.fold_in(_gk, 2), (50000,), 0, 6250, jnp.int32)
        _d = jax.random.randint(jax.random.fold_in(_gk, 3), (50000,), 0, 6250, jnp.int32)
        _loop = jnp.arange(6250, dtype=jnp.int32)
        src = jnp.concatenate([_s, _d, _loop])
        dst = jnp.concatenate([_d, _s, _loop])
        _o = jnp.argsort(dst, stable=True)
        src = src[_o]
        dst = dst[_o]
        edge_weight = jax.random.uniform(jax.random.fold_in(_gk, 13), (106250,), jnp.float32, 0.0, 1)
        return (x, src, dst, edge_weight)
    x, src, dst, edge_weight = _rec_inputs()

    def _L0_gnn_setup():
        import jax, jax.numpy as jnp
        import numpy as np
        N_NODES = 6250
        N_EDGES = 100000
        D_IN = 128
        D_OUT = 128
        key = jax.random.key(seed)
        k1, k2, k3 = jax.random.split(key, 3)
        x = jax.random.normal(k1, (N_NODES, D_IN), dtype=jnp.float32)
        edge_index = jax.random.randint(k2, (2, N_EDGES), 0, N_NODES, dtype=jnp.int64)
        weight = jax.random.normal(k3, (2 * D_IN, D_OUT), dtype=jnp.float32) * (6.0 / (2 * D_IN + D_OUT)) ** 0.5
        return {'x': x, 'edge_index': edge_index, 'weight': weight}
    _L0_gnn_all = _L0_gnn_setup()
    _L0_gnn_in = {k: v for k, v in _L0_gnn_all.items() if k in ('weight',)}
    del _L0_gnn_all

    def _L1_gnn_setup():
        import jax, jax.numpy as jnp
        import numpy as np
        N = 12500
        E = 100000
        D = 128
        key = jax.random.key(seed)
        ks = jax.random.split(key, 12)
        s = lambda fan_in: 1.0 / np.sqrt(fan_in)
        return {'h': jax.random.normal(ks[0], (N, D), dtype=jnp.float32), 'w': jax.random.uniform(ks[1], (E,), dtype=jnp.float32), 'src': jax.random.randint(ks[2], (E,), 0, N, dtype=jnp.int32), 'dst': jax.random.randint(ks[3], (E,), 0, N, dtype=jnp.int32), 'W1': jax.random.uniform(ks[4], (2 * D + 1, D), jnp.float32, -s(2 * D + 1), s(2 * D + 1)), 'b1': jnp.zeros((D,), jnp.float32), 'W2': jax.random.uniform(ks[5], (D, D), jnp.float32, -s(D), s(D)), 'b2': jnp.zeros((D,), jnp.float32), 'U1': jax.random.uniform(ks[6], (2 * D, D), jnp.float32, -s(2 * D), s(2 * D)), 'c1': jnp.zeros((D,), jnp.float32), 'U2': jax.random.uniform(ks[7], (D, D), jnp.float32, -s(D), s(D)), 'c2': jnp.zeros((D,), jnp.float32)}
    _L1_gnn_all = _L1_gnn_setup()
    _L1_gnn_in = {k: v for k, v in _L1_gnn_all.items() if k in ('W1', 'b1', 'W2', 'b2', 'U1', 'c1', 'U2', 'c2')}
    del _L1_gnn_all

    def _L2_gnn_setup():
        import jax, jax.numpy as jnp
        import numpy as np
        N_NODES = 6250
        N_EDGES = 100000
        IN_CH = 128
        OUT_CH = 128
        MLP_HID = 64
        key = jax.random.key(seed)
        ks = jax.random.split(key, 8)
        x = jax.random.normal(ks[0], (N_NODES, IN_CH), dtype=jnp.float32)
        edge_index = jax.random.randint(ks[1], (2, N_EDGES), 0, N_NODES, dtype=jnp.int64)
        s1 = 1.0 / np.sqrt(2 * IN_CH)
        mlp_w1 = jax.random.uniform(ks[2], (2 * IN_CH, MLP_HID), jnp.float32, -s1, s1)
        mlp_b1 = jax.random.uniform(ks[3], (MLP_HID,), jnp.float32, -s1, s1)
        s2 = 1.0 / np.sqrt(MLP_HID)
        mlp_w2 = jax.random.uniform(ks[4], (MLP_HID, 1), jnp.float32, -s2, s2)
        mlp_b2 = jax.random.uniform(ks[5], (1,), jnp.float32, -s2, s2)
        s3 = 1.0 / np.sqrt(IN_CH)
        conv_w = jax.random.uniform(ks[6], (IN_CH, OUT_CH), jnp.float32, -s3, s3)
        conv_b = jnp.zeros((OUT_CH,), jnp.float32)
        return {'x': x, 'edge_index': edge_index, 'mlp_w1': mlp_w1, 'mlp_b1': mlp_b1, 'mlp_w2': mlp_w2, 'mlp_b2': mlp_b2, 'conv_w': conv_w, 'conv_b': conv_b}
    _L2_gnn_all = _L2_gnn_setup()
    _L2_gnn_in = {k: v for k, v in _L2_gnn_all.items() if k in ('mlp_w1', 'mlp_b1', 'mlp_w2', 'mlp_b2', 'conv_w', 'conv_b')}
    del _L2_gnn_all

    def _L3_gnn_setup():
        import jax, jax.numpy as jnp
        import numpy as np
        N = 6250
        E = 100000
        IN_DIM = 128
        HEADS = 4
        OUT_C = 32
        HC = HEADS * OUT_C
        key = jax.random.key(seed)
        ks = jax.random.split(key, 12)
        x = jax.random.normal(ks[0], (N, IN_DIM), dtype=jnp.float32)
        edge_index = jax.random.randint(ks[1], (2, E), 0, N, dtype=jnp.int64)
        s = 1.0 / np.sqrt(IN_DIM)
        Wq = jax.random.normal(ks[2], (IN_DIM, HC), dtype=jnp.float32) * s
        bq = jnp.zeros((HC,), dtype=jnp.float32)
        Wk = jax.random.normal(ks[3], (IN_DIM, HC), dtype=jnp.float32) * s
        bk = jnp.zeros((HC,), dtype=jnp.float32)
        Wv = jax.random.normal(ks[4], (IN_DIM, HC), dtype=jnp.float32) * s
        bv = jnp.zeros((HC,), dtype=jnp.float32)
        Wskip = jax.random.normal(ks[5], (IN_DIM, HC), dtype=jnp.float32) * s
        bskip = jnp.zeros((HC,), dtype=jnp.float32)
        Wbeta = jax.random.normal(ks[6], (3 * HC, 1), dtype=jnp.float32) * (1.0 / np.sqrt(3 * HC))
        return {'x': x, 'edge_index': edge_index, 'Wq': Wq, 'bq': bq, 'Wk': Wk, 'bk': bk, 'Wv': Wv, 'bv': bv, 'Wskip': Wskip, 'bskip': bskip, 'Wbeta': Wbeta}
    _L3_gnn_all = _L3_gnn_setup()
    _L3_gnn_in = {k: v for k, v in _L3_gnn_all.items() if k in ('Wq', 'bq', 'Wk', 'bk', 'Wv', 'bv', 'Wskip', 'bskip', 'Wbeta')}
    del _L3_gnn_all
    return {'x': x, 'src': src, 'dst': dst, 'edge_weight': edge_weight, 'L0_gnn_weight': _L0_gnn_in['weight'], 'L1_gnn_W1': _L1_gnn_in['W1'], 'L1_gnn_b1': _L1_gnn_in['b1'], 'L1_gnn_W2': _L1_gnn_in['W2'], 'L1_gnn_b2': _L1_gnn_in['b2'], 'L1_gnn_U1': _L1_gnn_in['U1'], 'L1_gnn_c1': _L1_gnn_in['c1'], 'L1_gnn_U2': _L1_gnn_in['U2'], 'L1_gnn_c2': _L1_gnn_in['c2'], 'L2_gnn_mlp_w1': _L2_gnn_in['mlp_w1'], 'L2_gnn_mlp_b1': _L2_gnn_in['mlp_b1'], 'L2_gnn_mlp_w2': _L2_gnn_in['mlp_w2'], 'L2_gnn_mlp_b2': _L2_gnn_in['mlp_b2'], 'L2_gnn_conv_w': _L2_gnn_in['conv_w'], 'L2_gnn_conv_b': _L2_gnn_in['conv_b'], 'L3_gnn_Wq': _L3_gnn_in['Wq'], 'L3_gnn_bq': _L3_gnn_in['bq'], 'L3_gnn_Wk': _L3_gnn_in['Wk'], 'L3_gnn_bk': _L3_gnn_in['bk'], 'L3_gnn_Wv': _L3_gnn_in['Wv'], 'L3_gnn_bv': _L3_gnn_in['bv'], 'L3_gnn_Wskip': _L3_gnn_in['Wskip'], 'L3_gnn_bskip': _L3_gnn_in['bskip'], 'L3_gnn_Wbeta': _L3_gnn_in['Wbeta']}

def reference(x, src, dst, edge_weight, L0_gnn_weight, L1_gnn_W1, L1_gnn_b1, L1_gnn_W2, L1_gnn_b2, L1_gnn_U1, L1_gnn_c1, L1_gnn_U2, L1_gnn_c2, L2_gnn_mlp_w1, L2_gnn_mlp_b1, L2_gnn_mlp_w2, L2_gnn_mlp_b2, L2_gnn_conv_w, L2_gnn_conv_b, L3_gnn_Wq, L3_gnn_bq, L3_gnn_Wk, L3_gnn_bk, L3_gnn_Wv, L3_gnn_bv, L3_gnn_Wskip, L3_gnn_bskip, L3_gnn_Wbeta):
    import jax
    import jax.numpy as jnp

    def _L0_gnn_ref(x, edge_index, weight):
        import jax, jax.numpy as jnp
        import numpy as np
        N_NODES = 6250
        N_EDGES = 100000
        D_IN = 128
        D_OUT = 128
        src = edge_index[0]
        dst = edge_index[1]
        n = x.shape[0]
        msgs = x[src]
        agg_sum = jax.ops.segment_sum(msgs, dst, num_segments=n)
        counts = jax.ops.segment_sum(jnp.ones((src.shape[0],), dtype=x.dtype), dst, num_segments=n)
        agg_mean = agg_sum / jnp.maximum(counts, 1.0)[:, None]
        h = jnp.concatenate([x, agg_mean], axis=-1)
        return h @ weight

    def _L1_gnn_ref(h, w, src, dst, W1, b1, W2, b2, U1, c1, U2, c2):
        import jax, jax.numpy as jnp
        import numpy as np
        N = 12500
        E = 100000
        D = 128
        n = h.shape[0]
        msg_in = jnp.concatenate([h[src], h[dst], w[:, None]], axis=1)
        msg = jax.nn.relu(msg_in @ W1 + b1) @ W2 + b2
        agg = jax.ops.segment_max(msg, dst, num_segments=n)
        deg = jax.ops.segment_sum(jnp.ones((dst.shape[0],), jnp.int32), dst, num_segments=n)
        agg = jnp.where((deg > 0)[:, None], agg, jnp.zeros((), h.dtype))
        upd_in = jnp.concatenate([h, agg], axis=1)
        return jax.nn.relu(upd_in @ U1 + c1) @ U2 + c2

    def _L2_gnn_ref(x, edge_index, mlp_w1, mlp_b1, mlp_w2, mlp_b2, conv_w, conv_b):
        import jax, jax.numpy as jnp
        import numpy as np
        N_NODES = 6250
        N_EDGES = 100000
        IN_CH = 128
        OUT_CH = 128
        MLP_HID = 64
        n = x.shape[0]
        row, col = (edge_index[0], edge_index[1])
        edge_feat = jnp.concatenate([x[row], x[col]], axis=-1)
        h = jax.nn.gelu(edge_feat @ mlp_w1 + mlp_b1, approximate=False)
        edge_weight = jax.nn.sigmoid(h @ mlp_w2 + mlp_b2)[:, 0]
        loop = jnp.arange(n, dtype=row.dtype)
        row_f = jnp.concatenate([row, loop])
        col_f = jnp.concatenate([col, loop])
        ew_f = jnp.concatenate([edge_weight, jnp.ones((n,), x.dtype)])
        deg = jax.ops.segment_sum(ew_f, col_f, num_segments=n)
        dinv = jnp.where(deg > 0, jax.lax.rsqrt(deg), 0.0)
        norm = dinv[row_f] * ew_f * dinv[col_f]
        xt = x @ conv_w
        msg = xt[row_f] * norm[:, None]
        out = jax.ops.segment_sum(msg, col_f, num_segments=n)
        return out + conv_b

    def _L3_gnn_ref(x, edge_index, Wq, bq, Wk, bk, Wv, bv, Wskip, bskip, Wbeta):
        import jax, jax.numpy as jnp
        import numpy as np
        N = 6250
        E = 100000
        IN_DIM = 128
        HEADS = 4
        OUT_C = 32
        HC = HEADS * OUT_C
        n = x.shape[0]
        src = edge_index[0]
        dst = edge_index[1]
        q = (x @ Wq + bq).reshape(n, HEADS, OUT_C)
        k = (x @ Wk + bk).reshape(n, HEADS, OUT_C)
        v = (x @ Wv + bv).reshape(n, HEADS, OUT_C)
        score = jnp.einsum('ehc,ehc->eh', q[dst], k[src]) / jnp.sqrt(jnp.asarray(OUT_C, dtype=x.dtype))
        m = jax.ops.segment_max(score, dst, num_segments=n)
        m = jnp.where(jnp.isfinite(m), m, 0.0)
        p = jnp.exp(score - m[dst])
        denom = jax.ops.segment_sum(p, dst, num_segments=n)
        alpha = p / jnp.maximum(denom[dst], 1e-16)
        msg = v[src] * alpha[:, :, None]
        out = jax.ops.segment_sum(msg, dst, num_segments=n)
        out = out.reshape(n, HC)
        x_r = x @ Wskip + bskip
        beta = jax.nn.sigmoid(jnp.concatenate([out, x_r, out - x_r], axis=-1) @ Wbeta)
        return beta * x_r + (1.0 - beta) * out
    edge_index = jnp.stack([src, dst])
    x = _layernorm(x + _L0_gnn_ref(x, edge_index, L0_gnn_weight), axis=-1)
    x = _layernorm(x + _L1_gnn_ref(x, edge_weight, src, dst, L1_gnn_W1, L1_gnn_b1, L1_gnn_W2, L1_gnn_b2, L1_gnn_U1, L1_gnn_c1, L1_gnn_U2, L1_gnn_c2), axis=-1)
    x = _layernorm(x + _L2_gnn_ref(x, edge_index, L2_gnn_mlp_w1, L2_gnn_mlp_b1, L2_gnn_mlp_w2, L2_gnn_mlp_b2, L2_gnn_conv_w, L2_gnn_conv_b), axis=-1)
    x = _layernorm(x + _L3_gnn_ref(x, edge_index, L3_gnn_Wq, L3_gnn_bq, L3_gnn_Wk, L3_gnn_bk, L3_gnn_Wv, L3_gnn_bv, L3_gnn_Wskip, L3_gnn_bskip, L3_gnn_Wbeta), axis=-1)
    return x

_drawn_inputs = setup_inputs


def setup_inputs(seed=0):
    import zlib

    import numpy as np

    out = dict(_drawn_inputs(seed))
    spreads = {'L1_gnn_b1': (0.0, 0.8),
     'L1_gnn_b2': (0.0, 0.36),
     'L1_gnn_c1': (0.0, 0.1),
     'L1_gnn_c2': (0.0, 0.1),
     'L2_gnn_conv_b': (0.0, 0.1),
     'L3_gnn_bq': (0.0, 0.705),
     'L3_gnn_bk': (0.0, 2.0),
     'L3_gnn_bv': (0.0, 0.1),
     'L3_gnn_bskip': (0.0, 0.1)}
    factors = {'edge_weight': 200.0, 'L2_gnn_mlp_w1': 5.279, 'L2_gnn_mlp_b1': 8.0, 'L2_gnn_mlp_w2': 4.758}
    for name, (base, spread) in spreads.items():
        noise = np.random.default_rng([zlib.crc32(name.encode()), seed]).standard_normal(out[name].shape)
        drawn = base * np.exp(spread * noise) if base else spread * noise
        out[name] = jnp.asarray(drawn.astype(out[name].dtype))
    for name, factor in factors.items():
        out[name] = (out[name] * factor).astype(out[name].dtype)
    return out
```

```python
from contextlib import ExitStack

import numpy as np

import concourse.bass as bass
from concourse import mybir

F32 = mybir.dt.float32
I32 = mybir.dt.int32
BF16 = mybir.dt.bfloat16
ALU = mybir.AluOpType
ACT = mybir.ActivationFunctionType
AX = mybir.AxisListType.X

P = 128
N, E, D = 6250, 106250, 128
HID = 64
HEADS, HEAD = 4, 32
BT = 4
BE = BT * P
SLOTS = 4
TILES = -(-E // (P * BT * SLOTS)) * BT * SLOTS
BATCHES = TILES // BT
EP = TILES * P
NT = -(-N // (P * BT)) * BT
NP = NT * P
NB = NT // BT
NSLOTS = 2
FAR = -3.0e38
EPS = 1e-5
W3 = D + HEADS


def need(eng, sem, n):
    eng.wait_ge(sem, n + 1)


def room(eng, sem, n, depth):
    if isinstance(n, int) and n < depth:
        return
    eng.wait_ge(sem, n - depth + 1)


def landed(eng, sems, k, r, dmas=1):
    eng.wait_ge(sems[k], 16 * dmas * (r + 1))


def stored(eng, sems, k, r, dmas=1):
    if isinstance(r, int) and r < 1:
        return
    eng.wait_ge(sems[k], 16 * dmas * r)


def pipeline(eng, count, slots, stages):
    lag_max = max(lag for lag, _ in stages)
    head = -(-(lag_max + slots) // slots)
    rounds = count // slots

    def step(r0, k0, peeled):
        for lag, f in stages:
            q = k0 - lag
            k, r = q % slots, r0 + q // slots
            n = r * slots + k
            if peeled and not 0 <= n < count:
                continue
            f(n, k, r)

    for s in range(min(head, rounds) * slots):
        step(s // slots, s % slots, True)
    if rounds > head:
        with eng.Fori(head, rounds) as i:
            for k0 in range(slots):
                step(i, k0, False)
    for s in range(max(rounds, 0) * slots, count + lag_max):
        step(s // slots, s % slots, True)


class Phase:

    def __init__(self, nc, name):
        self.nc, self.name, self.sems, self.ctx = nc, name, [], ExitStack()

    def __enter__(self):
        return self

    def sb(self, name, shape, dtype=F32):
        return self.ctx.enter_context(self.nc.sbuf_tensor(f"{self.name}_{name}", shape, dtype))

    def ps(self, name, shape=(P, BE), dtype=F32):
        return self.ctx.enter_context(self.nc.psum_tensor(f"{self.name}_{name}", list(shape), dtype))

    def sem(self, name):
        s = self.nc.alloc_semaphore(name=f"{self.name}_{name}")
        self.sems.append(s)
        return s

    def slot_sems(self, name, count):
        return [self.sem(f"{name}{k}") for k in range(count)]

    def block(self):
        return self.ctx.enter_context(self.nc.Block())

    def __exit__(self, *args):
        self.ctx.close()
        self.nc.clear_and_free_semaphores(self.sems)
        self.nc.all_engine_barrier()


class Chain:

    def __init__(self, eng, sem, per=0):
        self.eng, self.sem, self.per, self.j, self.n = eng, sem, per, 0, 0

    def item(self, n):
        assert self.j in (0, self.per), (self.j, self.per)
        self.n, self.j = n, 0

    def __call__(self, ins):
        self.j += 1
        ins.then_inc(self.sem, 1)
        self.eng.wait_ge(self.sem, self.n * self.per + self.j)


def rows(tile):
    return tile.rearrange("p a b -> p (a b)")


def cols(t):
    return slice(t * P, (t + 1) * P)


def build(nc, d, out):
    with ExitStack() as ctx:
        def sb(name, shape, dtype=F32):
            return ctx.enter_context(nc.sbuf_tensor(name, shape, dtype))

        def dram(name, shape, dtype=F32):
            return nc.dram_tensor(name, shape, dtype, kind="Internal").ap()

        g = {}
        g["ident"] = sb("ident", [P, P])
        g["ones"] = sb("ones", [1, P])
        g["src"] = sb("src", [P, TILES + SLOTS * BT], I32)
        g["x"] = sb("x", [P, NT, D])
        g["xT"] = sb("xT", [P, NT * P])
        g["last"] = sb("last", [P, NT], I32)
        g["first"] = sb("first", [P, NT], I32)
        g["last_e"] = sb("last_e", [P, NT], I32)
        g["has"] = sb("has", [P, NT])
        g["mean"] = sb("mean", [P, NT])
        g["same_c"] = sb("same_c", [P, TILES], BF16)
        weights = {}
        for name in ("W0x", "W0a", "W1s", "W1d", "W2", "U1x", "U1a", "U2", "conv", "Wq", "Wskip"):
            weights[name] = sb("w_" + name, [P, D])
        weights["M1s"] = sb("w_M1s", [P, HID])
        weights["M1d"] = sb("w_M1d", [P, HID])
        weights["M2"] = sb("w_M2", [HID, 1])
        weights["Wkv"] = sb("w_Wkv", [P, 2 * D])
        rowsb = {n: sb("r_" + n, [1, w]) for n, w in (("b1", D), ("c2", D), ("m1", HID), ("bq", D), ("bkv", 2 * D), ("bskip", D))}
        wide = {n: sb("b_" + n, [P, w]) for n, w in (("W1w", D), ("b2", D), ("conv_b", D), ("beta", 3 * D), ("m2", 1))}
        g["c1"] = sb("c1", [P, 1])
        g["w"], g["row"], g["wide"] = weights, rowsb, wide
        g["same"] = dram("same", [EP], BF16)
        g["fresh"] = dram("fresh", [EP], BF16)
        g["ends"] = dram("ends", [EP], BF16)
        g["run"] = dram("run", [EP, D])
        g["run3"] = dram("run3", [EP, W3])
        g["seed"] = dram("seed", [EP, D])
        g["tab"] = dram("tab", [NP, D])
        g["tab_h"] = dram("tab_h", [NP, HID])
        g["tab_kv"] = dram("tab_kv", [NP, 2 * D])
        g["off"] = dram("off", [NP + 1, 1], I32)
        g["ew"] = dram("ew", [EP, 1])
        g["xt"] = sb("xt", [P, NT, D])
        g["dinv"] = sb("dinv", [P, NT])

        setup(nc, d, g)
        edges_sum(nc, g, "L0", d["x"], None)
        nodes(nc, g, 0, out)
        edges_max(nc, d, g)
        nodes(nc, g, 1, out)
        ew = sb("ew_sb", [P, TILES])
        edges_gate(nc, g, ew)
        degrees(nc, g, ew)
        edges_sum(nc, g, "L2", g["tab"], ew)
        nodes(nc, g, 2, out)
        edges_attention(nc, g)
        nodes(nc, g, 3, out)


def setup(nc, d, g):
    w, row, wide = g["w"], g["row"], g["wide"]
    loads = [
        (g["src"][:, :], d["src"]), (g["x"][:, :, :], d["x"].rearrange("(p t) f -> p t f", p=P)),
        (w["W0x"][:, :], d["L0_gnn_weight"][0:D, :]), (w["W0a"][:, :], d["L0_gnn_weight"][D:2 * D, :]),
        (w["W1s"][:, :], d["L1_gnn_W1"][0:D, :]), (w["W1d"][:, :], d["L1_gnn_W1"][D:2 * D, :]),
        (wide["W1w"][:, :], d["L1_gnn_W1"][2 * D:2 * D + 1, :].to_broadcast([P, D])),
        (w["W2"][:, :], d["L1_gnn_W2"]),
        (w["U1x"][:, :], d["L1_gnn_U1"][0:D, :]), (w["U1a"][:, :], d["L1_gnn_U1"][D:2 * D, :]),
        (w["U2"][:, :], d["L1_gnn_U2"]),
        (w["M1s"][:, :], d["L2_gnn_mlp_w1"][0:D, :]), (w["M1d"][:, :], d["L2_gnn_mlp_w1"][D:2 * D, :]),
        (w["M2"][:, :], d["L2_gnn_mlp_w2"]), (w["conv"][:, :], d["L2_gnn_conv_w"]),
        (w["Wkv"][:, 0:D], d["L3_gnn_Wk"]), (w["Wkv"][:, D:2 * D], d["L3_gnn_Wv"]),
        (w["Wq"][:, :], d["L3_gnn_Wq"]), (w["Wskip"][:, :], d["L3_gnn_Wskip"]),
        (g["c1"][:, :], d["L1_gnn_c1"].rearrange("(p a) -> p a", a=1)),
    ]
    line = lambda a: a.rearrange("(a n) -> a n", a=1)
    loads += [(row["b1"][:, :], line(d["L1_gnn_b1"])), (row["c2"][:, :], line(d["L1_gnn_c2"])),
              (row["m1"][:, :], line(d["L2_gnn_mlp_b1"])), (row["bq"][:, :], line(d["L3_gnn_bq"])),
              (row["bkv"][:, 0:D], line(d["L3_gnn_bk"])), (row["bkv"][:, D:2 * D], line(d["L3_gnn_bv"])),
              (row["bskip"][:, :], line(d["L3_gnn_bskip"]))]
    loads += [(wide["b2"][:, :], line(d["L1_gnn_b2"]).to_broadcast([P, D])),
              (wide["conv_b"][:, :], line(d["L2_gnn_conv_b"]).to_broadcast([P, D])),
              (wide["m2"][:, :], line(d["L2_gnn_mlp_b2"]).to_broadcast([P, 1]))]
    loads += [(wide["beta"][:, j * D:(j + 1) * D],
               d["L3_gnn_Wbeta"][j * D:(j + 1) * D, :].rearrange("n a -> a n").to_broadcast([P, D])) for j in range(3)]
    chunk = lambda a: a.rearrange("(p i) -> p i", p=P)
    with Phase(nc, "set") as ph:
        dst = [ph.sb(f"dst{j}", [P, TILES], I32) for j in range(3)]
        heads = ph.sb("heads", [P, TILES], I32)
        far = [ph.sb(f"far{j}", [P, TILES], BF16) for j in range(2)]
        node = ph.sb("node", [P, NT])
        flag = ph.sb("flag", [P, BT, TILES], BF16)
        tiles = ph.sb("tiles", [P, NT])
        tile_i = ph.sb("tile_i", [P, NT], I32)
        inside = ph.sb("inside", [P, NT])
        drow = [ph.sb(f"drow{k}", [P, BT, P], I32) for k in range(NSLOTS)]
        le = ph.sb("le", [P, BT, P])
        tmp = [ph.sb(f"tmp{j}", [P, NT]) for j in range(4)]
        ti = [ph.sb(f"ti{j}", [P, NT], I32) for j in range(4)]
        idx = [ph.sb(f"idx{k}", [P, BT], I32) for k in range(NSLOTS)]
        zero = ph.sb("zero", [P, 16 * D])
        pT = [ph.ps(f"pT{k}") for k in range(2)]
        s_dst, s_w, s_v, s_id, s_mask, s_tiles, s_off, s_back = (ph.sem(n) for n in
            ("dst", "w", "v", "id", "mask", "tiles", "off", "back"))
        s_zero, s_fill, s_tp, s_tc, s_cmp, s_ix, s_go, s_link = (ph.sem(n) for n in
            ("zero", "fill", "tp", "tc", "cmp", "ix", "go", "link"))
        s_row, s_xs = ph.slot_sems("row", NSLOTS), ph.slot_sems("xs", NSLOTS)
        xs = [ph.sb(f"xs{k}", [P, BT, D]) for k in range(NSLOTS)]
        block = ph.block()

        @block.sync
        def _(sp):
            for j in range(3):
                sp.dma_start(dst[j][:, :], chunk(d["dst"][j:j + EP])).then_inc(s_dst, 16)
            sp.dma_start(heads[:, :], line(d["heads"]).to_broadcast([P, TILES])).then_inc(s_dst, 16)
            for to, a in loads:
                sp.dma_start(to, a).then_inc(s_w, 16)

            def load_x(n, k, r):
                room(sp, s_tp, n, NSLOTS)
                sp.dma_start(xs[k][:, :, :], d["x"].rearrange("(p t) f -> p t f", p=P)[:, bass.ds(n * BT, BT), :]).then_inc(s_xs[k], 16)
            pipeline(sp, NB, NSLOTS, [(0, load_x)])
            sp.wait_ge(s_mask, 1)
            sp.dma_start(chunk(g["same"]), g["same_c"][:, :]).then_inc(s_w, 16)
            sp.wait_ge(s_mask, 2)
            sp.dma_start(chunk(g["fresh"]), far[0][:, :]).then_inc(s_w, 16)
            sp.wait_ge(s_mask, 3)
            sp.dma_start(chunk(g["ends"]), far[1][:, :]).then_inc(s_w, 16)
            sp.wait_ge(s_off, 1)
            sp.dma_start(g["off"][1:NP + 1, :].rearrange("(p t) a -> p (t a)", p=P), ti[0][:, :]).then_inc(s_back, 16)
            sp.dma_start(g["off"][0:1, :], ti[3][0:1, 0:1]).then_inc(s_back, 16)
            sp.wait_ge(s_back, 32)
            sp.dma_start(ti[1][:, :], g["off"][0:NP, :].rearrange("(p t) a -> p (t a)", p=P)).then_inc(s_back, 16)
            sp.wait_ge(s_w, 16 * (len(loads) + 3))

        @block.scalar
        def _(act):
            act.wait_ge(s_zero, 1)
            seed = g["seed"].rearrange("(p c t) f -> c p (t f)", p=P, t=16)
            for c in range(TILES // 16):
                act.dma_start(seed[c], zero[:, :]).then_inc(s_fill, 16)

            def copy(n, k, r):
                need(act, s_tp, n)
                act.activation(g["xT"][:, bass.ds(n * BE, BE)], pT[k][:, :], ACT.Copy).then_inc(s_tc, 1)
            pipeline(act, NB, NSLOTS, [(0, copy)])
            act.wait_ge(s_fill, 16 * (TILES // 16))

        @block.tensor
        def _(pe):
            pe.wait_ge(s_id, 2)

            def turn(n, k, r):
                landed(pe, s_xs, k, r)
                room(pe, s_tc, n, NSLOTS)
                for t in range(BT):
                    m = pe.transpose(pT[k][:, cols(t)], xs[k][:, t, :], g["ident"][:, :])
                m.then_inc(s_tp, 1)
            pipeline(pe, NB, NSLOTS, [(0, turn)])

        @block.gpsimd
        def _(gp):
            gp.memset(zero[:, :], 0.0).then_inc(s_zero, 1)
            gp.memset(g["ident"][:, :], 0.0).then_inc(s_id, 1)
            gp.wait_ge(s_id, 1)
            gp.affine_select(out=g["ident"][:, :], in_=g["ident"][:, :], compare_op=ALU.not_equal, fill=1.0, base=0,
                             pattern=[[-1, P]], channel_multiplier=1).then_inc(s_id, 1)
            gp.iota(ti[2][:, :], [[1, NT]], base=0, channel_multiplier=NT).then_inc(s_id, 1)
            gp.wait_ge(s_tiles, 1)

            def fetch(n, k, r):
                room(gp, s_cmp, n, NSLOTS)
                gp.tensor_copy(idx[k][:, :], tile_i[:, bass.ds(n * BT, BT)]).then_inc(s_ix, 1)
                need(gp, s_ix, n)
                gp.sem_inc(s_go, 1)
                for t in range(BT):
                    gp.indirect_dma_start(out=drow[k][:, t, :], out_offset=None, in_=d["dst_rows"],
                                          in_offset=bass.IndirectOffsetOnAxis(ap=idx[k][:, t:t + 1], axis=0)).then_inc(s_row[k], 16)
            pipeline(gp, NB, NSLOTS, [(0, fetch)])

        @block.vector
        def _(v):
            link = Chain(v, s_link)
            v.memset(g["ones"][:, :], 1.0)
            v.memset(ti[3][:, :], 0)
            v.wait_ge(s_dst, 64)
            v.tensor_tensor(g["same_c"][:, :], dst[1][:, :], dst[0][:, :], ALU.is_equal).then_inc(s_mask, 1)
            link(v.tensor_tensor(far[0][:, :], dst[1][:, :], dst[0][:, :], ALU.not_equal))
            v.tensor_scalar(far[0][:, :], far[0][:, :], FAR, None, ALU.mult).then_inc(s_mask, 1)
            link(v.tensor_tensor(far[1][:, :], dst[1][:, :], dst[2][:, :], ALU.not_equal))
            v.tensor_scalar(far[1][:, :], far[1][:, :], FAR, None, ALU.mult).then_inc(s_mask, 1)
            v.wait_ge(s_id, 3)
            link(v.tensor_copy(node[:, :], ti[2][:, :]))
            count = Chain(v, s_v, 2)

            def tiles_upto(n, k, r):
                count.item(n)
                count(v.tensor_tensor(flag[:, :, :], heads[:, :].unsqueeze(1).to_broadcast([P, BT, TILES]),
                                      node[:, bass.ds(n * BT, BT)].unsqueeze(2).to_broadcast([P, BT, TILES]), ALU.is_le))
                count(v.tensor_reduce(tiles[:, bass.ds(n * BT, BT)], flag[:, :, :], AX, ALU.add))
            pipeline(v, NB, NSLOTS, [(0, tiles_upto)])
            link(v.tensor_scalar(tiles[:, :], tiles[:, :], -1.0, 0.0, ALU.add, ALU.max))
            v.tensor_copy(tile_i[:, :], tiles[:, :]).then_inc(s_tiles, 1)

            def edges_upto(n, k, r):
                count.item(n + NB)
                landed(v, s_row, k, r, BT)
                count(v.tensor_tensor(le[:, :, :], drow[k][:, :, :],
                                      node[:, bass.ds(n * BT, BT)].unsqueeze(2).to_broadcast([P, BT, P]), ALU.is_le))
                count(v.tensor_reduce(inside[:, bass.ds(n * BT, BT)], le[:, :, :], AX, ALU.add))
                v.sem_inc(s_cmp, 1)
            pipeline(v, NB, NSLOTS, [(0, edges_upto)])
            off = tmp[0]
            link(v.scalar_tensor_tensor(off[:, :], tiles[:, :], float(P), inside[:, :], ALU.mult, ALU.add))
            v.tensor_copy(ti[0][:, :], off[:, :]).then_inc(s_off, 1)
            link(v.tensor_scalar(tmp[1][:, :], off[:, :], -1.0, 0.0, ALU.add, ALU.max))
            link(v.tensor_copy(g["last_e"][:, :], tmp[1][:, :]))
            link(v.tensor_scalar(inside[:, :], inside[:, :], -1.0, 0.0, ALU.add, ALU.max))
            link(v.scalar_tensor_tensor(tmp[1][:, :], inside[:, :], float(TILES), tiles[:, :], ALU.mult, ALU.add))
            link(v.tensor_copy(g["last"][:, :], tmp[1][:, :]))
            v.wait_ge(s_back, 48)
            link(v.tensor_copy(tmp[2][:, :], ti[1][:, :]))
            link(v.tensor_tensor(tmp[3][:, :], off[:, :], tmp[2][:, :], ALU.subtract))
            link(v.tensor_scalar(g["has"][:, :], tmp[3][:, :], 0.0, None, ALU.is_gt))
            link(v.tensor_scalar(tmp[3][:, :], tmp[3][:, :], 1.0, None, ALU.max))
            link(v.reciprocal(tmp[2][:, :], tmp[3][:, :]))
            link(v.tensor_tensor(g["mean"][:, :], tmp[2][:, :], g["has"][:, :], ALU.mult))
            link(v.tensor_scalar(ti[2][:, :], ti[1][:, :], 7, None, ALU.arith_shift_right))
            link(v.tensor_scalar(ti[1][:, :], ti[1][:, :], P - 1, None, ALU.bitwise_and))
            link(v.tensor_copy(tmp[1][:, :], ti[1][:, :]))
            link(v.tensor_copy(tmp[2][:, :], ti[2][:, :]))
            link(v.scalar_tensor_tensor(tmp[1][:, :], tmp[1][:, :], float(TILES), tmp[2][:, :], ALU.mult, ALU.add))
            link(v.tensor_scalar(tmp[1][:, :], tmp[1][:, :], float(-EP), None, ALU.add))
            link(v.tensor_tensor(tmp[1][:, :], tmp[1][:, :], g["has"][:, :], ALU.mult))
            link(v.tensor_scalar(tmp[1][:, :], tmp[1][:, :], float(EP), None, ALU.add))
            link(v.tensor_copy(g["first"][:, :], tmp[1][:, :]))


def edge_buffers(ph, width):
    gath = [ph.sb(f"gath{k}", [P, BT, width]) for k in range(SLOTS)]
    idx = [ph.sb(f"idx{k}", [P, BT], I32) for k in range(SLOTS)]
    return gath, idx, ph.slot_sems("gath", SLOTS), ph.sem("idx"), ph.sem("go")


def gatherer(gp, table, gath, idx, s_gath, s_idx, s_go, s_free):
    def gather(n, k, r):
        need(gp, s_idx, n)
        room(gp, s_free, n, SLOTS)
        gp.sem_inc(s_go, 1)
        for t in range(BT):
            gp.indirect_dma_start(out=gath[k][:, t, :], out_offset=None, in_=table,
                                  in_offset=bass.IndirectOffsetOnAxis(ap=idx[k][:, t:t + 1], axis=0)).then_inc(s_gath[k], 16)
    pipeline(gp, BATCHES, SLOTS, [(0, gather)])


def indexer(v, g, idx, s_idx, s_gath):
    for k in range(SLOTS):
        v.tensor_copy(idx[k][:, :], g["src"][:, k * BT:(k + 1) * BT]).then_inc(s_idx, 1)

    def ahead(n, k, r):
        landed(v, s_gath, k, r, BT)
        v.tensor_copy(idx[k][:, :], g["src"][:, bass.ds((n + SLOTS) * BT, BT)]).then_inc(s_idx, 1)
    return ahead


def start_of(acc, n, k):
    return 0.0 if isinstance(n, int) and n == 0 else acc[(k - 1) % len(acc)][:, BE - 1:BE]


def edges_sum(nc, g, name, table, ew):
    with Phase(nc, name) as ph:
        gath, idx, s_gath, s_idx, s_go = edge_buffers(ph, D)
        mask = [ph.sb(f"mask{k}", [P, BE], BF16) for k in range(SLOTS)]
        acc = [ph.sb(f"acc{k}", [P, BE]) for k in range(SLOTS)]
        back = [ph.sb(f"back{k}", [P, BT, D]) for k in range(SLOTS)]
        scaled = [ph.sb(f"scaled{k}", [P, BT, D]) for k in range(2)] if ew is not None else None
        pT = [ph.ps(f"pT{k}") for k in range(2)]
        pB = [ph.ps(f"pB{k}") for k in range(2)]
        s_turn, s_scan, s_ret, s_back, s_scale = (ph.sem(n) for n in ("turn", "scan", "ret", "back", "scale"))
        s_mask, s_out = ph.slot_sems("mask", SLOTS), ph.slot_sems("out", SLOTS)
        run = g["run"].rearrange("(p t) f -> p t f", p=P)
        s_free = s_turn if ew is None else s_scale
        block = ph.block()

        @block.sync
        def _(sp):
            def load(n, k, r):
                room(sp, s_scan, n, SLOTS)
                sp.dma_start(mask[k][:, :], g["same"][bass.ds(n * BE, BE)].unsqueeze(0).to_broadcast([P, BE])).then_inc(s_mask[k], 16)
            pipeline(sp, BATCHES, SLOTS, [(0, load)])

        @block.gpsimd
        def _(gp):
            gatherer(gp, table, gath, idx, s_gath, s_idx, s_go, s_free)

        @block.tensor
        def _(pe):
            def turn(n, k, r):
                if ew is None:
                    landed(pe, s_gath, k, r, BT)
                else:
                    need(pe, s_scale, n)
                room(pe, s_scan, n, 2)
                for t in range(BT):
                    rows_in = gath[k][:, t, :] if ew is None else scaled[k % 2][:, t, :]
                    m = pe.transpose(pT[k % 2][:, cols(t)], rows_in, g["ident"][:, :])
                m.then_inc(s_turn, 1)

            def ret(n, k, r):
                need(pe, s_scan, n)
                room(pe, s_back, n, 2)
                for t in range(BT):
                    m = pe.transpose(pB[k % 2][:, cols(t)], acc[k][:, cols(t)], g["ident"][:, :])
                m.then_inc(s_ret, 1)
            pipeline(pe, BATCHES, SLOTS, [(0, turn), (1, ret)])

        @block.vector
        def _(v):
            def scan(n, k, r):
                need(v, s_turn, n)
                landed(v, s_mask, k, r)
                room(v, s_ret, n, SLOTS)
                room(v, s_scan, n, 1)
                v.tensor_tensor_scan(acc[k][:, :], mask[k][:, :], pT[k % 2][:, :], start_of(acc, n, k),
                                     ALU.mult, ALU.add).then_inc(s_scan, 1)
            pipeline(v, BATCHES, SLOTS, [(0, scan), (0, indexer(v, g, idx, s_idx, s_gath))])

        @block.scalar
        def _(act):
            def scale(n, k, r):
                landed(act, s_gath, k, r, BT)
                room(act, s_turn, n, 2)
                for t in range(BT):
                    a = act.activation(scaled[k % 2][:, t, :], gath[k][:, t, :], ACT.Copy, scale=ew[:, bass.ds(n * BT + t, 1)])
                a.then_inc(s_scale, 1)

            def store(n, k, r):
                need(act, s_ret, n)
                stored(act, s_out, k, r)
                act.activation(rows(back[k][:, :, :]), pB[k % 2][:, :], ACT.Copy).then_inc(s_back, 1)
                need(act, s_back, n)
                act.dma_start(run[:, bass.ds(n * BT, BT), :], back[k][:, :, :]).then_inc(s_out[k], 16)
            pipeline(act, BATCHES, SLOTS, ([] if ew is None else [(0, scale)]) + [(2, store)])
            for k in range(SLOTS):
                act.wait_ge(s_out[k], 16 * BATCHES // SLOTS)


def mask_load(sp, table, mask, s_mask, s_free):
    def load(n, k, r):
        room(sp, s_free, n, SLOTS)
        sp.dma_start(mask[k][:, :], table[bass.ds(n * BE, BE)].unsqueeze(0).to_broadcast([P, BE])).then_inc(s_mask[k], 16)
    return load


def edges_max(nc, d, g):
    w = g["w"]
    with Phase(nc, "L1") as ph:
        gath, idx, s_gath, s_idx, s_go = edge_buffers(ph, D)
        slot = lambda name, width=BE, dtype=F32: [ph.sb(f"{name}{k}", [P, width], dtype) for k in range(SLOTS)]
        weight = ph.sb("weight", [P, TILES])
        same, fresh = slot("same", BE, BF16), slot("fresh", BE, BF16)
        seed, sent, dest, pre, hid, acc, back = (slot(n) for n in ("seed", "sent", "dest", "pre", "hid", "acc", "back"))
        pA = [ph.ps(f"pA{k}") for k in range(2)]
        pS = [ph.ps(f"pS{k}") for k in range(2)]
        pM = [ph.ps(f"pM{k}") for k in range(2)]
        pB = [ph.ps(f"pB{k}") for k in range(2)]
        s_wt, s_sent, s_turn, s_turns, s_dest, s_pre, s_hid, s_msg, s_max, s_ret, s_back = (ph.sem(n) for n in
            ("wt", "sent", "turn", "turns", "dest", "pre", "hid", "msg", "max", "ret", "back"))
        s_same, s_fresh, s_seed, s_out = (ph.slot_sems(n, SLOTS) for n in ("same", "fresh", "seed", "out"))
        run = g["run"].rearrange("(p t) f -> p t f", p=P)
        seeds = g["seed"].rearrange("(p t) f -> p t f", p=P)
        block = ph.block()

        @block.sync
        def _(sp):
            sp.dma_start(weight[:, :], d["weight"]).then_inc(s_wt, 16)

            def load_seed(n, k, r):
                room(sp, s_turns, n, SLOTS)
                sp.dma_start(seed[k][:, :].rearrange("p (t f) -> p t f", t=BT), seeds[:, bass.ds(n * BT, BT), :]).then_inc(s_seed[k], 16)
            pipeline(sp, BATCHES, SLOTS, [(0, load_seed), (0, mask_load(sp, g["same"], same, s_same, s_dest)),
                                          (0, mask_load(sp, g["fresh"], fresh, s_fresh, s_max))])

        @block.gpsimd
        def _(gp):
            gatherer(gp, g["tab"], gath, idx, s_gath, s_idx, s_go, s_sent)

        @block.tensor
        def _(pe):
            def turn_seed(n, k, r):
                landed(pe, s_seed, k, r)
                room(pe, s_dest, n, 2)
                for t in range(BT):
                    m = pe.transpose(pS[k % 2][:, cols(t)], seed[k][:, cols(t)], g["ident"][:, :])
                m.then_inc(s_turns, 1)

            def turn(n, k, r):
                need(pe, s_sent, n)
                room(pe, s_pre, n, 2)
                for t in range(BT):
                    m = pe.transpose(pA[k % 2][:, cols(t)], sent[k][:, cols(t)], g["ident"][:, :])
                m.then_inc(s_turn, 1)

            def message(n, k, r):
                need(pe, s_hid, n)
                room(pe, s_max, n, 2)
                pe.matmul(pM[k % 2][:, :], w["W2"][:, :], hid[k][:, :], start=True, stop=True).then_inc(s_msg, 1)

            def ret(n, k, r):
                need(pe, s_max, n)
                room(pe, s_back, n, 2)
                for t in range(BT):
                    m = pe.transpose(pB[k % 2][:, cols(t)], acc[k][:, cols(t)], g["ident"][:, :])
                m.then_inc(s_ret, 1)
            pipeline(pe, BATCHES, SLOTS, [(0, turn_seed), (0, turn), (1, message), (2, ret)])

        @block.vector
        def _(v):
            def add_weight(n, k, r):
                landed(v, s_gath, k, r, BT)
                room(v, s_turn, n, SLOTS)
                for t in range(BT):
                    a = v.scalar_tensor_tensor(sent[k][:, cols(t)], g["wide"]["W1w"][:, :], weight[:, bass.ds(n * BT + t, 1)],
                                               gath[k][:, t, :], ALU.mult, ALU.add)
                a.then_inc(s_sent, 1)

            def spread(n, k, r):
                need(v, s_turns, n)
                landed(v, s_same, k, r)
                room(v, s_dest, n, 1)
                room(v, s_pre, n, SLOTS)
                v.tensor_tensor_scan(dest[k][:, :], same[k][:, :], pS[k % 2][:, :], start_of(dest, n, k), ALU.mult, ALU.add).then_inc(s_dest, 1)

            def add_dest(n, k, r):
                need(v, s_turn, n)
                need(v, s_dest, n)
                room(v, s_hid, n, SLOTS)
                v.tensor_tensor(pre[k][:, :], pA[k % 2][:, :], dest[k][:, :], ALU.add).then_inc(s_pre, 1)

            def top(n, k, r):
                need(v, s_msg, n)
                landed(v, s_fresh, k, r)
                room(v, s_max, n, 1)
                room(v, s_ret, n, SLOTS)
                v.tensor_tensor_scan(acc[k][:, :], fresh[k][:, :], pM[k % 2][:, :], start_of(acc, n, k), ALU.add, ALU.max).then_inc(s_max, 1)
            v.wait_ge(s_wt, 16)
            ahead = indexer(v, g, idx, s_idx, s_gath)
            pipeline(v, BATCHES, SLOTS, [(0, add_weight), (0, ahead), (0, spread), (0, add_dest), (2, top)])

        @block.scalar
        def _(act):
            def relu(n, k, r):
                need(act, s_pre, n)
                room(act, s_msg, n, SLOTS)
                act.activation(hid[k][:, :], pre[k][:, :], ACT.Relu).then_inc(s_hid, 1)

            def store(n, k, r):
                need(act, s_ret, n)
                stored(act, s_out, k, r)
                act.activation(back[k][:, :], pB[k % 2][:, :], ACT.Copy).then_inc(s_back, 1)
                need(act, s_back, n)
                act.dma_start(run[:, bass.ds(n * BT, BT), :], back[k][:, :].rearrange("p (t f) -> p t f", t=BT)).then_inc(s_out[k], 16)
            pipeline(act, BATCHES, SLOTS, [(0, relu), (3, store)])
            for k in range(SLOTS):
                act.wait_ge(s_out[k], 16 * BATCHES // SLOTS)


def edges_gate(nc, g, z):
    w = g["w"]
    H = slice(0, HID)
    with Phase(nc, "L2a") as ph:
        gath, idx, s_gath, s_idx, s_go = edge_buffers(ph, HID)
        slot = lambda name, width=BE, dtype=F32, p=HID: [ph.sb(f"{name}{k}", [p, width], dtype) for k in range(SLOTS)]
        same, seed = slot("same", BE, BF16), slot("seed", BT * HID, F32, P)
        dest, pre, hid = (slot(n) for n in ("dest", "pre", "hid"))
        pA = [ph.ps(f"pA{k}") for k in range(2)]
        pS = [ph.ps(f"pS{k}") for k in range(2)]
        pZ = [ph.ps(f"pZ{k}") for k in range(2)]
        s_turn, s_turns, s_dest, s_pre, s_hid, s_dot, s_z, s_tgo = (ph.sem(n) for n in
            ("turn", "turns", "dest", "pre", "hid", "dot", "z", "tgo"))
        s_same, s_seed = (ph.slot_sems(n, SLOTS) for n in ("same", "seed"))
        seeds = g["seed"].rearrange("(p t) f -> p t f", p=P)
        block = ph.block()

        @block.sync
        def _(sp):
            def load_seed(n, k, r):
                room(sp, s_turns, n, SLOTS)
                sp.dma_start(seed[k][:, :].rearrange("p (t f) -> p t f", t=BT), seeds[:, bass.ds(n * BT, BT), 0:HID]).then_inc(s_seed[k], 16)

            def load_same(n, k, r):
                room(sp, s_dest, n, SLOTS)
                sp.dma_start(same[k][:, :], g["same"][bass.ds(n * BE, BE)].unsqueeze(0).to_broadcast([HID, BE])).then_inc(s_same[k], 16)
            pipeline(sp, BATCHES, SLOTS, [(0, load_seed), (0, load_same)])

        @block.gpsimd
        def _(gp):
            gatherer(gp, g["tab_h"], gath, idx, s_gath, s_idx, s_go, s_turn)

        @block.tensor
        def _(pe):
            def turn(n, k, r):
                landed(pe, s_seed, k, r)
                room(pe, s_dest, n, 2)
                pe.sem_inc(s_tgo, 1)
                for t in range(BT):
                    m = pe.transpose(pS[k % 2][H, cols(t)], seed[k][:, t * HID:(t + 1) * HID], g["ident"][:, :])
                m.then_inc(s_turns, 1)
                landed(pe, s_gath, k, r, BT)
                room(pe, s_pre, n, 2)
                pe.sem_inc(s_tgo, 1)
                for t in range(BT):
                    m = pe.transpose(pA[k % 2][H, cols(t)], gath[k][:, t, :], g["ident"][:, :])
                m.then_inc(s_turn, 1)

            def dot(n, k, r):
                need(pe, s_hid, n)
                room(pe, s_z, n, 2)
                for t in range(BT):
                    m = pe.matmul(pZ[k % 2][:, t:t + 1], hid[k][:, cols(t)], w["M2"][:, :], start=True, stop=True)
                m.then_inc(s_dot, 1)
            pipeline(pe, BATCHES, SLOTS, [(0, turn), (2, dot)])

        @block.vector
        def _(v):
            def spread(n, k, r):
                need(v, s_turns, n)
                landed(v, s_same, k, r)
                room(v, s_dest, n, 1)
                room(v, s_pre, n, SLOTS)
                v.tensor_tensor_scan(dest[k][:, :], same[k][:, :], pS[k % 2][H, :], start_of(dest, n, k), ALU.mult, ALU.add).then_inc(s_dest, 1)

            def add_dest(n, k, r):
                need(v, s_turn, n)
                need(v, s_dest, n)
                room(v, s_hid, n, SLOTS)
                v.tensor_tensor(pre[k][:, :], pA[k % 2][H, :], dest[k][:, :], ALU.add).then_inc(s_pre, 1)

            def keep(n, k, r):
                need(v, s_dot, n)
                v.tensor_copy(z[:, bass.ds(n * BT, BT)], pZ[k % 2][:, 0:BT]).then_inc(s_z, 1)
            ahead = indexer(v, g, idx, s_idx, s_gath)
            pipeline(v, BATCHES, SLOTS, [(0, spread), (0, add_dest), (0, ahead), (3, keep)])

        @block.scalar
        def _(act):
            def gelu(n, k, r):
                need(act, s_pre, n)
                room(act, s_dot, n, SLOTS)
                act.activation(hid[k][:, :], pre[k][:, :], ACT.Gelu).then_inc(s_hid, 1)
            pipeline(act, BATCHES, SLOTS, [(0, gelu)])


def degrees(nc, g, ew):
    with Phase(nc, "deg") as ph:
        wide_t = -(-TILES // P)
        lin = [ph.sb(f"lin{k}", [P, P]) for k in range(2)]
        c = ph.sb("c", [P, TILES])
        run = ph.sb("run", [P, TILES])
        open_ = ph.sb("open", [P, TILES])
        ends = ph.sb("ends", [1, 2, P])
        carry = ph.sb("carry", [1, P + 1])
        cin = ph.sb("cin", [P, 1])
        deg = ph.sb("deg", [P, NT])
        xs = [ph.sb(f"xs{k}", [P, BT, D]) for k in range(NSLOTS)]
        idx = [ph.sb(f"idx{k}", [P, BT], I32) for k in range(NSLOTS)]
        got = [ph.sb(f"got{k}", [P, BT]) for k in range(NSLOTS)]
        pT = [ph.ps(f"pT{k}") for k in range(2)]
        pE = ph.ps("pE")
        pC = ph.ps("pC")
        s_sig, s_t, s_lin, s_c, s_v, s_pe, s_run, s_ix, s_go, s_got, s_deg, s_xs = (ph.sem(n) for n in
            ("sig", "t", "lin", "c", "v", "pe", "run", "ix", "go", "got", "deg", "xs"))
        s_ld, s_gath, s_out = ph.slot_sems("ld", 2), ph.slot_sems("gath", NSLOTS), ph.slot_sems("out", NSLOTS)
        block = ph.block()

        @block.scalar
        def _(act):
            act.activation(ew[:, :], ew[:, :], ACT.Sigmoid, bias=g["wide"]["m2"][:, 0:1]).then_inc(s_sig, 1)
            for j in range(wide_t):
                width = min(P, TILES - j * P)
                need(act, s_t, j)
                if j >= 2:
                    act.wait_ge(s_ld[j % 2], 16 * (j // 2))
                act.activation(lin[j % 2][0:width, :], pT[j % 2][0:width, 0:P], ACT.Copy).then_inc(s_lin, 1)
                need(act, s_lin, j)
                act.dma_start(g["ew"].rearrange("(t l) a -> t (l a)", l=P)[j * P:j * P + width, :], lin[j % 2][0:width, :]).then_inc(s_ld[j % 2], 16)
            for k in range(2):
                act.wait_ge(s_ld[k], 16 * len(range(k, wide_t, 2)))
            act.dma_start(c[:, :], g["ew"].rearrange("(p i) a -> p (i a)", p=P)).then_inc(s_c, 16)
            act.wait_ge(s_run, 1)
            act.dma_start(g["ew"].rearrange("(p i) a -> p (i a)", p=P), run[:, :]).then_inc(s_c, 16)
            act.wait_ge(s_c, 32)
            act.sem_inc(s_run, 1)
            act.wait_ge(s_deg, 1)
            act.activation(deg[:, :], deg[:, :], ACT.Sqrt).then_inc(s_deg, 1)

        @block.tensor
        def _(pe):
            pe.wait_ge(s_sig, 1)
            for j in range(wide_t):
                width = min(P, TILES - j * P)
                room(pe, s_lin, j, 2)
                pe.transpose(pT[j % 2][0:width, 0:P], ew[:, j * P:j * P + width], g["ident"][:, :]).then_inc(s_t, 1)
            pe.wait_ge(s_v, 2)
            pe.transpose(pE[0:1, 0:P], run[:, TILES - 1:TILES], g["ident"][:, :])
            pe.transpose(pE[0:1, P:2 * P], open_[:, TILES - 1:TILES], g["ident"][:, :]).then_inc(s_pe, 1)
            pe.wait_ge(s_v, 5)
            pe.matmul(pC[:, 0:1], carry[0:1, 0:P], g["ones"][0:1, 0:1], start=True, stop=True).then_inc(s_pe, 1)

        @block.vector
        def _(v):
            link = Chain(v, s_v)
            v.wait_ge(s_c, 16)
            link(v.tensor_tensor_scan(run[:, :], g["same_c"][:, :], c[:, :], 0.0, ALU.mult, ALU.add))
            link(v.tensor_tensor_scan(open_[:, :], g["same_c"][:, :], g["same_c"][:, :], 1.0, ALU.mult, ALU.min))
            v.wait_ge(s_pe, 1)
            link(v.memset(carry[:, :], 0.0))
            link(v.tensor_copy(ends[:, :, :].rearrange("a b c -> a (b c)"), pE[0:1, 0:2 * P]))
            link(v.tensor_tensor_scan(carry[0:1, 1:P + 1], ends[0:1, 1, :], ends[0:1, 0, :], 0.0, ALU.mult, ALU.add))
            v.wait_ge(s_pe, 2)
            link(v.tensor_copy(cin[:, :], pC[:, 0:1]))
            v.scalar_tensor_tensor(run[:, :], open_[:, :], cin[:, 0:1], run[:, :], ALU.mult, ALU.add).then_inc(s_run, 1)

            def keep(n, k, r):
                landed(v, s_gath, k, r, BT)
                v.tensor_copy(deg[:, bass.ds(n * BT, BT)], got[k][:, :]).then_inc(s_got, 1)
            pipeline(v, NB, NSLOTS, [(0, keep)])
            v.wait_ge(s_got, NB)
            link(v.tensor_tensor(deg[:, :], deg[:, :], g["has"][:, :], ALU.mult))
            v.tensor_scalar(deg[:, :], deg[:, :], 1.0, None, ALU.add).then_inc(s_deg, 1)
            v.wait_ge(s_deg, 2)
            link(v.reciprocal(g["dinv"][:, :], deg[:, :]))

            def scale(n, k, r):
                stored(v, s_out, k, r)
                v.tensor_tensor(xs[k][:, :, :], g["xt"][:, bass.ds(n * BT, BT), :],
                                g["dinv"][:, bass.ds(n * BT, BT)].unsqueeze(2).to_broadcast([P, BT, D]), ALU.mult).then_inc(s_xs, 1)
            pipeline(v, NB, NSLOTS, [(0, scale)])

        @block.gpsimd
        def _(gp):
            gp.wait_ge(s_run, 2)

            def fetch(n, k, r):
                room(gp, s_got, n, NSLOTS)
                gp.tensor_copy(idx[k][:, :], g["last_e"][:, bass.ds(n * BT, BT)]).then_inc(s_ix, 1)
                need(gp, s_ix, n)
                gp.sem_inc(s_go, 1)
                for t in range(BT):
                    gp.indirect_dma_start(out=got[k][:, t:t + 1], out_offset=None, in_=g["ew"],
                                          in_offset=bass.IndirectOffsetOnAxis(ap=idx[k][:, t:t + 1], axis=0)).then_inc(s_gath[k], 16)
            pipeline(gp, NB, NSLOTS, [(0, fetch)])

        @block.sync
        def _(sp):
            tab = g["tab"].rearrange("(p t) f -> p t f", p=P)

            def store(n, k, r):
                need(sp, s_xs, n)
                sp.dma_start(tab[:, bass.ds(n * BT, BT), :], xs[k][:, :, :]).then_inc(s_out[k], 16)
            pipeline(sp, NB, NSLOTS, [(0, store)])
            for k in range(NSLOTS):
                sp.wait_ge(s_out[k], 16 * len(range(k, NB, NSLOTS)))


def edges_attention(nc, g):
    with Phase(nc, "L3") as ph:
        gath, idx, s_gath, s_idx, s_go = edge_buffers(ph, 2 * D)
        slot = lambda name, width=BE, dtype=F32, c=2: [ph.sb(f"{name}{k}", [P, width], dtype) for k in range(c)]
        same, fresh, ends = (slot(n, BE, BF16, SLOTS) for n in ("same", "fresh", "ends"))
        seed = slot("seed", BE, F32, SLOTS)
        dest, prod, top, ref, diff, prob, pv, num, den = (slot(n, w, F32, c) for n, w, c in (
            ("dest", BE, 2), ("prod", BE, 2), ("top", BE, 2), ("ref", BE, 2), ("diff", BE + 1, 2), ("prob", BE + 1, 2),
            ("pv", BE, 1), ("num", BE, 2), ("den", BE, 2)))
        pv = pv[0]
        start = slot("start", 2, F32, 1)[0]
        back = [ph.sb(f"back{k}", [P, BT, W3]) for k in range(SLOTS)]
        blocks = ph.sb("blocks", [P, P])
        pick = ph.sb("pick", [P, HEADS])
        pS, pK, pB, pD = (ph.ps(n) for n in ("pS", "pK", "pB", "pD"))
        pV = [ph.ps(f"pV{k}") for k in range(2)]
        pC = [ph.ps(f"pC{k}") for k in range(2)]
        (s_c, s_cc, s_turns, s_turnk, s_turnv, s_dest, s_prod, s_score, s_top, s_ref, s_diff, s_prob, s_pv, s_init, s_num, s_den,
         s_ret, s_back, s_col) = (ph.sem(n) for n in ("c", "cc", "turns", "turnk", "turnv", "dest", "prod", "score", "top", "ref",
                                      "diff", "prob", "pv", "init", "num", "den", "ret", "back", "col"))
        s_same, s_fresh, s_ends, s_seed, s_out = (ph.slot_sems(n, SLOTS) for n in ("same", "fresh", "ends", "seed", "out"))
        run = g["run3"].rearrange("(p t) f -> p t f", p=P)
        seeds = g["seed"].rearrange("(p t) f -> p t f", p=P)
        block = ph.block()

        @block.sync
        def _(sp):
            def load_seed(n, k, r):
                room(sp, s_turns, n, SLOTS)
                sp.dma_start(seed[k][:, :].rearrange("p (t f) -> p t f", t=BT), seeds[:, bass.ds(n * BT, BT), :]).then_inc(s_seed[k], 16)
            pipeline(sp, BATCHES, SLOTS, [(0, load_seed), (0, mask_load(sp, g["same"], same, s_same, s_den)),
                                          (0, mask_load(sp, g["fresh"], fresh, s_fresh, s_top)),
                                          (0, mask_load(sp, g["ends"], ends, s_ends, s_ref))])

        @block.gpsimd
        def _(gp):
            gatherer(gp, g["tab_kv"], gath, idx, s_gath, s_idx, s_go, s_turnv)

        @block.tensor
        def _(pe):
            def turn(n, k, r):
                landed(pe, s_seed, k, r)
                room(pe, s_dest, n, 1)
                for t in range(BT):
                    m = pe.transpose(pS[:, cols(t)], seed[k][:, cols(t)], g["ident"][:, :])
                m.then_inc(s_turns, 1)
                landed(pe, s_gath, k, r, BT)
                room(pe, s_prod, n, 1)
                for t in range(BT):
                    m = pe.transpose(pK[:, cols(t)], gath[k][:, t, 0:D], g["ident"][:, :])
                m.then_inc(s_turnk, 1)
                room(pe, s_pv, n, 2)
                for t in range(BT):
                    m = pe.transpose(pV[k % 2][:, cols(t)], gath[k][:, t, D:2 * D], g["ident"][:, :])
                m.then_inc(s_turnv, 1)

            def score(n, k, r):
                need(pe, s_prod, n)
                room(pe, s_diff, n, 2)
                pe.matmul(pC[k % 2][:, :], blocks[:, :], prod[k % 2][:, :], start=True, stop=True).then_inc(s_score, 1)

            def ret(n, k, r):
                need(pe, s_num, n)
                need(pe, s_den, n)
                room(pe, s_back, n, 1)
                for t in range(BT):
                    pe.transpose(pB[:, cols(t)], num[k % 2][:, cols(t)], g["ident"][:, :])
                for t in range(BT):
                    m = pe.matmul(pD[:, t * HEADS:(t + 1) * HEADS], den[k % 2][:, cols(t)], pick[:, :], start=True, stop=True)
                m.then_inc(s_ret, 1)
            pe.wait_ge(s_cc, 2 * HEADS)
            pipeline(pe, BATCHES, SLOTS, [(0, turn), (0, score), (2, ret)])

        @block.vector
        def _(v):
            v.memset(blocks[:, :], 0.0).then_inc(s_c, 1)
            v.memset(pick[:, :], 0.0).then_inc(s_c, 1)
            v.wait_ge(s_c, 2)
            for h in range(HEADS):
                part = slice(h * HEAD, (h + 1) * HEAD)
                v.memset(blocks[part, part], float(HEAD) ** -0.5).then_inc(s_cc, 1)
                v.memset(pick[h * HEAD:h * HEAD + 1, h:h + 1], 1.0).then_inc(s_cc, 1)

            def spread(n, k, r):
                need(v, s_turns, n)
                landed(v, s_same, k, r)
                room(v, s_dest, n, 1)
                room(v, s_prod, n, 2)
                v.tensor_tensor_scan(dest[k % 2][:, :], same[k][:, :], pS[:, :], start_of(dest, n, k % 2), ALU.mult, ALU.add).then_inc(s_dest, 1)
                need(v, s_turnk, n)
                need(v, s_dest, n)
                room(v, s_score, n, 2)
                v.tensor_tensor(prod[k % 2][:, :], pK[:, :], dest[k % 2][:, :], ALU.mult).then_inc(s_prod, 1)

            def peak(n, k, r):
                need(v, s_score, n)
                landed(v, s_fresh, k, r)
                landed(v, s_ends, k, r)
                room(v, s_top, n, 1)
                room(v, s_ref, n, 2)
                v.tensor_tensor_scan(top[k % 2][:, :], fresh[k][:, :], pC[k % 2][:, :], start_of(top, n, k % 2), ALU.add, ALU.max).then_inc(s_top, 1)
                need(v, s_top, n)
                room(v, s_diff, n, 2)
                v.tensor_tensor_scan(ref[k % 2][:, ::-1], ends[k][:, ::-1], top[k % 2][:, ::-1], FAR, ALU.add, ALU.max).then_inc(s_ref, 1)
                need(v, s_ref, n)
                room(v, s_prob, n, 2)
                if isinstance(n, int) and n == 0:
                    v.memset(diff[k % 2][:, BE:BE + 1], 0.0).then_inc(s_col, 1)
                    v.wait_ge(s_col, 1)
                else:
                    v.tensor_tensor(diff[k % 2][:, BE:BE + 1], ref[(k - 1) % 2][:, BE - 1:BE], ref[k % 2][:, 0:1], ALU.subtract).then_inc(s_col, 1)
                    need(v, s_col, n)
                v.tensor_scalar(diff[k % 2][:, BE:BE + 1], diff[k % 2][:, BE:BE + 1], 0.0, None, ALU.min)
                v.tensor_tensor(diff[k % 2][:, 0:BE], pC[k % 2][:, :], ref[k % 2][:, :], ALU.subtract).then_inc(s_diff, 1)

            def total(n, k, r):
                need(v, s_prob, n)
                landed(v, s_same, k, r)
                need(v, s_turnv, n)
                room(v, s_num, n, 1)
                v.tensor_tensor(pv[:, :], pV[k % 2][:, :], prob[k % 2][:, 0:BE], ALU.mult).then_inc(s_pv, 1)
                first = isinstance(n, int) and n == 0
                room(v, s_den, n, 1)
                if first:
                    v.memset(start[:, :], 0.0).then_inc(s_init, 1)
                else:
                    v.tensor_tensor(start[:, 0:1], num[(k - 1) % 2][:, BE - 1:BE], prob[k % 2][:, BE:BE + 1], ALU.mult)
                    v.tensor_tensor(start[:, 1:2], den[(k - 1) % 2][:, BE - 1:BE], prob[k % 2][:, BE:BE + 1], ALU.mult).then_inc(s_init, 1)
                need(v, s_init, n)
                need(v, s_pv, n)
                room(v, s_ret, n, 2)
                v.tensor_tensor_scan(num[k % 2][:, :], same[k][:, :], pv[:, :], start[:, 0:1], ALU.mult, ALU.add).then_inc(s_num, 1)
                v.tensor_tensor_scan(den[k % 2][:, :], same[k][:, :], prob[k % 2][:, 0:BE], start[:, 1:2], ALU.mult, ALU.add).then_inc(s_den, 1)
            ahead = indexer(v, g, idx, s_idx, s_gath)
            pipeline(v, BATCHES, SLOTS, [(0, spread), (1, total), (0, peak), (0, ahead)])

        @block.scalar
        def _(act):
            def exps(n, k, r):
                need(act, s_diff, n)
                room(act, s_den, n, 2)
                act.activation(prob[k % 2][:, :], diff[k % 2][:, :], ACT.Exp).then_inc(s_prob, 1)

            def store(n, k, r):
                need(act, s_ret, n)
                stored(act, s_out, k, r)
                act.activation(back[k][:, :, 0:D], pB[:, :].rearrange("p (t f) -> p t f", t=BT), ACT.Copy)
                act.activation(back[k][:, :, D:W3], pD[:, 0:BT * HEADS].rearrange("p (t h) -> p t h", t=BT), ACT.Copy).then_inc(s_back, 1)
                need(act, s_back, n)
                act.dma_start(run[:, bass.ds(n * BT, BT), :], back[k][:, :, :]).then_inc(s_out[k], 16)
            pipeline(act, BATCHES, SLOTS, [(0, exps), (2, store)])
            for k in range(SLOTS):
                act.wait_ge(s_out[k], 16 * BATCHES // SLOTS)


def nodes(nc, g, layer, out):
    w, row, wide = g["w"], g["row"], g["wide"]
    width = W3 if layer == 3 else D
    table = g["run3"] if layer == 3 else g["run"]
    nxt = [("W1s", None, g["tab"]), ("M1s", None, g["tab_h"]), ("Wkv", "bkv", g["tab_kv"]), None][layer]
    seed_w = [("W1d", "b1"), ("M1d", "m1"), ("Wq", "bq"), None][layer]
    last_layer = layer == 3
    with Phase(nc, f"N{layer}") as ph:
        slot = lambda name, shape, dtype=F32: [ph.sb(f"{name}{k}", shape, dtype) for k in range(NSLOTS)]
        idx, idf = slot("idx", [P, BT], I32), slot("idf", [P, BT], I32)
        got = slot("got", [P, BT, width])
        agg = slot("agg", [P, BT, D])
        aT, xT, xn_T, uT = (slot(n, [P, BE]) for n in ("aT", "xT", "xnT", "uT"))
        y, xn, seed = (slot(n, [P, BT, D]) for n in ("y", "xn", "seed"))
        tw = w[nxt[0]].shape[1] if nxt else D
        tab = slot("tab", [P, BT, tw])
        sq, t1, t2 = (ph.sb(n, [P, BT, D]) for n in ("sq", "t1", "t2"))
        s1, s2, s3, s4, s5 = (ph.sb(n, [P, BT]) for n in ("s1", "s2", "s3", "s4", "s5"))
        std = ph.sb("std", [P, BT])
        zb, beta = ph.sb("zb", [P, BT]), ph.sb("beta", [P, BT])
        r4 = ph.sb("r4", [P, BT, HEADS])
        pA, pU, pY, pX, pQ = (ph.ps(n) for n in ("pA", "pU", "pY", "pX", "pQ"))
        pT = [ph.ps(f"pT{j}") for j in range(2)]
        (s_ix, s_if, s_go, s_gz, s_agg, s_turn, s_aT, s_xs, s_u, s_uT, s_y, s_z, s_beta, s_dv, s_sum, s_var, s_std, s_xn, s_xt, s_xnT, s_keep,
         s_tab, s_tabc, s_seedc, s_c1, s_c2, s_zero, s_rec) = (ph.sem(n) for n in ("ix", "if", "go", "gz", "agg", "turn", "aT", "xs", "u", "uT", "y",
            "z", "beta", "dv", "sum", "var", "std", "xn", "xt", "xnT", "keep", "tab", "tabc", "seedc", "c1", "c2", "zero", "rec"))
        s_got, s_scat, s_tout = (ph.slot_sems(n, NSLOTS) for n in ("got", "scat", "tout"))
        block = ph.block()
        over = lambda a, n, m=D: a.unsqueeze(2).to_broadcast([P, n, m])
        tiled = lambda a: a.unsqueeze(1).to_broadcast([P, BT, D])
        now = lambda a, n: a[:, bass.ds(n * BT, BT)]

        @block.gpsimd
        def _(gp):
            if seed_w and w[seed_w[0]].shape[1] < D:
                for k in range(NSLOTS):
                    gp.memset(seed[k][:, :, :], 0.0).then_inc(s_zero, 1)

            def fetch(n, k, r):
                room(gp, s_agg, n, NSLOTS)
                gp.tensor_copy(idx[k][:, :], now(g["last"], n)).then_inc(s_ix, 1)
                need(gp, s_ix, n)
                gp.sem_inc(s_go, 1)
                for t in range(BT):
                    gp.indirect_dma_start(out=got[k][:, t, :], out_offset=None, in_=table,
                                          in_offset=bass.IndirectOffsetOnAxis(ap=idx[k][:, t:t + 1], axis=0)).then_inc(s_got[k], 16)

            def scatter(n, k, r):
                stored(gp, s_scat, k, r, BT)
                gp.tensor_copy(idf[k][:, :], now(g["first"], n)).then_inc(s_if, 1)
                need(gp, s_if, n)
                need(gp, s_seedc, n)
                gp.sem_inc(s_gz, 1)
                for t in range(BT):
                    gp.indirect_dma_start(out=g["seed"], out_offset=bass.IndirectOffsetOnAxis(ap=idf[k][:, t:t + 1], axis=0),
                                          in_=seed[k][:, t, :], in_offset=None, bounds_check=EP - 1, oob_is_err=False).then_inc(s_scat[k], 16)
            pipeline(gp, NB, NSLOTS, [(0, fetch)] + ([] if last_layer else [(1, scatter)]))
            if not last_layer:
                for k in range(NSLOTS):
                    gp.wait_ge(s_scat[k], 16 * BT * len(range(k, NB, NSLOTS)))

        @block.sync
        def _(sp):
            if last_layer:
                full, rest = N // NT, N % NT

                def store(n, k, r):
                    need(sp, s_xn, n)
                    sp.dma_start(out[0:full * NT, :].rearrange("(p t) f -> p t f", t=NT)[:, bass.ds(n * BT, BT), :], xn[k][0:full, :, :]).then_inc(s_tout[k], 16)
                pipeline(sp, NB, NSLOTS, [(0, store)])
                for k in range(NSLOTS):
                    sp.wait_ge(s_tout[k], 16 * len(range(k, NB, NSLOTS)))
                sp.wait_ge(s_keep, NB)
                sp.dma_start(out[full * NT:N, :].unsqueeze(0), g["x"][full:full + 1, 0:rest, :]).then_inc(s_tout[0], 16)
                sp.wait_ge(s_tout[0], 16 * (len(range(0, NB, NSLOTS)) + 1))
            else:
                to = nxt[2].rearrange("(p t) f -> p t f", p=P)

                def store(n, k, r):
                    need(sp, s_tabc, n)
                    sp.dma_start(to[:, bass.ds(n * BT, BT), :], tab[k][:, :, :]).then_inc(s_tout[k], 16)
                pipeline(sp, NB, NSLOTS, [(0, store)])
                for k in range(NSLOTS):
                    sp.wait_ge(s_tout[k], 16 * len(range(k, NB, NSLOTS)))

        @block.tensor
        def _(pe):
            def product(to, left, w_name, bias):
                width_ = w[w_name].shape[1]
                m = pe.matmul(to, left, w[w_name][:, :], start=True, stop=bias is None)
                if bias is not None:
                    m = pe.matmul(to, g["ones"][0:1, :], row[bias][0:1, 0:width_], start=False, stop=True)
                return m

            def update(n, k, r):
                if layer in (0, 1):
                    need(pe, s_agg, n)
                    room(pe, s_aT, n, 1)
                    for t in range(BT):
                        m = pe.transpose(pA[:, cols(t)], agg[k][:, t, :], g["ident"][:, :])
                    m.then_inc(s_turn, 1)
                if layer == 0:
                    need(pe, s_xs, n)
                    need(pe, s_aT, n)
                    room(pe, s_sum, n, 1)
                    for t in range(BT):
                        pe.matmul(pY[:, cols(t)], xT[k][:, cols(t)], w["W0x"][:, :], start=True, stop=False)
                        m = pe.matmul(pY[:, cols(t)], aT[k][:, cols(t)], w["W0a"][:, :], start=False, stop=True)
                    m.then_inc(s_y, 1)
                if layer == 1:
                    need(pe, s_xs, n)
                    need(pe, s_aT, n)
                    room(pe, s_uT, n, 1)
                    pe.matmul(pU[:, :], w["U1x"][:, :], xT[k][:, :], start=True, stop=False)
                    pe.matmul(pU[:, :], w["U1a"][:, :], aT[k][:, :], start=False, stop=True).then_inc(s_u, 1)
                    need(pe, s_uT, n)
                    room(pe, s_sum, n, 1)
                    for t in range(BT):
                        m = product(pY[:, cols(t)], uT[k][:, cols(t)], "U2", "c2")
                    m.then_inc(s_y, 1)
                if layer == 3:
                    need(pe, s_xs, n)
                    room(pe, s_beta, n, 1)
                    for t in range(BT):
                        m = product(pY[:, cols(t)], xT[k][:, cols(t)], "Wskip", "bskip")
                    m.then_inc(s_y, 1)

            def tables(n, k, r):
                need(pe, s_xn, n)
                room(pe, s_xnT, n, 1)
                for t in range(BT):
                    m = pe.transpose(pX[:, cols(t)], xn[k][:, t, :], g["ident"][:, :])
                m.then_inc(s_xt, 1)
                need(pe, s_xnT, n)
                room(pe, s_seedc, n, 1)
                room(pe, s_tabc, n, 1)
                for t in range(BT):
                    bank, at = (pT[t * tw // BE], t * tw % BE)
                    product(bank[:, at:at + tw], xn_T[k][:, cols(t)], nxt[0], nxt[1])
                    if layer == 1:
                        product(pT[1][:, cols(t)], xn_T[k][:, cols(t)], "conv", None)
                    m = product(pQ[:, t * D:t * D + w[seed_w[0]].shape[1]], xn_T[k][:, cols(t)], *seed_w)
                m.then_inc(s_tab, 1)
            pipeline(pe, NB, NSLOTS, ([] if layer == 2 else [(0, update)]) + ([] if last_layer else [(1, tables)]))

        per_prep = {0: 0, 1: 1, 2: 3, 3: 0}[layer]
        per_norm = {0: 5, 1: 5, 2: 5, 3: 5}[layer]

        @block.vector
        def _(v):
            prep_link, link = Chain(v, s_c1, per_prep), Chain(v, s_c2, per_norm)
            v_link = Chain(v, s_dv, {3: 12}.get(layer, 0))
            if layer == 2:
                v.tensor_tensor(g["mean"][:, :], g["dinv"][:, :], g["has"][:, :], ALU.mult).then_inc(s_z, 1)
                v.wait_ge(s_z, 1)

            def prep(n, k, r):
                landed(v, s_got, k, r, BT)
                prep_link.item(n)
                if layer == 0:
                    room(v, s_turn, n, NSLOTS)
                    v.tensor_tensor(agg[k][:, :, :], got[k][:, :, :], over(now(g["mean"], n), BT), ALU.mult).then_inc(s_agg, 1)
                elif layer == 1:
                    room(v, s_turn, n, NSLOTS)
                    prep_link(v.tensor_tensor(agg[k][:, :, :], got[k][:, :, :], tiled(wide["b2"][:, :]), ALU.add))
                    v.tensor_tensor(agg[k][:, :, :], agg[k][:, :, :], over(now(g["has"], n), BT), ALU.mult).then_inc(s_agg, 1)
                elif layer == 2:
                    room(v, s_sum, n, NSLOTS)
                    prep_link(v.tensor_tensor(agg[k][:, :, :], got[k][:, :, :], over(now(g["mean"], n), BT), ALU.mult))
                    dinv = over(now(g["dinv"], n), BT)
                    prep_link(v.tensor_tensor(t1[:, :, :], g["xt"][:, bass.ds(n * BT, BT), :], dinv, ALU.mult))
                    v.tensor_tensor(t1[:, :, :], t1[:, :, :], dinv, ALU.mult).then_inc(s_c1, 1)
                    v.wait_ge(s_c1, n * 3 + 3)
                    prep_link.j = 3
                    v.tensor_tensor(agg[k][:, :, :], agg[k][:, :, :], t1[:, :, :], ALU.add).then_inc(s_agg, 1)

            def attend(n, k, r):
                landed(v, s_got, k, r, BT)
                v_link.item(n)
                v_link(v.tensor_scalar(r4[:, :, :], got[k][:, :, D:W3], 1e-16, None, ALU.max))
                v_link(v.reciprocal(r4[:, :, :], r4[:, :, :]))
                v_link(v.tensor_tensor(r4[:, :, :], r4[:, :, :], over(now(g["has"], n), BT, HEADS), ALU.mult))
                for t in range(BT):
                    a = v.tensor_tensor(agg[k][:, t, :].rearrange("p (h c) -> p h c", h=HEADS),
                                        got[k][:, t, 0:D].rearrange("p (h c) -> p h c", h=HEADS), over(r4[:, t, :], HEADS, HEAD), ALU.mult)
                v_link(a)
                v.sem_inc(s_agg, 1)
                need(v, s_y, n)
                wb = lambda j: tiled(wide["beta"][:, j * D:(j + 1) * D])
                skip = pY[:, :].rearrange("p (t f) -> p t f", t=BT)
                v_link(v.tensor_tensor(t1[:, :, :], agg[k][:, :, :], skip, ALU.subtract))
                v_link(v.tensor_tensor(t2[:, :, :], t1[:, :, :], wb(2), ALU.mult))
                v_link(v.tensor_tensor(sq[:, :, :], agg[k][:, :, :], wb(0), ALU.mult))
                v_link(v.tensor_tensor(t2[:, :, :], t2[:, :, :], sq[:, :, :], ALU.add))
                v_link(v.tensor_tensor(sq[:, :, :], skip, wb(1), ALU.mult))
                v_link(v.tensor_tensor(t2[:, :, :], t2[:, :, :], sq[:, :, :], ALU.add))
                v.tensor_reduce(zb[:, :], t2[:, :, :], AX, ALU.add).then_inc(s_z, 1)
                need(v, s_beta, n)
                v_link(v.tensor_tensor(t1[:, :, :], t1[:, :, :], over(beta[:, :], BT), ALU.mult))
                v_link(v.tensor_tensor(agg[k][:, :, :], agg[k][:, :, :], t1[:, :, :], ALU.subtract))

            def norm(n, k, r):
                if layer in (0, 1):
                    need(v, s_y, n)
                    other = pY[:, :].rearrange("p (t f) -> p t f", t=BT)
                else:
                    if layer == 3:
                        attend(n, k, r)
                    else:
                        need(v, s_agg, n)
                    other = agg[k][:, :, :]
                v.tensor_tensor(y[k][:, :, :], other, g["x"][:, bass.ds(n * BT, BT), :], ALU.add).then_inc(s_sum, 1)
                need(v, s_sum, n)
                link.item(n)
                if layer == 2:
                    v.tensor_tensor(y[k][:, :, :], y[k][:, :, :], tiled(wide["conv_b"][:, :]), ALU.add).then_inc(s_dv, 1)
                    need(v, s_dv, n)
                link(v.tensor_reduce(s1[:, :], y[k][:, :, :], AX, ALU.add))
                link(v.tensor_scalar(s2[:, :], s1[:, :], -1.0 / D, None, ALU.mult))
                link(v.tensor_tensor(y[k][:, :, :], y[k][:, :, :], over(s2[:, :], BT), ALU.add))
                link(v.tensor_tensor(sq[:, :, :], y[k][:, :, :], y[k][:, :, :], ALU.mult))
                link(v.tensor_reduce(s3[:, :], sq[:, :, :], AX, ALU.add))
                v.tensor_scalar(s4[:, :], s3[:, :], 1.0 / D, EPS, ALU.mult, ALU.add).then_inc(s_var, 1)
                need(v, s_std, n)
                v.reciprocal(s5[:, :], std[:, :]).then_inc(s_rec, 1)
                need(v, s_rec, n)
                if last_layer:
                    stored(v, s_tout, k, r)
                else:
                    room(v, s_xt, n, NSLOTS)
                room(v, s_keep, n, NSLOTS)
                v.tensor_tensor(xn[k][:, :, :], y[k][:, :, :], over(s5[:, :], BT), ALU.mult).then_inc(s_xn, 1)
            pipeline(v, NB, NSLOTS, ([] if layer == 3 else [(0, prep)]) + [(1, norm)])

        @block.scalar
        def _(act):
            def first(n, k, r):
                if layer != 2:
                    room(act, s_y if layer != 1 else s_u, n, NSLOTS)
                    act.activation(xT[k][:, :], g["xT"][:, bass.ds(n * BE, BE)], ACT.Copy).then_inc(s_xs, 1)
                if layer in (0, 1):
                    need(act, s_turn, n)
                    act.activation(aT[k][:, :], pA[:, :], ACT.Copy).then_inc(s_aT, 1)
                if layer == 1:
                    need(act, s_u, n)
                    room(act, s_y, n, NSLOTS)
                    act.activation(uT[k][:, :], pU[:, :], ACT.Relu, bias=g["c1"][:, 0:1]).then_inc(s_uT, 1)

            def second(n, k, r):
                if layer == 3:
                    need(act, s_z, n)
                    act.activation(beta[:, :], zb[:, :], ACT.Sigmoid).then_inc(s_beta, 1)
                need(act, s_var, n)
                act.activation(std[:, :], s4[:, :], ACT.Sqrt).then_inc(s_std, 1)
                need(act, s_xn, n)
                act.activation(g["x"][:, bass.ds(n * BT, BT), :], xn[k][:, :, :], ACT.Copy).then_inc(s_keep, 1)
                if last_layer:
                    return
                need(act, s_xt, n)
                room(act, s_tab, n, NSLOTS)
                act.activation(xn_T[k][:, :], pX[:, :], ACT.Copy)
                act.activation(g["xT"][:, bass.ds(n * BE, BE)], pX[:, :], ACT.Copy).then_inc(s_xnT, 1)
                need(act, s_tab, n)
                stored(act, s_tout, k, r)
                half = BE // tw if tw > D else BT
                for j in range(BT // half):
                    a = act.activation(tab[k][:, j * half:(j + 1) * half, :], pT[j][:, 0:half * tw].rearrange("p (t f) -> p t f", f=tw), ACT.Copy)
                if layer == 1:
                    a = act.activation(g["xt"][:, bass.ds(n * BT, BT), :], pT[1][:, :].rearrange("p (t f) -> p t f", t=BT), ACT.Copy)
                a.then_inc(s_tabc, 1)
                stored(act, s_scat, k, r, BT)
                sw = w[seed_w[0]].shape[1]
                act.activation(seed[k][:, :, 0:sw], pQ[:, :].rearrange("p (t f) -> p t f", t=BT)[:, :, 0:sw], ACT.Copy).then_inc(s_seedc, 1)
            if seed_w and w[seed_w[0]].shape[1] < D:
                act.wait_ge(s_zero, NSLOTS)
            pipeline(act, NB, NSLOTS, [(0, first), (1, second)])


_WEIGHTS = ["L0_gnn_weight", "L1_gnn_W1", "L1_gnn_b1", "L1_gnn_W2", "L1_gnn_b2", "L1_gnn_U1", "L1_gnn_c1", "L1_gnn_U2", "L1_gnn_c2",
            "L2_gnn_mlp_w1", "L2_gnn_mlp_b1", "L2_gnn_mlp_w2", "L2_gnn_mlp_b2", "L2_gnn_conv_w", "L2_gnn_conv_b",
            "L3_gnn_Wq", "L3_gnn_bq", "L3_gnn_Wk", "L3_gnn_bk", "L3_gnn_Wv", "L3_gnn_bv", "L3_gnn_Wskip", "L3_gnn_bskip", "L3_gnn_Wbeta"]


def kernel(**inputs):
    import numpy as _np
    import concourse.bacc as _bacc
    from concourse import mybir as _mybir
    from concourse.bass_utils import run_bass_kernel_spmd as _run

    nc = _bacc.Bacc("TRN2", target_bir_lowering=False, num_devices=1)
    x = _np.zeros((NP, D), _np.float32)
    x[:N] = inputs["x"]
    src = _np.zeros((EP + SLOTS * BE,), _np.int32)
    src[:E] = inputs["src"]
    dst = _np.full((EP + 2,), N, _np.int32)
    dst[0] = -1
    dst[1:E + 1] = inputs["dst"]
    dst[EP + 1] = N + 1
    weight = _np.zeros((EP,), _np.float32)
    weight[:E] = inputs["edge_weight"]
    arrays = {
        "x": x,
        "src": _np.ascontiguousarray(src.reshape(-1, P).T),
        "dst": dst,
        "dst_rows": _np.ascontiguousarray(dst[1:EP + 1].reshape(TILES, P)),
        "heads": _np.ascontiguousarray(dst[1:EP + 1].reshape(TILES, P)[:, 0]),
        "weight": _np.ascontiguousarray(weight.reshape(TILES, P).T),
    }
    for name in _WEIGHTS:
        arrays[name] = _np.ascontiguousarray(inputs[name])
    d = {n: nc.dram_tensor("in_" + n, a.shape, _mybir.dt.from_np(a.dtype), kind="ExternalInput").ap() for n, a in arrays.items()}
    out = nc.dram_tensor("out_0", (N, D), F32, kind="ExternalOutput").ap()
    build(nc, d, out)
    r = _run(nc, [{"in_" + n: a for n, a in arrays.items()}], core_ids=[0])
    return r.results[0]["out_0"]
```

```python
from contextlib import ExitStack

import numpy as np

import concourse.bass as bass
from concourse import mybir

F32 = mybir.dt.float32
I32 = mybir.dt.int32
BF16 = mybir.dt.bfloat16
ALU = mybir.AluOpType
ACT = mybir.ActivationFunctionType
AX = mybir.AxisListType.X

P = 128
N, E, D = 6250, 106250, 128
HID = 64
HEADS, HEAD = 4, 32
BT = 4
BE = BT * P
SLOTS = 4
TILES = -(-E // (P * BT * SLOTS)) * BT * SLOTS
BATCHES = TILES // BT
EP = TILES * P
NT = -(-N // (P * BT)) * BT
NP = NT * P
NB = NT // BT
NSLOTS = 3
FAR = -3.0e38
EPS = 1e-5
W3 = D + HEADS
W2 = HID + D
LO = 7
HIGH = NP // P


def need(eng, sem, n):
    eng.wait_ge(sem, n + 1)


def room(eng, sem, n, depth):
    if isinstance(n, int) and n < depth:
        return
    eng.wait_ge(sem, n - depth + 1)


def landed(eng, sems, k, r, dmas=1):
    eng.wait_ge(sems[k], 16 * dmas * (r + 1))


def stored(eng, sems, k, r, dmas=1):
    if isinstance(r, int) and r < 1:
        return
    eng.wait_ge(sems[k], 16 * dmas * r)


def pipeline(eng, count, slots, stages):
    lag_max = max(lag for lag, _ in stages)
    head = -(-(lag_max + slots) // slots)
    rounds = count // slots

    def step(r0, k0, peeled):
        for lag, f in stages:
            q = k0 - lag
            k, r = q % slots, r0 + q // slots
            n = r * slots + k
            if peeled and not 0 <= n < count:
                continue
            f(n, k, r)

    for s in range(min(head, rounds) * slots):
        step(s // slots, s % slots, True)
    if rounds > head:
        with eng.Fori(head, rounds) as i:
            for k0 in range(slots):
                step(i, k0, False)
    for s in range(max(rounds, 0) * slots, count + lag_max):
        step(s // slots, s % slots, True)


class Phase:

    def __init__(self, nc, name):
        self.nc, self.name, self.sems, self.ctx = nc, name, [], ExitStack()

    def __enter__(self):
        return self

    def sb(self, name, shape, dtype=F32):
        return self.ctx.enter_context(self.nc.sbuf_tensor(f"{self.name}_{name}", shape, dtype))

    def ps(self, name, shape=(P, BE), dtype=F32):
        return self.ctx.enter_context(self.nc.psum_tensor(f"{self.name}_{name}", list(shape), dtype))

    def sem(self, name):
        s = self.nc.alloc_semaphore(name=f"{self.name}_{name}")
        self.sems.append(s)
        return s

    def slot_sems(self, name, count):
        return [self.sem(f"{name}{k}") for k in range(count)]

    def block(self):
        return self.ctx.enter_context(self.nc.Block())

    def __exit__(self, *args):
        self.ctx.close()
        self.nc.clear_and_free_semaphores(self.sems)
        self.nc.all_engine_barrier()


class Chain:

    def __init__(self, eng, sem, per=0):
        self.eng, self.sem, self.per, self.j, self.n = eng, sem, per, 0, 0

    def item(self, n):
        assert self.j in (0, self.per), (self.j, self.per)
        self.n, self.j = n, 0

    def __call__(self, ins):
        self.j += 1
        ins.then_inc(self.sem, 1)
        self.eng.wait_ge(self.sem, self.n * self.per + self.j)


def rows(tile):
    return tile.rearrange("p a b -> p (a b)")


def cols(t):
    return slice(t * P, (t + 1) * P)


def build(nc, d, out):
    with ExitStack() as ctx:
        def sb(name, shape, dtype=F32):
            return ctx.enter_context(nc.sbuf_tensor(name, shape, dtype))

        def dram(name, shape, dtype=F32):
            return nc.dram_tensor(name, shape, dtype, kind="Internal").ap()

        g = {}
        g["ident"] = sb("ident", [P, P])
        g["ones"] = sb("ones", [1, P])
        g["src"] = sb("src", [P, TILES + SLOTS * BT], I32)
        g["x"] = sb("x", [P, NT, D])
        g["xT"] = sb("xT", [P, NT * P])
        g["last"] = sb("last", [P, NT], I32)
        g["first"] = sb("first", [P, NT], I32)
        g["last_e"] = sb("last_e", [P, NT], I32)
        g["has"] = sb("has", [P, NT])
        g["mean"] = sb("mean", [P, NT])
        g["same_c"] = sb("same_c", [P, TILES], BF16)
        weights = {}
        for name in ("W0x", "W0a", "W1s", "W1d", "W2", "U1x", "U1a", "U2", "conv", "Wq", "Wskip"):
            weights[name] = sb("w_" + name, [P, D])
        weights["M1s"] = sb("w_M1s", [P, HID])
        weights["M1d"] = sb("w_M1d", [P, HID])
        weights["M2"] = sb("w_M2", [HID, 1])
        weights["Wkv"] = sb("w_Wkv", [P, 2 * D])
        rowsb = {n: sb("r_" + n, [1, w]) for n, w in (("b1", D), ("c2", D), ("m1", HID), ("bq", D), ("bkv", 2 * D), ("bskip", D))}
        wide = {n: sb("b_" + n, [P, w]) for n, w in (("W1w", D), ("b2", D), ("conv_b", D), ("beta", 3 * D), ("m2", 1))}
        g["c1"] = sb("c1", [P, 1])
        g["w"], g["row"], g["wide"] = weights, rowsb, wide
        g["same"] = dram("same", [EP], BF16)
        g["fresh"] = dram("fresh", [EP], BF16)
        g["ends"] = dram("ends", [EP], BF16)
        g["run"] = dram("run", [EP, D])
        g["run3"] = dram("run3", [EP, W3])
        g["seed"] = dram("seed", [EP, D])
        g["tab"] = dram("tab", [NP, D])
        g["tab_h"] = dram("tab_h", [NP, W2])
        g["low"] = dram("low", [EP], BF16)
        g["sent"] = dram("sent", [EP, D])
        g["dinv_row"] = dram("dinv_row", [NP])
        g["tab_kv"] = dram("tab_kv", [NP, 2 * D])
        g["off"] = dram("off", [NP + 1, 1], I32)
        g["ew"] = dram("ew", [EP, 1])
        g["xt"] = sb("xt", [P, NT, D])
        g["dinv"] = sb("dinv", [P, NT])
        g["dinv_low"] = sb("dinv_low", [P, 3, HIGH], BF16)

        setup(nc, d, g)
        edges_sum(nc, d, g)
        nodes(nc, g, 0, out)
        edges_max(nc, d, g)
        nodes(nc, g, 1, out)
        ew = sb("ew_sb", [P, TILES])
        edges_gate(nc, g, ew)
        degrees(nc, g, ew)
        edges_conv(nc, g, ew)
        nodes(nc, g, 2, out)
        edges_attention(nc, g)
        nodes(nc, g, 3, out)


def setup(nc, d, g):
    w, row, wide = g["w"], g["row"], g["wide"]
    loads = [
        (g["src"][:, :], d["src"]), (g["x"][:, :, :], d["x"].rearrange("(p t) f -> p t f", p=P)),
        (w["W0x"][:, :], d["L0_gnn_weight"][0:D, :]), (w["W0a"][:, :], d["L0_gnn_weight"][D:2 * D, :]),
        (w["W1s"][:, :], d["L1_gnn_W1"][0:D, :]), (w["W1d"][:, :], d["L1_gnn_W1"][D:2 * D, :]),
        (wide["W1w"][:, :], d["L1_gnn_W1"][2 * D:2 * D + 1, :].to_broadcast([P, D])),
        (w["W2"][:, :], d["L1_gnn_W2"]),
        (w["U1x"][:, :], d["L1_gnn_U1"][0:D, :]), (w["U1a"][:, :], d["L1_gnn_U1"][D:2 * D, :]),
        (w["U2"][:, :], d["L1_gnn_U2"]),
        (w["M1s"][:, :], d["L2_gnn_mlp_w1"][0:D, :]), (w["M1d"][:, :], d["L2_gnn_mlp_w1"][D:2 * D, :]),
        (w["M2"][:, :], d["L2_gnn_mlp_w2"]), (w["conv"][:, :], d["L2_gnn_conv_w"]),
        (w["Wkv"][:, 0:D], d["L3_gnn_Wk"]), (w["Wkv"][:, D:2 * D], d["L3_gnn_Wv"]),
        (w["Wq"][:, :], d["L3_gnn_Wq"]), (w["Wskip"][:, :], d["L3_gnn_Wskip"]),
        (g["c1"][:, :], d["L1_gnn_c1"].rearrange("(p a) -> p a", a=1)),
    ]
    line = lambda a: a.rearrange("(a n) -> a n", a=1)
    loads += [(row["b1"][:, :], line(d["L1_gnn_b1"])), (row["c2"][:, :], line(d["L1_gnn_c2"])),
              (row["m1"][:, :], line(d["L2_gnn_mlp_b1"])), (row["bq"][:, :], line(d["L3_gnn_bq"])),
              (row["bkv"][:, 0:D], line(d["L3_gnn_bk"])), (row["bkv"][:, D:2 * D], line(d["L3_gnn_bv"])),
              (row["bskip"][:, :], line(d["L3_gnn_bskip"]))]
    loads += [(wide["b2"][:, :], line(d["L1_gnn_b2"]).to_broadcast([P, D])),
              (wide["conv_b"][:, :], line(d["L2_gnn_conv_b"]).to_broadcast([P, D])),
              (wide["m2"][:, :], line(d["L2_gnn_mlp_b2"]).to_broadcast([P, 1]))]
    loads += [(wide["beta"][:, j * D:(j + 1) * D],
               d["L3_gnn_Wbeta"][j * D:(j + 1) * D, :].rearrange("n a -> a n").to_broadcast([P, D])) for j in range(3)]
    chunk = lambda a: a.rearrange("(p i) -> p i", p=P)
    with Phase(nc, "set") as ph:
        dst = [ph.sb(f"dst{j}", [P, TILES], I32) for j in range(3)]
        far = [ph.sb(f"far{j}", [P, TILES], BF16) for j in range(2)]
        src, low = ph.sb("src", [P, TILES], I32), ph.sb("low", [P, TILES], BF16)
        xs = [ph.sb(f"xs{k}", [P, BT, D]) for k in range(NSLOTS)]
        pT = [ph.ps(f"pT{k}") for k in range(NSLOTS)]
        s_dst, s_w, s_id, s_mask, s_tp, s_tc, s_link = (ph.sem(n) for n in ("dst", "w", "id", "mask", "tp", "tc", "link"))
        s_xs = ph.slot_sems("xs", NSLOTS)
        block = ph.block()

        @block.sync
        def _(sp):
            for j in range(3):
                sp.dma_start(dst[j][:, :], chunk(d["dst"][j:j + EP])).then_inc(s_dst, 16)
            sp.dma_start(src[:, :], chunk(d["src_row"])).then_inc(s_dst, 16)

            def load_x(n, k, r):
                room(sp, s_tp, n, NSLOTS)
                sp.dma_start(xs[k][:, :, :], d["x"].rearrange("(p t) f -> p t f", p=P)[:, bass.ds(n * BT, BT), :]).then_inc(s_xs[k], 16)
            pipeline(sp, NB, NSLOTS, [(0, load_x)])
            sp.wait_ge(s_mask, 1)
            sp.dma_start(chunk(g["same"]), g["same_c"][:, :]).then_inc(s_w, 16)
            sp.wait_ge(s_mask, 2)
            sp.dma_start(chunk(g["fresh"]), far[0][:, :]).then_inc(s_w, 16)
            sp.wait_ge(s_mask, 3)
            sp.dma_start(chunk(g["ends"]), far[1][:, :]).then_inc(s_w, 16)
            sp.wait_ge(s_mask, 4)
            sp.dma_start(chunk(g["low"]), low[:, :]).then_inc(s_w, 16)
            sp.wait_ge(s_w, 16 * (len(loads) + 4))

        @block.scalar
        def _(act):
            for to, a in loads:
                act.dma_start(to, a).then_inc(s_w, 16)

            def copy(n, k, r):
                need(act, s_tp, n)
                act.activation(g["xT"][:, bass.ds(n * BE, BE)], pT[k][:, :], ACT.Copy).then_inc(s_tc, 1)
            pipeline(act, NB, NSLOTS, [(0, copy)])

        @block.tensor
        def _(pe):
            pe.wait_ge(s_id, 2)

            def turn(n, k, r):
                landed(pe, s_xs, k, r)
                room(pe, s_tc, n, NSLOTS)
                for t in range(BT):
                    m = pe.transpose(pT[k][:, cols(t)], xs[k][:, t, :], g["ident"][:, :])
                m.then_inc(s_tp, 1)
            pipeline(pe, NB, NSLOTS, [(0, turn)])

        @block.gpsimd
        def _(gp):
            gp.memset(g["ident"][:, :], 0.0).then_inc(s_id, 1)
            gp.wait_ge(s_id, 1)
            gp.affine_select(out=g["ident"][:, :], in_=g["ident"][:, :], compare_op=ALU.not_equal, fill=1.0, base=0,
                             pattern=[[-1, P]], channel_multiplier=1).then_inc(s_id, 1)

        @block.vector
        def _(v):
            link = Chain(v, s_link)
            v.memset(g["ones"][:, :], 1.0)
            v.wait_ge(s_dst, 64)
            v.tensor_tensor(g["same_c"][:, :], dst[1][:, :], dst[0][:, :], ALU.is_equal).then_inc(s_mask, 1)
            link(v.tensor_tensor(far[0][:, :], dst[1][:, :], dst[0][:, :], ALU.not_equal))
            v.tensor_scalar(far[0][:, :], far[0][:, :], FAR, None, ALU.mult).then_inc(s_mask, 1)
            link(v.tensor_tensor(far[1][:, :], dst[1][:, :], dst[2][:, :], ALU.not_equal))
            v.tensor_scalar(far[1][:, :], far[1][:, :], FAR, None, ALU.mult).then_inc(s_mask, 1)
            link(v.tensor_scalar(src[:, :], src[:, :], P - 1, None, ALU.bitwise_and))
            v.tensor_copy(low[:, :], src[:, :]).then_inc(s_mask, 1)


class NodeEdges:

    FILL = SLOTS * BT

    def __init__(self, ph, d, g):
        assert BATCHES // SLOTS == NT
        self.d, self.g = d, g
        self.heads = ph.sb("heads", [P, TILES], I32)
        self.flag = ph.sb("flag", [P, TILES], BF16)
        self.node = ph.sb("node", [P, NT])
        self.tiles = ph.sb("tiles", [P, NT])
        self.inside = ph.sb("inside", [P, NT])
        self.tile_i = ph.sb("tile_i", [P, NT], I32)
        self.dst_row = [ph.sb(f"drow{k}", [P, BT, P], I32) for k in range(NSLOTS)]
        self.idx = [ph.sb(f"nidx{k}", [P, BT], I32) for k in range(NSLOTS)]
        self.le = ph.sb("le", [P, BT, P])
        self.off, self.a, self.b, self.c = (ph.sb(n, [P, NT]) for n in ("off", "ta", "tb", "tc"))
        self.off_i, self.first_i, self.high = (ph.sb(n, [P, NT], I32) for n in ("offi", "firsti", "high"))
        self.none = ph.sb("none", [1, 1], I32)
        self.zero = ph.sb("zeros", [P, self.FILL * D])
        (self.s_heads, self.s_iota, self.s_zero, self.s_fill, self.s_flag, self.s_count, self.s_tiles, self.s_off, self.s_back, self.s_cmp,
         self.s_ix, self.s_go, self.s_link) = (ph.sem(n) for n in ("heads", "iota", "zero", "fill", "flag", "count", "tilesd", "offd", "backd", "cmp",
                                                                   "nix", "ngo", "link"))
        self.s_le = ph.sem("le")
        self.s_row = ph.slot_sems("row", NSLOTS)

    def pool_before(self, gp):
        gp.memset(self.zero[:, :], 0.0).then_inc(self.s_zero, 1)
        gp.iota(self.off_i[:, :], [[1, NT]], base=0, channel_multiplier=NT).then_inc(self.s_iota, 1)

    def pool_after(self, gp):
        gp.wait_ge(self.s_tiles, 1)

        def fetch(n, k, r):
            room(gp, self.s_cmp, n, NSLOTS)
            gp.tensor_copy(self.idx[k][:, :], self.tile_i[:, bass.ds(n * BT, BT)]).then_inc(self.s_ix, 1)
            need(gp, self.s_ix, n)
            gp.sem_inc(self.s_go, 1)
            for t in range(BT):
                gp.indirect_dma_start(out=self.dst_row[k][:, t, :], out_offset=None, in_=self.d["dst_rows"],
                                      in_offset=bass.IndirectOffsetOnAxis(ap=self.idx[k][:, t:t + 1], axis=0)).then_inc(self.s_row[k], 16)
        pipeline(gp, NB, NSLOTS, [(0, fetch)])

    def sync_before(self, sp):
        sp.dma_start(self.heads[:, :], self.d["heads"].rearrange("(a n) -> a n", a=1).to_broadcast([P, TILES])).then_inc(self.s_heads, 16)
        sp.wait_ge(self.s_zero, 1)

    def sync_stage(self, sp):
        seed = self.g["seed"].rearrange("(p t) f -> p t f", p=P)

        def fill(n, k, r):
            if k == 0:
                if not isinstance(r, int) or r > 0:
                    sp.wait_ge(self.s_fill, 16 * r)
                sp.dma_start(seed[:, bass.ds(r * self.FILL, self.FILL), :], self.zero[:, :].rearrange("p (t f) -> p t f", t=self.FILL)).then_inc(self.s_fill, 16)
        return fill

    def sync_after(self, sp):
        g = self.g
        sp.wait_ge(self.s_off, 1)
        sp.dma_start(g["off"][1:NP + 1, :].rearrange("(p t) a -> p (t a)", p=P), self.off_i[:, :]).then_inc(self.s_back, 16)
        sp.dma_start(g["off"][0:1, :], self.none[:, :]).then_inc(self.s_back, 16)
        sp.wait_ge(self.s_back, 32)
        sp.dma_start(self.first_i[:, :], g["off"][0:NP, :].rearrange("(p t) a -> p (t a)", p=P)).then_inc(self.s_back, 16)
        sp.wait_ge(self.s_fill, 16 * (TILES // self.FILL))

    def vector_before(self, v):
        v.memset(self.none[:, :], 0)
        v.wait_ge(self.s_iota, 1)
        v.tensor_copy(self.node[:, :], self.off_i[:, :]).then_inc(self.s_count, 1)
        v.wait_ge(self.s_heads, 16)
        v.wait_ge(self.s_count, 1)

    def vector_stage(self, v):
        def stage(n, k, r):
            if k == 0:
                v.wait_ge(self.s_count, r + 1)
                v.tensor_scalar(self.flag[:, :], self.heads[:, :], self.node[:, bass.ds(r, 1)], None, ALU.is_le).then_inc(self.s_flag, 1)
            if k == 2:
                v.wait_ge(self.s_flag, r + 1)
                v.tensor_reduce(self.tiles[:, bass.ds(r, 1)], self.flag[:, :], AX, ALU.add).then_inc(self.s_count, 1)
        return stage

    def vector_after(self, v):
        g, link = self.g, Chain(v, self.s_link)
        tiles, inside, off, a, b, c = self.tiles, self.inside, self.off, self.a, self.b, self.c
        v.wait_ge(self.s_count, NT + 1)
        link(v.tensor_scalar(tiles[:, :], tiles[:, :], -1.0, 0.0, ALU.add, ALU.max))
        v.tensor_copy(self.tile_i[:, :], tiles[:, :]).then_inc(self.s_tiles, 1)

        def edges_upto(n, k, r):
            landed(v, self.s_row, k, r, BT)
            room(v, self.s_cmp, n, 1)
            v.tensor_tensor(self.le[:, :, :], self.dst_row[k][:, :, :],
                            self.node[:, bass.ds(n * BT, BT)].unsqueeze(2).to_broadcast([P, BT, P]), ALU.is_le).then_inc(self.s_le, 1)
            need(v, self.s_le, n)
            v.tensor_reduce(inside[:, bass.ds(n * BT, BT)], self.le[:, :, :], AX, ALU.add).then_inc(self.s_cmp, 1)
        pipeline(v, NB, NSLOTS, [(0, edges_upto)])
        need(v, self.s_cmp, NB - 1)
        link(v.scalar_tensor_tensor(off[:, :], tiles[:, :], float(P), inside[:, :], ALU.mult, ALU.add))
        v.tensor_copy(self.off_i[:, :], off[:, :]).then_inc(self.s_off, 1)
        link(v.tensor_scalar(a[:, :], off[:, :], -1.0, 0.0, ALU.add, ALU.max))
        link(v.tensor_copy(g["last_e"][:, :], a[:, :]))
        link(v.tensor_scalar(inside[:, :], inside[:, :], -1.0, 0.0, ALU.add, ALU.max))
        link(v.scalar_tensor_tensor(a[:, :], inside[:, :], float(TILES), tiles[:, :], ALU.mult, ALU.add))
        link(v.tensor_copy(g["last"][:, :], a[:, :]))
        v.wait_ge(self.s_back, 48)
        link(v.tensor_copy(b[:, :], self.first_i[:, :]))
        link(v.tensor_tensor(c[:, :], off[:, :], b[:, :], ALU.subtract))
        link(v.tensor_scalar(g["has"][:, :], c[:, :], 0.0, None, ALU.is_gt))
        link(v.tensor_scalar(c[:, :], c[:, :], 1.0, None, ALU.max))
        link(v.reciprocal(b[:, :], c[:, :]))
        link(v.tensor_tensor(g["mean"][:, :], b[:, :], g["has"][:, :], ALU.mult))
        link(v.tensor_scalar(self.high[:, :], self.first_i[:, :], 7, None, ALU.arith_shift_right))
        link(v.tensor_scalar(self.first_i[:, :], self.first_i[:, :], P - 1, None, ALU.bitwise_and))
        link(v.tensor_copy(a[:, :], self.first_i[:, :]))
        link(v.tensor_copy(b[:, :], self.high[:, :]))
        link(v.scalar_tensor_tensor(a[:, :], a[:, :], float(TILES), b[:, :], ALU.mult, ALU.add))
        link(v.tensor_scalar(a[:, :], a[:, :], float(-EP), None, ALU.add))
        link(v.tensor_tensor(a[:, :], a[:, :], g["has"][:, :], ALU.mult))
        link(v.tensor_scalar(a[:, :], a[:, :], float(EP), None, ALU.add))
        link(v.tensor_copy(g["first"][:, :], a[:, :]))


def edge_buffers(ph, width):
    gath = [ph.sb(f"gath{k}", [P, BT, width]) for k in range(SLOTS)]
    idx = [ph.sb(f"idx{k}", [P, BT], I32) for k in range(SLOTS)]
    return gath, idx, ph.slot_sems("gath", SLOTS), ph.sem("idx"), ph.sem("go")


def gatherer(gp, table, gath, idx, s_gath, s_idx, s_go, s_free, s_copied=None):
    def gather(n, k, r):
        if s_copied:
            stored(gp, s_copied, k, r)
        need(gp, s_idx, n)
        room(gp, s_free, n, SLOTS)
        gp.sem_inc(s_go, 1)
        for t in range(BT):
            gp.indirect_dma_start(out=gath[k][:, t, :], out_offset=None, in_=table,
                                  in_offset=bass.IndirectOffsetOnAxis(ap=idx[k][:, t:t + 1], axis=0)).then_inc(s_gath[k], 16)
    pipeline(gp, BATCHES, SLOTS, [(0, gather)])


def indexer(v, g, idx, s_idx, s_gath):
    for k in range(SLOTS):
        v.tensor_copy(idx[k][:, :], g["src"][:, k * BT:(k + 1) * BT]).then_inc(s_idx, 1)

    def ahead(n, k, r):
        landed(v, s_gath, k, r, BT)
        v.tensor_copy(idx[k][:, :], g["src"][:, bass.ds((n + SLOTS) * BT, BT)]).then_inc(s_idx, 1)
    return ahead


def start_of(acc, n, k):
    return 0.0 if isinstance(n, int) and n == 0 else acc[(k - 1) % len(acc)][:, BE - 1:BE]


def edges_sum(nc, d, g):
    with Phase(nc, "L0") as ph:
        gath, idx, s_gath, s_idx, s_go = edge_buffers(ph, D)
        mask = [ph.sb(f"mask{k}", [P, BE], BF16) for k in range(SLOTS)]
        acc = [ph.sb(f"acc{k}", [P, BE]) for k in range(SLOTS)]
        back = [ph.sb(f"back{k}", [P, BT, D]) for k in range(SLOTS)]
        pT = [ph.ps(f"pT{k}") for k in range(2)]
        pB = [ph.ps(f"pB{k}") for k in range(2)]
        s_turn, s_scan, s_ret, s_back = (ph.sem(n) for n in ("turn", "scan", "ret", "back"))
        s_mask, s_out = ph.slot_sems("mask", SLOTS), ph.slot_sems("out", SLOTS)
        run = g["run"].rearrange("(p t) f -> p t f", p=P)
        beside = NodeEdges(ph, d, g)
        block = ph.block()

        @block.sync
        def _(sp):
            beside.sync_before(sp)
            pipeline(sp, BATCHES, SLOTS, [(0, mask_load(sp, g["same"], mask, s_mask, s_scan)), (0, beside.sync_stage(sp))])
            beside.sync_after(sp)

        @block.gpsimd
        def _(gp):
            beside.pool_before(gp)
            gatherer(gp, d["x"], gath, idx, s_gath, s_idx, s_go, s_turn)
            beside.pool_after(gp)

        @block.tensor
        def _(pe):
            def turn(n, k, r):
                landed(pe, s_gath, k, r, BT)
                room(pe, s_scan, n, 2)
                for t in range(BT):
                    m = pe.transpose(pT[k % 2][:, cols(t)], gath[k][:, t, :], g["ident"][:, :])
                m.then_inc(s_turn, 1)
            pipeline(pe, BATCHES, SLOTS, [(0, turn), (1, turn_back(pe, g, acc, pB, s_scan, s_back, s_ret))])

        @block.vector
        def _(v):
            ahead = indexer(v, g, idx, s_idx, s_gath)
            beside.vector_before(v)
            pipeline(v, BATCHES, SLOTS, [(0, running_sum(v, pT, mask, acc, s_turn, s_mask, s_ret, s_scan)), (0, ahead),
                                         (0, beside.vector_stage(v))])
            beside.vector_after(v)

        @block.scalar
        def _(act):
            pipeline(act, BATCHES, SLOTS, [(2, store_rows(act, run, back, pB, s_ret, s_back, s_out))])
            all_stored(act, s_out)


def turn_back(pe, g, acc, pB, s_acc, s_back, s_ret):
    def ret(n, k, r):
        need(pe, s_acc, n)
        room(pe, s_back, n, 2)
        for t in range(BT):
            m = pe.transpose(pB[k % 2][:, cols(t)], acc[k][:, cols(t)], g["ident"][:, :])
        m.then_inc(s_ret, 1)
    return ret


def running_sum(v, pT, mask, acc, s_turn, s_mask, s_ret, s_scan):
    def scan(n, k, r):
        need(v, s_turn, n)
        landed(v, s_mask, k, r)
        room(v, s_ret, n, SLOTS)
        room(v, s_scan, n, 1)
        v.tensor_tensor_scan(acc[k][:, :], mask[k][:, :], pT[k % 2][:, :], start_of(acc, n, k), ALU.mult, ALU.add).then_inc(s_scan, 1)
    return scan


def store_rows(act, run, back, pB, s_ret, s_back, s_out):
    def store(n, k, r):
        need(act, s_ret, n)
        stored(act, s_out, k, r)
        act.activation(rows(back[k][:, :, :]), pB[k % 2][:, :], ACT.Copy).then_inc(s_back, 1)
        need(act, s_back, n)
        act.dma_start(run[:, bass.ds(n * BT, BT), :], back[k][:, :, :]).then_inc(s_out[k], 16)
    return store


def all_stored(eng, s_out):
    for k in range(SLOTS):
        eng.wait_ge(s_out[k], 16 * BATCHES // SLOTS)


def edges_conv(nc, g, ew):
    with Phase(nc, "L2") as ph:
        slot = lambda name, shape, dtype=F32: [ph.sb(f"{name}{k}", shape, dtype) for k in range(SLOTS)]
        mask, low = slot("mask", [P, BE], BF16), slot("low", [P, BE], BF16)
        sent, scaled, back = (slot(n, [P, BT, D]) for n in ("sent", "scaled", "back"))
        acc, hot_low, hot_high = slot("acc", [P, BE]), slot("hotl", [P, BE], BF16), slot("hoth", [P, BT, HIGH], BF16)
        found, scale = slot("found", [P, BT]), slot("scale", [P, BT])
        part = [ph.sb(f"part{k}", [P, BT, HIGH]) for k in range(2)]
        high = ph.sb("high", [P, TILES], BF16)
        work = ph.sb("work", [P, TILES], I32)
        lane_i, lane, row_i, row = ph.sb("lane_i", [P, 1], I32), ph.sb("lane", [P, 1]), ph.sb("row_i", [P, HIGH], I32), ph.sb("row", [P, HIGH], BF16)
        pT = [ph.ps(f"pT{k}") for k in range(2)]
        pB = [ph.ps(f"pB{k}") for k in range(2)]
        pL = [ph.ps(f"pL{k}") for k in range(2)]
        s_iota, s_prep, s_hotl, s_hoth, s_look, s_part, s_pick, s_scale, s_turn, s_scan, s_ret, s_back, s_sum = (ph.sem(n) for n in
            ("iota", "prep", "hotl", "hoth", "look", "part", "pick", "scale", "turn", "scan", "ret", "back", "sum"))
        s_mask, s_low, s_sent, s_out = (ph.slot_sems(n, SLOTS) for n in ("mask", "low", "sent", "out"))
        run = g["run"].rearrange("(p t) f -> p t f", p=P)
        table = g["sent"].rearrange("(p t) f -> p t f", p=P)
        block = ph.block()

        @block.sync
        def _(sp):
            def load(n, k, r):
                room(sp, s_scale, n, SLOTS)
                sp.dma_start(sent[k][:, :, :], table[:, bass.ds(n * BT, BT), :]).then_inc(s_sent[k], 16)
            pipeline(sp, BATCHES, SLOTS, [(0, mask_load(sp, g["low"], low, s_low, s_hotl)), (0, load),
                                          (2, mask_load(sp, g["same"], mask, s_mask, s_scan))])

        @block.gpsimd
        def _(gp):
            gp.iota(lane_i[:, :], [[1, 1]], base=0, channel_multiplier=1).then_inc(s_iota, 1)
            gp.iota(row_i[:, :], [[1, HIGH]], base=0, channel_multiplier=0).then_inc(s_iota, 1)

        @block.tensor
        def _(pe):
            def look(n, k, r):
                need(pe, s_hotl, n)
                room(pe, s_part, n, 2)
                for t in range(BT):
                    for j in range(3):
                        m = pe.matmul(pL[k % 2][:, t * HIGH:(t + 1) * HIGH], hot_low[k][:, cols(t)], g["dinv_low"][:, j, :],
                                      start=j == 0, stop=j == 2)
                m.then_inc(s_look, 1)

            def turn(n, k, r):
                need(pe, s_scale, n)
                room(pe, s_scan, n, 2)
                for t in range(BT):
                    m = pe.transpose(pT[k % 2][:, cols(t)], scaled[k][:, t, :], g["ident"][:, :])
                m.then_inc(s_turn, 1)
            pipeline(pe, BATCHES, SLOTS, [(0, look), (2, turn), (4, turn_back(pe, g, acc, pB, s_scan, s_back, s_ret))])

        @block.vector
        def _(v):
            v.wait_ge(s_iota, 2)
            v.tensor_copy(lane[:, :], lane_i[:, :]).then_inc(s_prep, 1)
            v.tensor_copy(row[:, :], row_i[:, :]).then_inc(s_prep, 1)
            v.tensor_scalar(work[:, :], g["src"][:, 0:TILES], LO, None, ALU.arith_shift_right).then_inc(s_prep, 1)
            v.wait_ge(s_prep, 3)
            v.tensor_copy(high[:, :], work[:, :]).then_inc(s_prep, 1)
            v.wait_ge(s_prep, 4)

            def hot(n, k, r):
                landed(v, s_low, k, r)
                room(v, s_look, n, SLOTS)
                v.tensor_scalar(hot_low[k][:, :], low[k][:, :], lane[:, 0:1], None, ALU.is_equal).then_inc(s_hotl, 1)

            def hot_of_high(n, k, r):
                room(v, s_part, n, SLOTS)
                v.tensor_tensor(hot_high[k][:, :, :], row[:, :].unsqueeze(1).to_broadcast([P, BT, HIGH]),
                                high[:, bass.ds(n * BT, BT)].unsqueeze(2).to_broadcast([P, BT, HIGH]), ALU.is_equal).then_inc(s_hoth, 1)

            def pick(n, k, r):
                need(v, s_look, n)
                need(v, s_hoth, n)
                room(v, s_sum, n, 2)
                v.tensor_tensor(rows(part[k % 2][:, :, :]), pL[k % 2][:, 0:BT * HIGH], rows(hot_high[k][:, :, :]), ALU.mult).then_inc(s_part, 1)

            def gather_up(n, k, r):
                need(v, s_part, n)
                v.tensor_reduce(found[k][:, :], part[k % 2][:, :, :], AX, ALU.add).then_inc(s_sum, 1)

            def times_weight(n, k, r):
                need(v, s_sum, n)
                room(v, s_scale, n, SLOTS)
                v.tensor_tensor(scale[k][:, :], found[k][:, :], ew[:, bass.ds(n * BT, BT)], ALU.mult).then_inc(s_pick, 1)
            pipeline(v, BATCHES, SLOTS, [(0, hot), (1, pick), (0, hot_of_high), (1, gather_up), (3, running_sum(v, pT, mask, acc, s_turn, s_mask, s_ret, s_scan)),
                                         (1, times_weight)])

        @block.scalar
        def _(act):
            def weigh(n, k, r):
                landed(act, s_sent, k, r)
                need(act, s_pick, n)
                room(act, s_turn, n, SLOTS)
                for t in range(BT):
                    a = act.activation(scaled[k][:, t, :], sent[k][:, t, :], ACT.Copy, scale=scale[k][:, t:t + 1])
                a.then_inc(s_scale, 1)
            pipeline(act, BATCHES, SLOTS, [(0, weigh), (3, store_rows(act, run, back, pB, s_ret, s_back, s_out))])
            all_stored(act, s_out)


def mask_load(sp, table, mask, s_mask, s_free):
    def load(n, k, r):
        room(sp, s_free, n, SLOTS)
        sp.dma_start(mask[k][:, :], table[bass.ds(n * BE, BE)].unsqueeze(0).to_broadcast([P, BE])).then_inc(s_mask[k], 16)
    return load


def edges_max(nc, d, g):
    w = g["w"]
    with Phase(nc, "L1") as ph:
        gath, idx, s_gath, s_idx, s_go = edge_buffers(ph, D)
        slot = lambda name, width=BE, dtype=F32: [ph.sb(f"{name}{k}", [P, width], dtype) for k in range(SLOTS)]
        weight = ph.sb("weight", [P, TILES])
        same, fresh = slot("same", BE, BF16), slot("fresh", BE, BF16)
        seed, sent, dest, pre, hid, acc = (slot(n) for n in ("seed", "sent", "dest", "pre", "hid", "acc"))
        back = [ph.sb(f"back{k}", [P, BT, D]) for k in range(SLOTS)]
        pA = [ph.ps(f"pA{k}") for k in range(2)]
        pS = [ph.ps(f"pS{k}") for k in range(2)]
        pM = [ph.ps(f"pM{k}") for k in range(2)]
        pB = [ph.ps(f"pB{k}") for k in range(2)]
        s_wt, s_sent, s_turn, s_turns, s_dest, s_pre, s_hid, s_msg, s_max, s_ret, s_back = (ph.sem(n) for n in
            ("wt", "sent", "turn", "turns", "dest", "pre", "hid", "msg", "max", "ret", "back"))
        s_same, s_fresh, s_seed, s_out = (ph.slot_sems(n, SLOTS) for n in ("same", "fresh", "seed", "out"))
        run = g["run"].rearrange("(p t) f -> p t f", p=P)
        seeds = g["seed"].rearrange("(p t) f -> p t f", p=P)
        block = ph.block()

        @block.sync
        def _(sp):
            sp.dma_start(weight[:, :], d["weight"]).then_inc(s_wt, 16)

            def load_seed(n, k, r):
                room(sp, s_turns, n, SLOTS)
                sp.dma_start(seed[k][:, :].rearrange("p (t f) -> p t f", t=BT), seeds[:, bass.ds(n * BT, BT), :]).then_inc(s_seed[k], 16)
            pipeline(sp, BATCHES, SLOTS, [(0, load_seed), (0, mask_load(sp, g["same"], same, s_same, s_dest)),
                                          (0, mask_load(sp, g["fresh"], fresh, s_fresh, s_max))])

        @block.gpsimd
        def _(gp):
            gatherer(gp, g["tab"], gath, idx, s_gath, s_idx, s_go, s_sent)

        @block.tensor
        def _(pe):
            def turn_seed(n, k, r):
                landed(pe, s_seed, k, r)
                room(pe, s_dest, n, 2)
                for t in range(BT):
                    m = pe.transpose(pS[k % 2][:, cols(t)], seed[k][:, cols(t)], g["ident"][:, :])
                m.then_inc(s_turns, 1)

            def turn(n, k, r):
                need(pe, s_sent, n)
                room(pe, s_pre, n, 2)
                for t in range(BT):
                    m = pe.transpose(pA[k % 2][:, cols(t)], sent[k][:, cols(t)], g["ident"][:, :])
                m.then_inc(s_turn, 1)

            def message(n, k, r):
                need(pe, s_hid, n)
                room(pe, s_max, n, 2)
                pe.matmul(pM[k % 2][:, :], w["W2"][:, :], hid[k][:, :], start=True, stop=True).then_inc(s_msg, 1)

            pipeline(pe, BATCHES, SLOTS, [(0, turn_seed), (0, turn), (1, message), (2, turn_back(pe, g, acc, pB, s_max, s_back, s_ret))])

        @block.vector
        def _(v):
            def add_weight(n, k, r):
                landed(v, s_gath, k, r, BT)
                room(v, s_turn, n, SLOTS)
                for t in range(BT):
                    a = v.scalar_tensor_tensor(sent[k][:, cols(t)], g["wide"]["W1w"][:, :], weight[:, bass.ds(n * BT + t, 1)],
                                               gath[k][:, t, :], ALU.mult, ALU.add)
                a.then_inc(s_sent, 1)

            def spread(n, k, r):
                need(v, s_turns, n)
                landed(v, s_same, k, r)
                room(v, s_dest, n, 1)
                room(v, s_pre, n, SLOTS)
                v.tensor_tensor_scan(dest[k][:, :], same[k][:, :], pS[k % 2][:, :], start_of(dest, n, k), ALU.mult, ALU.add).then_inc(s_dest, 1)

            def add_dest(n, k, r):
                need(v, s_turn, n)
                need(v, s_dest, n)
                room(v, s_hid, n, SLOTS)
                v.tensor_tensor(pre[k][:, :], pA[k % 2][:, :], dest[k][:, :], ALU.add).then_inc(s_pre, 1)

            def top(n, k, r):
                need(v, s_msg, n)
                landed(v, s_fresh, k, r)
                room(v, s_max, n, 1)
                room(v, s_ret, n, SLOTS)
                v.tensor_tensor_scan(acc[k][:, :], fresh[k][:, :], pM[k % 2][:, :], start_of(acc, n, k), ALU.add, ALU.max).then_inc(s_max, 1)
            v.wait_ge(s_wt, 16)
            ahead = indexer(v, g, idx, s_idx, s_gath)
            pipeline(v, BATCHES, SLOTS, [(0, add_weight), (0, ahead), (0, spread), (0, add_dest), (2, top)])

        @block.scalar
        def _(act):
            def relu(n, k, r):
                need(act, s_pre, n)
                room(act, s_msg, n, SLOTS)
                act.activation(hid[k][:, :], pre[k][:, :], ACT.Relu).then_inc(s_hid, 1)

            pipeline(act, BATCHES, SLOTS, [(0, relu), (3, store_rows(act, run, back, pB, s_ret, s_back, s_out))])
            all_stored(act, s_out)


def edges_gate(nc, g, z):
    w = g["w"]
    H = slice(0, HID)
    with Phase(nc, "L2a") as ph:
        gath, idx, s_gath, s_idx, s_go = edge_buffers(ph, W2)
        slot = lambda name, width=BE, dtype=F32, p=HID: [ph.sb(f"{name}{k}", [p, width], dtype) for k in range(SLOTS)]
        same, seed = slot("same", BE, BF16), slot("seed", BT * HID, F32, P)
        dest, pre, hid = (slot(n) for n in ("dest", "pre", "hid"))
        pA = [ph.ps(f"pA{k}") for k in range(2)]
        pS = [ph.ps(f"pS{k}") for k in range(2)]
        pZ = [ph.ps(f"pZ{k}") for k in range(2)]
        s_turn, s_turns, s_dest, s_pre, s_hid, s_dot, s_z, s_tgo = (ph.sem(n) for n in
            ("turn", "turns", "dest", "pre", "hid", "dot", "z", "tgo"))
        s_same, s_seed, s_aside = (ph.slot_sems(n, SLOTS) for n in ("same", "seed", "aside"))
        aside = g["sent"].rearrange("(p t) f -> p t f", p=P)
        seeds = g["seed"].rearrange("(p t) f -> p t f", p=P)
        block = ph.block()

        @block.sync
        def _(sp):
            def load_seed(n, k, r):
                room(sp, s_turns, n, SLOTS)
                sp.dma_start(seed[k][:, :].rearrange("p (t f) -> p t f", t=BT), seeds[:, bass.ds(n * BT, BT), 0:HID]).then_inc(s_seed[k], 16)

            def load_same(n, k, r):
                room(sp, s_dest, n, SLOTS)
                sp.dma_start(same[k][:, :], g["same"][bass.ds(n * BE, BE)].unsqueeze(0).to_broadcast([HID, BE])).then_inc(s_same[k], 16)
            pipeline(sp, BATCHES, SLOTS, [(0, load_seed), (0, load_same)])

        @block.gpsimd
        def _(gp):
            gatherer(gp, g["tab_h"], gath, idx, s_gath, s_idx, s_go, s_turn, s_aside)

        @block.tensor
        def _(pe):
            def turn(n, k, r):
                landed(pe, s_seed, k, r)
                room(pe, s_dest, n, 2)
                pe.sem_inc(s_tgo, 1)
                for t in range(BT):
                    m = pe.transpose(pS[k % 2][H, cols(t)], seed[k][:, t * HID:(t + 1) * HID], g["ident"][:, :])
                m.then_inc(s_turns, 1)
                landed(pe, s_gath, k, r, BT)
                room(pe, s_pre, n, 2)
                pe.sem_inc(s_tgo, 1)
                for t in range(BT):
                    m = pe.transpose(pA[k % 2][H, cols(t)], gath[k][:, t, H], g["ident"][:, :])
                m.then_inc(s_turn, 1)

            def dot(n, k, r):
                need(pe, s_hid, n)
                room(pe, s_z, n, 2)
                for t in range(BT):
                    m = pe.matmul(pZ[k % 2][:, t:t + 1], hid[k][:, cols(t)], w["M2"][:, :], start=True, stop=True)
                m.then_inc(s_dot, 1)
            pipeline(pe, BATCHES, SLOTS, [(0, turn), (2, dot)])

        @block.vector
        def _(v):
            def spread(n, k, r):
                need(v, s_turns, n)
                landed(v, s_same, k, r)
                room(v, s_dest, n, 1)
                room(v, s_pre, n, SLOTS)
                v.tensor_tensor_scan(dest[k][:, :], same[k][:, :], pS[k % 2][H, :], start_of(dest, n, k), ALU.mult, ALU.add).then_inc(s_dest, 1)

            def add_dest(n, k, r):
                need(v, s_turn, n)
                need(v, s_dest, n)
                room(v, s_hid, n, SLOTS)
                v.tensor_tensor(pre[k][:, :], pA[k % 2][H, :], dest[k][:, :], ALU.add).then_inc(s_pre, 1)

            def keep(n, k, r):
                need(v, s_dot, n)
                v.tensor_copy(z[:, bass.ds(n * BT, BT)], pZ[k % 2][:, 0:BT]).then_inc(s_z, 1)
            ahead = indexer(v, g, idx, s_idx, s_gath)
            pipeline(v, BATCHES, SLOTS, [(0, spread), (0, add_dest), (0, ahead), (3, keep)])

        @block.scalar
        def _(act):
            def gelu(n, k, r):
                need(act, s_pre, n)
                room(act, s_dot, n, SLOTS)
                act.activation(hid[k][:, :], pre[k][:, :], ACT.Gelu).then_inc(s_hid, 1)

            def put_aside(n, k, r):
                landed(act, s_gath, k, r, BT)
                act.dma_start(aside[:, bass.ds(n * BT, BT), :], gath[k][:, :, HID:W2]).then_inc(s_aside[k], 16)
            pipeline(act, BATCHES, SLOTS, [(0, put_aside), (0, gelu)])
            all_stored(act, s_aside)


def degrees(nc, g, ew):
    with Phase(nc, "deg") as ph:
        wide_t = -(-TILES // P)
        lin = [ph.sb(f"lin{k}", [P, P]) for k in range(2)]
        c = ph.sb("c", [P, TILES])
        run = ph.sb("run", [P, TILES])
        open_ = ph.sb("open", [P, TILES])
        ends = ph.sb("ends", [1, 2, P])
        carry = ph.sb("carry", [1, P + 1])
        cin = ph.sb("cin", [P, 1])
        deg = ph.sb("deg", [P, NT])
        by_high, rest = ph.sb("by_high", [HIGH, P]), ph.sb("rest", [P, HIGH])
        idx = [ph.sb(f"idx{k}", [P, BT], I32) for k in range(NSLOTS)]
        got = [ph.sb(f"got{k}", [P, BT]) for k in range(NSLOTS)]
        pT = [ph.ps(f"pT{k}") for k in range(2)]
        pE = ph.ps("pE")
        pC = ph.ps("pC")
        s_sig, s_t, s_lin, s_c, s_v, s_pe, s_run, s_ix, s_go, s_got, s_deg, s_lay = (ph.sem(n) for n in
            ("sig", "t", "lin", "c", "v", "pe", "run", "ix", "go", "got", "deg", "lay"))
        s_ld, s_gath = ph.slot_sems("ld", 2), ph.slot_sems("gath", NSLOTS)
        block = ph.block()

        @block.scalar
        def _(act):
            act.activation(ew[:, :], ew[:, :], ACT.Sigmoid, bias=g["wide"]["m2"][:, 0:1]).then_inc(s_sig, 1)
            for j in range(wide_t):
                width = min(P, TILES - j * P)
                need(act, s_t, j)
                if j >= 2:
                    act.wait_ge(s_ld[j % 2], 16 * (j // 2))
                act.activation(lin[j % 2][0:width, :], pT[j % 2][0:width, 0:P], ACT.Copy).then_inc(s_lin, 1)
                need(act, s_lin, j)
                act.dma_start(g["ew"].rearrange("(t l) a -> t (l a)", l=P)[j * P:j * P + width, :], lin[j % 2][0:width, :]).then_inc(s_ld[j % 2], 16)
            for k in range(2):
                act.wait_ge(s_ld[k], 16 * len(range(k, wide_t, 2)))
            act.dma_start(c[:, :], g["ew"].rearrange("(p i) a -> p (i a)", p=P)).then_inc(s_c, 16)
            act.wait_ge(s_run, 1)
            act.dma_start(g["ew"].rearrange("(p i) a -> p (i a)", p=P), run[:, :]).then_inc(s_c, 16)
            act.wait_ge(s_c, 32)
            act.sem_inc(s_run, 1)
            act.wait_ge(s_deg, 1)
            act.activation(deg[:, :], deg[:, :], ACT.Sqrt).then_inc(s_deg, 1)

        @block.tensor
        def _(pe):
            pe.wait_ge(s_sig, 1)
            for j in range(wide_t):
                width = min(P, TILES - j * P)
                room(pe, s_lin, j, 2)
                pe.transpose(pT[j % 2][0:width, 0:P], ew[:, j * P:j * P + width], g["ident"][:, :]).then_inc(s_t, 1)
            pe.wait_ge(s_v, 2)
            pe.transpose(pE[0:1, 0:P], run[:, TILES - 1:TILES], g["ident"][:, :])
            pe.transpose(pE[0:1, P:2 * P], open_[:, TILES - 1:TILES], g["ident"][:, :]).then_inc(s_pe, 1)
            pe.wait_ge(s_v, 5)
            pe.matmul(pC[:, 0:1], carry[0:1, 0:P], g["ones"][0:1, 0:1], start=True, stop=True).then_inc(s_pe, 1)
            pe.wait_ge(s_lay, 32)
            pe.transpose(pC[:, P:P + HIGH], by_high[:, :], g["ident"][0:HIGH, 0:HIGH]).then_inc(s_pe, 1)

        @block.vector
        def _(v):
            link = Chain(v, s_v)
            v.wait_ge(s_c, 16)
            link(v.tensor_tensor_scan(run[:, :], g["same_c"][:, :], c[:, :], 0.0, ALU.mult, ALU.add))
            link(v.tensor_tensor_scan(open_[:, :], g["same_c"][:, :], g["same_c"][:, :], 1.0, ALU.mult, ALU.min))
            v.wait_ge(s_pe, 1)
            link(v.memset(carry[:, :], 0.0))
            link(v.tensor_copy(ends[:, :, :].rearrange("a b c -> a (b c)"), pE[0:1, 0:2 * P]))
            link(v.tensor_tensor_scan(carry[0:1, 1:P + 1], ends[0:1, 1, :], ends[0:1, 0, :], 0.0, ALU.mult, ALU.add))
            v.wait_ge(s_pe, 2)
            link(v.tensor_copy(cin[:, :], pC[:, 0:1]))
            v.scalar_tensor_tensor(run[:, :], open_[:, :], cin[:, 0:1], run[:, :], ALU.mult, ALU.add).then_inc(s_run, 1)

            def keep(n, k, r):
                landed(v, s_gath, k, r, BT)
                v.tensor_copy(deg[:, bass.ds(n * BT, BT)], got[k][:, :]).then_inc(s_got, 1)
            pipeline(v, NB, NSLOTS, [(0, keep)])
            v.wait_ge(s_got, NB)
            link(v.tensor_tensor(deg[:, :], deg[:, :], g["has"][:, :], ALU.mult))
            v.tensor_scalar(deg[:, :], deg[:, :], 1.0, None, ALU.add).then_inc(s_deg, 1)
            v.wait_ge(s_deg, 2)
            v.reciprocal(g["dinv"][:, :], deg[:, :]).then_inc(s_deg, 1)
            v.wait_ge(s_pe, 3)
            link(v.tensor_copy(rest[:, :], pC[:, P:P + HIGH]))
            for j in range(3):
                link(v.tensor_copy(g["dinv_low"][:, j, :], rest[:, :]))
                if j < 2:
                    link(v.tensor_tensor(rest[:, :], rest[:, :], g["dinv_low"][:, j, :], ALU.subtract))

        @block.gpsimd
        def _(gp):
            gp.wait_ge(s_run, 2)

            def fetch(n, k, r):
                room(gp, s_got, n, NSLOTS)
                gp.tensor_copy(idx[k][:, :], g["last_e"][:, bass.ds(n * BT, BT)]).then_inc(s_ix, 1)
                need(gp, s_ix, n)
                gp.sem_inc(s_go, 1)
                for t in range(BT):
                    gp.indirect_dma_start(out=got[k][:, t:t + 1], out_offset=None, in_=g["ew"],
                                          in_offset=bass.IndirectOffsetOnAxis(ap=idx[k][:, t:t + 1], axis=0)).then_inc(s_gath[k], 16)
            pipeline(gp, NB, NSLOTS, [(0, fetch)])

        @block.sync
        def _(sp):
            sp.wait_ge(s_deg, 3)
            sp.dma_start(g["dinv_row"].rearrange("(p t) -> p t", p=P), g["dinv"][:, :]).then_inc(s_lay, 16)
            sp.wait_ge(s_lay, 16)
            sp.dma_start(by_high[:, :], g["dinv_row"].rearrange("(h l) -> h l", l=P)).then_inc(s_lay, 16)


def edges_attention(nc, g):
    with Phase(nc, "L3") as ph:
        gath, idx, s_gath, s_idx, s_go = edge_buffers(ph, 2 * D)
        slot = lambda name, width=BE, dtype=F32, c=2: [ph.sb(f"{name}{k}", [P, width], dtype) for k in range(c)]
        same, fresh, ends = (slot(n, BE, BF16, SLOTS) for n in ("same", "fresh", "ends"))
        seed = slot("seed", BE, F32, SLOTS)
        dest, prod, top, ref, back_by, prob, pv, num, den = (slot(n, w, F32, c) for n, w, c in (
            ("dest", BE, 2), ("prod", BE, 2), ("top", BE, 2), ("ref", BE, 2), ("back_by", 1, 2), ("prob", BE + 1, 2),
            ("pv", BE, 1), ("num", BE, 2), ("den", BE, 2)))
        pv = pv[0]
        start, zero = slot("start", 2, F32, 1)[0], slot("zero", 1, F32, 1)[0]
        back = [ph.sb(f"back{k}", [P, BT, W3]) for k in range(SLOTS)]
        blocks = ph.sb("blocks", [P, P])
        minus = ph.sb("minus", [P, P])
        pS, pK, pB, pD = (ph.ps(n) for n in ("pS", "pK", "pB", "pD"))
        pV = [ph.ps(f"pV{k}") for k in range(2)]
        pC = [ph.ps(f"pC{k}") for k in range(2)]
        (s_c, s_cc, s_turns, s_turnk, s_turnv, s_dest, s_prod, s_score, s_top, s_ref, s_diff, s_prob, s_pv, s_init, s_num, s_den,
         s_ret, s_back, s_col) = (ph.sem(n) for n in ("c", "cc", "turns", "turnk", "turnv", "dest", "prod", "score", "top", "ref",
                                      "diff", "prob", "pv", "init", "num", "den", "ret", "back", "col"))
        s_same, s_fresh, s_ends, s_seed, s_out = (ph.slot_sems(n, SLOTS) for n in ("same", "fresh", "ends", "seed", "out"))
        run = g["run3"].rearrange("(p t) f -> p t f", p=P)
        seeds = g["seed"].rearrange("(p t) f -> p t f", p=P)
        block = ph.block()

        @block.sync
        def _(sp):
            def load_seed(n, k, r):
                room(sp, s_turns, n, SLOTS)
                sp.dma_start(seed[k][:, :].rearrange("p (t f) -> p t f", t=BT), seeds[:, bass.ds(n * BT, BT), :]).then_inc(s_seed[k], 16)
            pipeline(sp, BATCHES, SLOTS, [(0, load_seed), (0, mask_load(sp, g["same"], same, s_same, s_num)),
                                          (0, mask_load(sp, g["fresh"], fresh, s_fresh, s_top)),
                                          (0, mask_load(sp, g["ends"], ends, s_ends, s_ref))])

        @block.gpsimd
        def _(gp):
            gatherer(gp, g["tab_kv"], gath, idx, s_gath, s_idx, s_go, s_turnv)

        @block.tensor
        def _(pe):
            def turn(n, k, r):
                landed(pe, s_seed, k, r)
                room(pe, s_dest, n, 1)
                for t in range(BT):
                    m = pe.transpose(pS[:, cols(t)], seed[k][:, cols(t)], g["ident"][:, :])
                m.then_inc(s_turns, 1)
                landed(pe, s_gath, k, r, BT)
                room(pe, s_prod, n, 1)
                for t in range(BT):
                    m = pe.transpose(pK[:, cols(t)], gath[k][:, t, 0:D], g["ident"][:, :])
                m.then_inc(s_turnk, 1)

            def turn_values(n, k, r):
                room(pe, s_pv, n, 2)
                for t in range(BT):
                    m = pe.transpose(pV[k % 2][:, cols(t)], gath[k][:, t, D:2 * D], g["ident"][:, :])
                m.then_inc(s_turnv, 1)

            def score(n, k, r):
                need(pe, s_prod, n)
                room(pe, s_prob, n, 2)
                pe.matmul(pC[k % 2][:, :], blocks[:, :], prod[k % 2][:, :], start=True, stop=True).then_inc(s_score, 1)

            def distance(n, k, r):
                need(pe, s_top, n)
                need(pe, s_ref, n)
                pe.matmul(pC[k % 2][:, :], minus[:, :], ref[k % 2][:, :], start=False, stop=True, skip_group_check=True).then_inc(s_diff, 1)

            def ret(n, k, r):
                need(pe, s_num, n)
                need(pe, s_den, n)
                room(pe, s_back, n, 1)
                for t in range(BT):
                    pe.transpose(pB[:, cols(t)], num[k % 2][:, cols(t)], g["ident"][:, :])
                for t in range(BT):
                    m = pe.transpose(pD[:, cols(t)], den[k % 2][:, cols(t)], g["ident"][:, :])
                m.then_inc(s_ret, 1)
            pe.wait_ge(s_cc, HEADS + 1)
            pipeline(pe, BATCHES, SLOTS, [(0, turn), (1, distance), (0, score), (1, turn_values), (3, ret)])

        @block.vector
        def _(v):
            v.memset(blocks[:, :], 0.0).then_inc(s_c, 1)
            v.memset(zero[:, :], 0.0).then_inc(s_c, 1)
            v.tensor_scalar(minus[:, :], g["ident"][:, :], -1.0, None, ALU.mult).then_inc(s_cc, 1)
            v.wait_ge(s_c, 2)
            for h in range(HEADS):
                part = slice(h * HEAD, (h + 1) * HEAD)
                v.memset(blocks[part, part], float(HEAD) ** -0.5).then_inc(s_cc, 1)

            def spread(n, k, r):
                need(v, s_turns, n)
                landed(v, s_same, k, r)
                room(v, s_dest, n, 1)
                room(v, s_prod, n, 2)
                v.tensor_tensor_scan(dest[k % 2][:, :], same[k][:, :], pS[:, :], start_of(dest, n, k % 2), ALU.mult, ALU.add).then_inc(s_dest, 1)

            def query(n, k, r):
                need(v, s_turnk, n)
                need(v, s_dest, n)
                room(v, s_score, n, 2)
                v.tensor_tensor(prod[k % 2][:, :], pK[:, :], dest[k % 2][:, :], ALU.mult).then_inc(s_prod, 1)

            def peak(n, k, r):
                need(v, s_score, n)
                landed(v, s_fresh, k, r)
                room(v, s_top, n, 1)
                room(v, s_ref, n, 2)
                v.tensor_tensor_scan(top[k % 2][:, :], fresh[k][:, :], pC[k % 2][:, :], start_of(top, n, k % 2), ALU.add, ALU.max).then_inc(s_top, 1)

            def reference(n, k, r):
                landed(v, s_ends, k, r)
                need(v, s_top, n)
                room(v, s_diff, n, 1)
                v.tensor_tensor_scan(ref[k % 2][:, ::-1], ends[k][:, ::-1], top[k % 2][:, ::-1], FAR, ALU.add, ALU.max).then_inc(s_ref, 1)

            def step_back(n, k, r):
                need(v, s_ref, n)
                room(v, s_prob, n, 2)
                if isinstance(n, int) and n == 0:
                    v.memset(back_by[k % 2][:, :], 0.0).then_inc(s_col, 1)
                else:
                    v.scalar_tensor_tensor(back_by[k % 2][:, :], ref[(k - 1) % 2][:, BE - 1:BE], ref[k % 2][:, 0:1], zero[:, :],
                                           ALU.subtract, ALU.min).then_inc(s_col, 1)

            def weigh(n, k, r):
                need(v, s_prob, n)
                need(v, s_turnv, n)
                room(v, s_num, n, 1)
                v.tensor_tensor(pv[:, :], pV[k % 2][:, :], prob[k % 2][:, 0:BE], ALU.mult).then_inc(s_pv, 1)

            def rescale(n, k, r):
                need(v, s_prob, n)
                room(v, s_num, n, 1)
                if isinstance(n, int) and n == 0:
                    v.memset(start[:, :], 0.0).then_inc(s_init, 1)
                else:
                    v.tensor_tensor(start[:, 0:1], num[(k - 1) % 2][:, BE - 1:BE], prob[k % 2][:, BE:BE + 1], ALU.mult)
                    v.tensor_tensor(start[:, 1:2], den[(k - 1) % 2][:, BE - 1:BE], prob[k % 2][:, BE:BE + 1], ALU.mult).then_inc(s_init, 1)

            def total(n, k, r):
                landed(v, s_same, k, r)
                need(v, s_init, n)
                room(v, s_ret, n, 2)
                v.tensor_tensor_scan(den[k % 2][:, :], same[k][:, :], prob[k % 2][:, 0:BE], start[:, 1:2], ALU.mult, ALU.add).then_inc(s_den, 1)
                need(v, s_pv, n)
                v.tensor_tensor_scan(num[k % 2][:, :], same[k][:, :], pv[:, :], start[:, 0:1], ALU.mult, ALU.add).then_inc(s_num, 1)
            ahead = indexer(v, g, idx, s_idx, s_gath)
            pipeline(v, BATCHES, SLOTS, [(1, peak), (0, spread), (1, reference), (0, query), (0, ahead), (1, step_back),
                                         (2, rescale), (2, weigh), (2, total)])

        @block.scalar
        def _(act):
            def exps(n, k, r):
                need(act, s_diff, n)
                need(act, s_col, n)
                room(act, s_den, n, 2)
                act.activation(prob[k % 2][:, BE:BE + 1], back_by[k % 2][:, :], ACT.Exp)
                act.activation(prob[k % 2][:, 0:BE], pC[k % 2][:, :], ACT.Exp).then_inc(s_prob, 1)

            def store(n, k, r):
                need(act, s_ret, n)
                stored(act, s_out, k, r)
                act.activation(back[k][:, :, 0:D], pB[:, :].rearrange("p (t f) -> p t f", t=BT), ACT.Copy)
                act.activation(back[k][:, :, D:W3], pD[:, 0:BE:HEAD].rearrange("p (t h) -> p t h", t=BT), ACT.Copy).then_inc(s_back, 1)
                need(act, s_back, n)
                act.dma_start(run[:, bass.ds(n * BT, BT), :], back[k][:, :, :]).then_inc(s_out[k], 16)
            pipeline(act, BATCHES, SLOTS, [(0, exps), (2, store)])
            all_stored(act, s_out)


def nodes(nc, g, layer, out):
    w, row, wide = g["w"], g["row"], g["wide"]
    width = W3 if layer == 3 else D
    table = g["run3"] if layer == 3 else g["run"]
    nxt = [("W1s", None, g["tab"]), ("M1s", None, g["tab_h"]), ("Wkv", "bkv", g["tab_kv"]), None][layer]
    seed_w = [("W1d", "b1"), ("M1d", "m1"), ("Wq", "bq"), None][layer]
    last_layer = layer == 3
    tw = w[nxt[0]].shape[1] if nxt else 0
    sw = w[seed_w[0]].shape[1] if nxt else 0
    with Phase(nc, f"N{layer}") as ph:
        slot = lambda name, shape, dtype=F32: [ph.sb(f"{name}{k}", shape, dtype) for k in range(NSLOTS)]
        idx = slot("idx", [P, BT], I32)
        got = ph.sb("got", [P, NT, width])
        agg, y, xn = (slot(n, [P, BT, D]) for n in ("agg", "y", "xn"))
        xT = slot("xT", [P, BE]) if layer != 2 else None
        aT = slot("aT", [P, BE]) if layer in (0, 1) else None
        uT = slot("uT", [P, BE]) if layer == 1 else None
        if not last_layer:
            idf, xn_T, seed, tab = slot("idf", [P, BT], I32), slot("xnT", [P, BE]), slot("seed", [P, BT, D]), slot("tab", [P, BT, W2 if layer == 1 else tw])
        sq = ph.sb("sq", [P, BT, D])
        minus, var, inv, std = (ph.sb(n, [P, BT]) for n in ("minus", "var", "inv", "std"))
        if layer >= 2:
            part = ph.sb("part", [P, BT, D])
        if last_layer:
            part2 = ph.sb("part2", [P, BT, D])
            dot, beta = ph.sb("dot", [P, BT]), ph.sb("beta", [P, BT])
            inv_den = ph.sb("inv_den", [P, BT, HEADS])
            w_out, w_skip = ph.sb("w_out", [P, D]), ph.sb("w_skip", [P, D])
        pA, pU, pY, pX, pQ = (ph.ps(n) for n in ("pA", "pU", "pY", "pX", "pQ"))
        pT = [ph.ps(f"pT{j}") for j in range(2)]
        (s_ix, s_if, s_go, s_gz, s_agg, s_turn, s_aT, s_xs, s_u, s_uT, s_y, s_dot, s_beta, s_sum, s_bias, s_var, s_std, s_inv, s_xn,
         s_turnx, s_xnT, s_keep, s_tab, s_tabc, s_seedc, s_prep, s_norm, s_att, s_mix, s_zero, s_pre, s_ago) = (ph.sem(n) for n in (
            "ix", "if", "go", "gz", "agg", "turn", "aT", "xs", "u", "uT", "y", "dot", "beta", "sum", "bias", "var", "std", "inv", "xn",
            "turnx", "xnT", "keep", "tab", "tabc", "seedc", "prep", "norm", "att", "mix", "zero", "pre", "ago"))
        s_got, s_scat, s_tout = (ph.slot_sems(n, NSLOTS) for n in ("got", "scat", "tout"))
        block = ph.block()
        over = lambda a, n, m=D: a.unsqueeze(2).to_broadcast([P, n, m])
        tiled = lambda a: a.unsqueeze(1).to_broadcast([P, BT, D])
        now = lambda a, n: a[:, bass.ds(n * BT, BT)]
        now3 = lambda a, n: a[:, bass.ds(n * BT, BT), :]
        per_slot = lambda k: len(range(k, NB, NSLOTS))

        @block.gpsimd
        def _(gp):
            if not last_layer and sw < D:
                for k in range(NSLOTS):
                    gp.memset(seed[k][:, :, :], 0.0).then_inc(s_zero, 1)

            def fetch(n, k, r):
                stored(gp, s_got, k, r, BT)
                gp.tensor_copy(idx[k][:, :], now(g["last"], n)).then_inc(s_ix, 1)
                need(gp, s_ix, n)
                gp.sem_inc(s_go, 1)
                for t in range(BT):
                    gp.indirect_dma_start(out=got[:, n * BT + t, :], out_offset=None, in_=table,
                                          in_offset=bass.IndirectOffsetOnAxis(ap=idx[k][:, t:t + 1], axis=0)).then_inc(s_got[k], 16)

            def scatter(n, k, r):
                stored(gp, s_scat, k, r, BT)
                gp.tensor_copy(idf[k][:, :], now(g["first"], n)).then_inc(s_if, 1)
                need(gp, s_if, n)
                need(gp, s_seedc, n)
                gp.sem_inc(s_gz, 1)
                for t in range(BT):
                    gp.indirect_dma_start(out=g["seed"], out_offset=bass.IndirectOffsetOnAxis(ap=idf[k][:, t:t + 1], axis=0),
                                          in_=seed[k][:, t, :], in_offset=None, bounds_check=EP - 1, oob_is_err=False).then_inc(s_scat[k], 16)
            for n in range(NB):
                fetch(n, n % NSLOTS, n // NSLOTS)
            if not last_layer:
                pipeline(gp, NB, NSLOTS, [(0, scatter)])
                for k in range(NSLOTS):
                    gp.wait_ge(s_scat[k], 16 * BT * per_slot(k))

        @block.sync
        def _(sp):
            if last_layer:
                full, rest = N // NT, N % NT

                def store(n, k, r):
                    need(sp, s_xn, n)
                    sp.dma_start(now3(out[0:full * NT, :].rearrange("(p t) f -> p t f", t=NT), n), xn[k][0:full, :, :]).then_inc(s_tout[k], 16)
                pipeline(sp, NB, NSLOTS, [(0, store)])
                for k in range(NSLOTS):
                    sp.wait_ge(s_tout[k], 16 * per_slot(k))
                need(sp, s_keep, NB - 1)
                sp.dma_start(out[full * NT:N, :].unsqueeze(0), g["x"][full:full + 1, 0:rest, :]).then_inc(s_tout[0], 16)
                sp.wait_ge(s_tout[0], 16 * (per_slot(0) + 1))
            else:
                to = nxt[2].rearrange("(p t) f -> p t f", p=P)

                def store(n, k, r):
                    need(sp, s_tabc, n)
                    sp.dma_start(now3(to, n), tab[k][:, :, :]).then_inc(s_tout[k], 16)
                pipeline(sp, NB, NSLOTS, [(0, store)])
                for k in range(NSLOTS):
                    sp.wait_ge(s_tout[k], 16 * per_slot(k))

        @block.tensor
        def _(pe):
            def product(to, left, w_name, bias):
                m = pe.matmul(to, left, w[w_name][:, :], start=True, stop=bias is None)
                if bias is not None:
                    m = pe.matmul(to, g["ones"][0:1, :], row[bias][0:1, 0:w[w_name].shape[1]], start=False, stop=True)
                return m

            def turn_agg(n, k, r):
                need(pe, s_agg, n)
                room(pe, s_aT, n, 1)
                for t in range(BT):
                    m = pe.transpose(pA[:, cols(t)], agg[k][:, t, :], g["ident"][:, :])
                m.then_inc(s_turn, 1)

            def hidden(n, k, r):
                need(pe, s_xs, n)
                need(pe, s_aT, n)
                room(pe, s_uT, n, 1)
                pe.matmul(pU[:, :], w["U1x"][:, :], xT[k][:, :], start=True, stop=False)
                pe.matmul(pU[:, :], w["U1a"][:, :], aT[k][:, :], start=False, stop=True).then_inc(s_u, 1)

            def result(n, k, r):
                room(pe, s_dot if last_layer else s_sum, n, 1)
                if layer == 0:
                    need(pe, s_xs, n)
                    need(pe, s_aT, n)
                    for t in range(BT):
                        pe.matmul(pY[:, cols(t)], xT[k][:, cols(t)], w["W0x"][:, :], start=True, stop=False)
                        m = pe.matmul(pY[:, cols(t)], aT[k][:, cols(t)], w["W0a"][:, :], start=False, stop=True)
                elif layer == 1:
                    need(pe, s_uT, n)
                    for t in range(BT):
                        m = product(pY[:, cols(t)], uT[k][:, cols(t)], "U2", "c2")
                else:
                    need(pe, s_xs, n)
                    for t in range(BT):
                        m = product(pY[:, cols(t)], xT[k][:, cols(t)], "Wskip", "bskip")
                m.then_inc(s_y, 1)

            def turn_new(n, k, r):
                need(pe, s_xn, n)
                room(pe, s_xnT, n, 1)
                for t in range(BT):
                    m = pe.transpose(pX[:, cols(t)], xn[k][:, t, :], g["ident"][:, :])
                m.then_inc(s_turnx, 1)

            def tables(n, k, r):
                need(pe, s_xnT, n)
                room(pe, s_tabc, n, 1)
                room(pe, s_seedc, n, 1)
                for t in range(BT):
                    bank, at = (pT[t * tw // BE], t * tw % BE)
                    product(bank[:, at:at + tw], xn_T[k][:, cols(t)], nxt[0], nxt[1])
                    if layer == 1:
                        product(pT[1][:, cols(t)], xn_T[k][:, cols(t)], "conv", None)
                    m = product(pQ[:, t * D:t * D + sw], xn_T[k][:, cols(t)], *seed_w)
                m.then_inc(s_tab, 1)
            stages = {0: [(0, turn_agg), (2, turn_new), (2, tables), (0, result)],
                      1: [(0, turn_agg), (2, turn_new), (0, hidden), (2, tables), (0, result)],
                      2: [(2, turn_new), (2, tables)],
                      3: [(0, result)]}[layer]
            pipeline(pe, NB, NSLOTS, stages)

        @block.vector
        def _(v):
            prep_link, norm_link, att_link, mix_link = (Chain(v, s, per) for s, per in (
                (s_prep, {1: 1, 2: 3}.get(layer, 0)), (s_norm, 5), (s_att, 8), (s_mix, 2)))
            pre_link = Chain(v, s_pre)
            if layer == 2:
                pre_link(v.tensor_tensor(g["mean"][:, :], g["dinv"][:, :], g["has"][:, :], ALU.mult))
            if last_layer:
                wb = lambda j: wide["beta"][:, j * D:(j + 1) * D]
                pre_link(v.tensor_tensor(w_out[:, :], wb(0), wb(2), ALU.add))
                pre_link(v.tensor_tensor(w_skip[:, :], wb(1), wb(2), ALU.subtract))

            def prep(n, k, r):
                landed(v, s_got, k, r, BT)
                prep_link.item(n)
                mine = now3(got, n)
                if layer == 0:
                    room(v, s_turn, n, NSLOTS)
                    v.tensor_tensor(agg[k][:, :, :], mine, over(now(g["mean"], n), BT), ALU.mult).then_inc(s_agg, 1)
                elif layer == 1:
                    room(v, s_turn, n, NSLOTS)
                    prep_link(v.tensor_tensor(agg[k][:, :, :], mine, tiled(wide["b2"][:, :]), ALU.add))
                    v.tensor_tensor(agg[k][:, :, :], agg[k][:, :, :], over(now(g["has"], n), BT), ALU.mult).then_inc(s_agg, 1)
                else:
                    room(v, s_sum, n, NSLOTS)
                    dinv = over(now(g["dinv"], n), BT)
                    prep_link(v.tensor_tensor(agg[k][:, :, :], mine, over(now(g["mean"], n), BT), ALU.mult))
                    prep_link(v.tensor_tensor(part[:, :, :], now3(g["xt"], n), dinv, ALU.mult))
                    prep_link(v.tensor_tensor(part[:, :, :], part[:, :, :], dinv, ALU.mult))
                    v.tensor_tensor(agg[k][:, :, :], agg[k][:, :, :], part[:, :, :], ALU.add).then_inc(s_agg, 1)

            def attend(n, k, r):
                landed(v, s_got, k, r, BT)
                att_link.item(n)
                mine = now3(got, n)
                att_link(v.tensor_scalar(inv_den[:, :, :], mine[:, :, D:W3], 1e-16, None, ALU.max))
                att_link(v.reciprocal(inv_den[:, :, :], inv_den[:, :, :]))
                att_link(v.tensor_tensor(inv_den[:, :, :], inv_den[:, :, :], over(now(g["has"], n), BT, HEADS), ALU.mult))
                room(v, s_sum, n, NSLOTS)
                for t in range(BT):
                    a = v.tensor_tensor(agg[k][:, t, :].rearrange("p (h c) -> p h c", h=HEADS),
                                        got[:, bass.ds(n * BT + t, 1), 0:D].rearrange("p a (h c) -> p (a h) c", h=HEADS),
                                        over(inv_den[:, t, :], HEADS, HEAD), ALU.mult)
                att_link(a)
                need(v, s_y, n)
                skip = pY[:, :].rearrange("p (t f) -> p t f", t=BT)
                att_link(v.tensor_tensor(part[:, :, :], agg[k][:, :, :], skip, ALU.subtract))
                att_link(v.tensor_tensor(part2[:, :, :], skip, tiled(w_skip[:, :]), ALU.mult))
                att_link(v.tensor_tensor(sq[:, :, :], agg[k][:, :, :], tiled(w_out[:, :]), ALU.mult))
                att_link(v.tensor_tensor(part2[:, :, :], part2[:, :, :], sq[:, :, :], ALU.add))
                v.tensor_reduce(dot[:, :], part2[:, :, :], AX, ALU.add).then_inc(s_dot, 1)

            def mix(n, k, r):
                need(v, s_beta, n)
                mix_link.item(n)
                mix_link(v.tensor_tensor(part[:, :, :], part[:, :, :], over(beta[:, :], BT), ALU.mult))
                mix_link(v.tensor_tensor(agg[k][:, :, :], agg[k][:, :, :], part[:, :, :], ALU.subtract))

            def centre(n, k, r):
                room(v, s_xn, n, NSLOTS)
                if layer < 2:
                    need(v, s_y, n)
                    other = pY[:, :].rearrange("p (t f) -> p t f", t=BT)
                else:
                    other = agg[k][:, :, :]
                    if layer == 2:
                        need(v, s_agg, n)
                v.tensor_tensor(y[k][:, :, :], other, now3(g["x"], n), ALU.add).then_inc(s_sum, 1)
                need(v, s_sum, n)
                if layer == 2:
                    v.tensor_tensor(y[k][:, :, :], y[k][:, :, :], tiled(wide["conv_b"][:, :]), ALU.add).then_inc(s_bias, 1)
                    need(v, s_bias, n)
                norm_link.item(n)
                norm_link(v.tensor_reduce(minus[:, :], y[k][:, :, :], AX, ALU.add))
                norm_link(v.tensor_scalar(minus[:, :], minus[:, :], -1.0 / D, None, ALU.mult))
                norm_link(v.tensor_tensor(y[k][:, :, :], y[k][:, :, :], over(minus[:, :], BT), ALU.add))
                norm_link(v.tensor_tensor(sq[:, :, :], y[k][:, :, :], y[k][:, :, :], ALU.mult))
                norm_link(v.tensor_reduce(var[:, :], sq[:, :, :], AX, ALU.add))
                v.tensor_scalar(var[:, :], var[:, :], 1.0 / D, EPS, ALU.mult, ALU.add).then_inc(s_var, 1)

            def scale(n, k, r):
                need(v, s_std, n)
                v.reciprocal(inv[:, :], std[:, :]).then_inc(s_inv, 1)
                need(v, s_inv, n)
                if last_layer:
                    stored(v, s_tout, k, r)
                else:
                    room(v, s_turnx, n, NSLOTS)
                room(v, s_keep, n, NSLOTS)
                v.tensor_tensor(xn[k][:, :, :], y[k][:, :, :], over(inv[:, :], BT), ALU.mult).then_inc(s_xn, 1)
            pipeline(v, NB, NSLOTS, [(1, attend), (1, mix), (1, centre), (1, scale)] if last_layer else [(1, centre), (0, prep), (1, scale)])

        @block.scalar
        def _(act):
            def load_xT(n, k, r):
                room(act, s_u if layer == 1 else s_y, n, NSLOTS)
                act.activation(xT[k][:, :], g["xT"][:, bass.ds(n * BE, BE)], ACT.Copy).then_inc(s_xs, 1)

            def copy_agg(n, k, r):
                need(act, s_turn, n)
                room(act, s_u if layer == 1 else s_y, n, NSLOTS)
                act.activation(aT[k][:, :], pA[:, :], ACT.Copy).then_inc(s_aT, 1)

            def relu(n, k, r):
                need(act, s_u, n)
                room(act, s_y, n, NSLOTS)
                act.activation(uT[k][:, :], pU[:, :], ACT.Relu, bias=g["c1"][:, 0:1]).then_inc(s_uT, 1)

            def gate(n, k, r):
                need(act, s_dot, n)
                act.activation(beta[:, :], dot[:, :], ACT.Sigmoid).then_inc(s_beta, 1)

            def root(n, k, r):
                need(act, s_var, n)
                act.activation(std[:, :], var[:, :], ACT.Sqrt).then_inc(s_std, 1)

            def keep(n, k, r):
                need(act, s_xn, n)
                act.sem_inc(s_ago, 1)
                act.activation(now3(g["x"], n), xn[k][:, :, :], ACT.Copy).then_inc(s_keep, 1)

            def copy_new(n, k, r):
                need(act, s_turnx, n)
                room(act, s_tab, n, NSLOTS)
                act.activation(xn_T[k][:, :], pX[:, :], ACT.Copy).then_inc(s_xnT, 1)

            def keep_T(n, k, r):
                need(act, s_xnT, n)
                act.sem_inc(s_ago, 1)
                act.activation(g["xT"][:, bass.ds(n * BE, BE)], xn_T[k][:, :], ACT.Copy)

            def copy_tables(n, k, r):
                need(act, s_tab, n)
                stored(act, s_tout, k, r)
                half = BE // tw if tw > D else BT
                for j in range(BT // half):
                    a = act.activation(tab[k][:, j * half:(j + 1) * half, 0:tw], pT[j][:, 0:half * tw].rearrange("p (t f) -> p t f", f=tw), ACT.Copy)
                if layer == 1:
                    act.activation(tab[k][:, :, HID:W2], pT[1][:, :].rearrange("p (t f) -> p t f", t=BT), ACT.Copy)
                    a = act.activation(now3(g["xt"], n), pT[1][:, :].rearrange("p (t f) -> p t f", t=BT), ACT.Copy)
                a.then_inc(s_tabc, 1)
                stored(act, s_scat, k, r, BT)
                act.activation(seed[k][:, :, 0:sw], pQ[:, :].rearrange("p (t f) -> p t f", t=BT)[:, :, 0:sw], ACT.Copy).then_inc(s_seedc, 1)
            if not last_layer and sw < D:
                act.wait_ge(s_zero, NSLOTS)
            table_stages = [(2, copy_new), (2, copy_tables), (2, keep_T)]
            pipeline(act, NB, NSLOTS, {
                0: [(0, load_xT), (1, root), (0, copy_agg), (1, keep)] + table_stages,
                1: [(0, load_xT), (1, root), (0, copy_agg), (2, copy_new), (0, relu), (1, keep)] + table_stages[1:],
                2: [(1, root), (1, keep)] + table_stages,
                3: [(0, load_xT), (1, gate), (1, root), (1, keep)]}[layer])


_WEIGHTS = ["L0_gnn_weight", "L1_gnn_W1", "L1_gnn_b1", "L1_gnn_W2", "L1_gnn_b2", "L1_gnn_U1", "L1_gnn_c1", "L1_gnn_U2", "L1_gnn_c2",
            "L2_gnn_mlp_w1", "L2_gnn_mlp_b1", "L2_gnn_mlp_w2", "L2_gnn_mlp_b2", "L2_gnn_conv_w", "L2_gnn_conv_b",
            "L3_gnn_Wq", "L3_gnn_bq", "L3_gnn_Wk", "L3_gnn_bk", "L3_gnn_Wv", "L3_gnn_bv", "L3_gnn_Wskip", "L3_gnn_bskip", "L3_gnn_Wbeta"]


def kernel(**inputs):
    import numpy as _np
    import concourse.bacc as _bacc
    from concourse import mybir as _mybir
    from concourse.bass_utils import run_bass_kernel_spmd as _run

    nc = _bacc.Bacc("TRN2", target_bir_lowering=False, num_devices=1)
    x = _np.zeros((NP, D), _np.float32)
    x[:N] = inputs["x"]
    src = _np.zeros((EP + SLOTS * BE,), _np.int32)
    src[:E] = inputs["src"]
    dst = _np.full((EP + 2,), N, _np.int32)
    dst[0] = -1
    dst[1:E + 1] = inputs["dst"]
    dst[EP + 1] = N + 1
    weight = _np.zeros((EP,), _np.float32)
    weight[:E] = inputs["edge_weight"]
    arrays = {
        "x": x,
        "src": _np.ascontiguousarray(src.reshape(-1, P).T),
        "src_row": src[:EP],
        "dst": dst,
        "dst_rows": _np.ascontiguousarray(dst[1:EP + 1].reshape(TILES, P)),
        "heads": _np.ascontiguousarray(dst[1:EP + 1].reshape(TILES, P)[:, 0]),
        "weight": _np.ascontiguousarray(weight.reshape(TILES, P).T),
    }
    for name in _WEIGHTS:
        arrays[name] = _np.ascontiguousarray(inputs[name])
    d = {n: nc.dram_tensor("in_" + n, a.shape, _mybir.dt.from_np(a.dtype), kind="ExternalInput").ap() for n, a in arrays.items()}
    out = nc.dram_tensor("out_0", (N, D), F32, kind="ExternalOutput").ap()
    build(nc, d, out)
    r = _run(nc, [{"in_" + n: a for n, a in arrays.items()}], core_ids=[0])
    return r.results[0]["out_0"]
```

```python
from contextlib import ExitStack

import concourse.bass as bass
from concourse import mybir

F32 = mybir.dt.float32
I32 = mybir.dt.int32
BF16 = mybir.dt.bfloat16
ALU = mybir.AluOpType
ACT = mybir.ActivationFunctionType
AX = mybir.AxisListType.X

P = 128
N, E, D = 6250, 106250, 128
HID = 64
HEADS, HEAD = 4, 32
BT = 4
BE = BT * P
SLOTS = 4
TILES = -(-E // (P * BT * SLOTS)) * BT * SLOTS
BATCHES = TILES // BT
EP = TILES * P
NT = -(-N // (P * BT)) * BT
NP = NT * P
NB = NT // BT
NSLOTS = 3
FAR = -3.0e38
EPS = 1e-5
W3 = D + HEADS
W2 = HID + D
LO = 7
HIGH = NP // P


def need(eng, sem, n):
    eng.wait_ge(sem, n + 1)


def room(eng, sem, n, depth):
    if isinstance(n, int) and n < depth:
        return
    eng.wait_ge(sem, n - depth + 1)


def landed(eng, sems, k, r, dmas=1):
    eng.wait_ge(sems[k], 16 * dmas * (r + 1))


def stored(eng, sems, k, r, dmas=1):
    if isinstance(r, int) and r < 1:
        return
    eng.wait_ge(sems[k], 16 * dmas * r)


def pipeline(eng, count, slots, stages):
    lag_max = max(lag for lag, _ in stages)
    head = -(-(lag_max + slots) // slots)
    rounds = count // slots

    def step(r0, k0, peeled):
        for lag, f in stages:
            q = k0 - lag
            k, r = q % slots, r0 + q // slots
            n = r * slots + k
            if peeled and not 0 <= n < count:
                continue
            f(n, k, r)

    for s in range(min(head, rounds) * slots):
        step(s // slots, s % slots, True)
    if rounds > head:
        with eng.Fori(head, rounds) as i:
            for k0 in range(slots):
                step(i, k0, False)
    for s in range(max(rounds, 0) * slots, count + lag_max):
        step(s // slots, s % slots, True)


class Phase:

    def __init__(self, nc, name):
        self.nc, self.name, self.sems, self.ctx = nc, name, [], ExitStack()

    def __enter__(self):
        return self

    def sb(self, name, shape, dtype=F32):
        return self.ctx.enter_context(self.nc.sbuf_tensor(f"{self.name}_{name}", shape, dtype))

    def ps(self, name, shape=(P, BE), dtype=F32):
        return self.ctx.enter_context(self.nc.psum_tensor(f"{self.name}_{name}", list(shape), dtype))

    def sem(self, name):
        s = self.nc.alloc_semaphore(name=f"{self.name}_{name}")
        self.sems.append(s)
        return s

    def slot_sems(self, name, count):
        return [self.sem(f"{name}{k}") for k in range(count)]

    def block(self):
        return self.ctx.enter_context(self.nc.Block())

    def __exit__(self, *args):
        self.ctx.close()
        self.nc.clear_and_free_semaphores(self.sems)
        self.nc.all_engine_barrier()


class Chain:

    def __init__(self, eng, sem, per=0):
        self.eng, self.sem, self.per, self.j, self.n = eng, sem, per, 0, 0

    def item(self, n):
        assert self.j in (0, self.per), (self.j, self.per)
        self.n, self.j = n, 0

    def __call__(self, ins):
        self.j += 1
        ins.then_inc(self.sem, 1)
        self.eng.wait_ge(self.sem, self.n * self.per + self.j)


def rows(tile):
    return tile.rearrange("p a b -> p (a b)")


def cols(t):
    return slice(t * P, (t + 1) * P)


def build(nc, d, out):
    with ExitStack() as ctx:
        def sb(name, shape, dtype=F32):
            return ctx.enter_context(nc.sbuf_tensor(name, shape, dtype))

        def dram(name, shape, dtype=F32):
            return nc.dram_tensor(name, shape, dtype, kind="Internal").ap()

        g = {}
        g["ident"] = sb("ident", [P, P])
        g["ones"] = sb("ones", [1, P])
        g["src"] = sb("src", [P, TILES + SLOTS * BT], I32)
        g["x"] = sb("x", [P, NT, D])
        g["xT"] = sb("xT", [P, NT * P])
        g["last"] = sb("last", [P, NT], I32)
        g["first"] = sb("first", [P, NT], I32)
        g["last_e"] = sb("last_e", [P, NT], I32)
        g["has"] = sb("has", [P, NT])
        g["mean"] = sb("mean", [P, NT])
        g["same_c"] = sb("same_c", [P, TILES], BF16)
        weights = {}
        for name in ("W0x", "W0a", "W1s", "W1d", "W2", "U1x", "U1a", "U2", "conv", "Wq", "Wskip"):
            weights[name] = sb("w_" + name, [P, D])
        weights["M1s"] = sb("w_M1s", [P, HID])
        weights["M1d"] = sb("w_M1d", [P, HID])
        weights["M2"] = sb("w_M2", [HID, 1])
        weights["Wkv"] = sb("w_Wkv", [P, 2 * D])
        bias_w = (("b1", D), ("c2", D), ("m1", HID), ("bq", D), ("bkv", 2 * D), ("bskip", D))
        bias_all = sum(width for _, width in bias_w)
        g["bias"] = sb("bias", [3, bias_all], BF16)
        g["ones3"] = sb("ones3", [3, P], BF16)
        g["bias_at"] = {n: sum(width for _, width in bias_w[:j]) for j, (n, _) in enumerate(bias_w)}
        wide = {n: sb("b_" + n, [P, w]) for n, w in (("W1w", D), ("b2", D), ("conv_b", D), ("beta", 3 * D), ("m2", 1))}
        g["c1"] = sb("c1", [P, 1])
        g["w"], g["wide"] = weights, wide
        g["same"] = dram("same", [EP], BF16)
        g["fresh"] = dram("fresh", [EP], BF16)
        g["ends"] = dram("ends", [EP], BF16)
        g["run"] = dram("run", [EP, D])
        g["run3"] = dram("run3", [EP, W3])
        g["seed"] = dram("seed", [EP, D])
        g["tab"] = dram("tab", [NP, D])
        g["tab_h"] = dram("tab_h", [NP, W2])
        g["low"] = dram("low", [EP], BF16)
        g["sent"] = dram("sent", [EP, D])
        g["dinv_row"] = dram("dinv_row", [NP])
        g["tab_kv"] = dram("tab_kv", [NP, 2 * D])
        g["off"] = dram("off", [NP + 1, 1], I32)
        g["ew"] = dram("ew", [EP, 1])
        g["xt"] = sb("xt", [P, NT, D])
        g["dinv"] = sb("dinv", [P, NT])
        g["dinv_low"] = sb("dinv_low", [P, 3, HIGH], BF16)

        setup(nc, d, g)
        edges_sum(nc, d, g)
        nodes(nc, g, 0, out)
        edges_max(nc, d, g)
        nodes(nc, g, 1, out)
        ew = sb("ew_sb", [P, TILES])
        edges_gate(nc, g, ew)
        degrees(nc, g, ew)
        edges_conv(nc, g, ew)
        nodes(nc, g, 2, out)
        edges_attention(nc, g)
        nodes(nc, g, 3, out)


def setup(nc, d, g):
    w, wide, at = g["w"], g["wide"], g["bias_at"]
    loads = [
        (g["src"][:, :], d["src"]), (g["x"][:, :, :], d["x"].rearrange("(p t) f -> p t f", p=P)),
        (w["W0x"][:, :], d["L0_gnn_weight"][0:D, :]), (w["W0a"][:, :], d["L0_gnn_weight"][D:2 * D, :]),
        (w["W1s"][:, :], d["L1_gnn_W1"][0:D, :]), (w["W1d"][:, :], d["L1_gnn_W1"][D:2 * D, :]),
        (wide["W1w"][:, :], d["L1_gnn_W1"][2 * D:2 * D + 1, :].to_broadcast([P, D])),
        (w["W2"][:, :], d["L1_gnn_W2"]),
        (w["U1x"][:, :], d["L1_gnn_U1"][0:D, :]), (w["U1a"][:, :], d["L1_gnn_U1"][D:2 * D, :]),
        (w["U2"][:, :], d["L1_gnn_U2"]),
        (w["M1s"][:, :], d["L2_gnn_mlp_w1"][0:D, :]), (w["M1d"][:, :], d["L2_gnn_mlp_w1"][D:2 * D, :]),
        (w["M2"][:, :], d["L2_gnn_mlp_w2"]), (w["conv"][:, :], d["L2_gnn_conv_w"]),
        (w["Wkv"][:, 0:D], d["L3_gnn_Wk"]), (w["Wkv"][:, D:2 * D], d["L3_gnn_Wv"]),
        (w["Wq"][:, :], d["L3_gnn_Wq"]), (w["Wskip"][:, :], d["L3_gnn_Wskip"]),
        (g["c1"][:, :], d["L1_gnn_c1"].rearrange("(p a) -> p a", a=1)),
    ]
    line = lambda a: a.rearrange("(a n) -> a n", a=1)
    biases = [("b1", "L1_gnn_b1"), ("c2", "L1_gnn_c2"), ("m1", "L2_gnn_mlp_b1"), ("bq", "L3_gnn_bq"), ("bkv", "L3_gnn_bk"),
              ("bkv", "L3_gnn_bv"), ("bskip", "L3_gnn_bskip")]
    loads += [(wide["b2"][:, :], line(d["L1_gnn_b2"]).to_broadcast([P, D])),
              (wide["conv_b"][:, :], line(d["L2_gnn_conv_b"]).to_broadcast([P, D])),
              (wide["m2"][:, :], line(d["L2_gnn_mlp_b2"]).to_broadcast([P, 1]))]
    loads += [(wide["beta"][:, j * D:(j + 1) * D],
               d["L3_gnn_Wbeta"][j * D:(j + 1) * D, :].rearrange("n a -> a n").to_broadcast([P, D])) for j in range(3)]
    chunk = lambda a: a.rearrange("(p i) -> p i", p=P)
    with Phase(nc, "set") as ph:
        dst = [ph.sb(f"dst{j}", [P, TILES], I32) for j in range(3)]
        far = [ph.sb(f"far{j}", [P, TILES], BF16) for j in range(2)]
        bias_all = g["bias"].shape[1]
        bias = ph.sb("bias", [1, bias_all])
        part = [ph.sb(f"part{j}", [1, bias_all], BF16) for j in range(3)]
        src, low = ph.sb("src", [P, TILES], I32), ph.sb("low", [P, TILES], BF16)
        xs = [ph.sb(f"xs{k}", [P, BT, D]) for k in range(NSLOTS)]
        pT = [ph.ps(f"pT{k}") for k in range(NSLOTS)]
        s_dst, s_w, s_id, s_mask, s_tp, s_tc, s_link, s_bias, s_part = (ph.sem(n) for n in ("dst", "w", "id", "mask", "tp", "tc", "link", "bias", "part"))
        s_xs = ph.slot_sems("xs", NSLOTS)
        block = ph.block()

        @block.sync
        def _(sp):
            for j in range(3):
                sp.dma_start(dst[j][:, :], chunk(d["dst"][j:j + EP])).then_inc(s_dst, 16)
            sp.dma_start(src[:, :], chunk(d["src_row"])).then_inc(s_dst, 16)

            def load_x(n, k, r):
                room(sp, s_tp, n, NSLOTS)
                sp.dma_start(xs[k][:, :, :], d["x"].rearrange("(p t) f -> p t f", p=P)[:, bass.ds(n * BT, BT), :]).then_inc(s_xs[k], 16)
            pipeline(sp, NB, NSLOTS, [(0, load_x)])
            sp.wait_ge(s_mask, 1)
            sp.dma_start(chunk(g["same"]), g["same_c"][:, :]).then_inc(s_w, 16)
            sp.wait_ge(s_mask, 2)
            sp.dma_start(chunk(g["fresh"]), far[0][:, :]).then_inc(s_w, 16)
            sp.wait_ge(s_mask, 3)
            sp.dma_start(chunk(g["ends"]), far[1][:, :]).then_inc(s_w, 16)
            sp.wait_ge(s_mask, 4)
            sp.dma_start(chunk(g["low"]), low[:, :]).then_inc(s_w, 16)
            for j in range(3):
                sp.wait_ge(s_part, j + 1)
                sp.dma_start(g["bias"][j:j + 1, :], part[j][:, :]).then_inc(s_w, 16)
            sp.wait_ge(s_w, 16 * (len(loads) + 7))

        @block.scalar
        def _(act):
            for j, (name, source) in enumerate(biases):
                first = at[name] + (D if source == "L3_gnn_bv" else 0)
                act.dma_start(bias[:, first:first + d[source].shape[0]], line(d[source])).then_inc(s_bias, 16)
            for to, a in loads:
                act.dma_start(to, a).then_inc(s_w, 16)

            def copy(n, k, r):
                need(act, s_tp, n)
                act.activation(g["xT"][:, bass.ds(n * BE, BE)], pT[k][:, :], ACT.Copy).then_inc(s_tc, 1)
            pipeline(act, NB, NSLOTS, [(0, copy)])

        @block.tensor
        def _(pe):
            pe.wait_ge(s_id, 2)

            def turn(n, k, r):
                landed(pe, s_xs, k, r)
                room(pe, s_tc, n, NSLOTS)
                for t in range(BT):
                    m = pe.transpose(pT[k][:, cols(t)], xs[k][:, t, :], g["ident"][:, :])
                m.then_inc(s_tp, 1)
            pipeline(pe, NB, NSLOTS, [(0, turn)])

        @block.gpsimd
        def _(gp):
            gp.memset(g["ident"][:, :], 0.0).then_inc(s_id, 1)
            gp.wait_ge(s_id, 1)
            gp.affine_select(out=g["ident"][:, :], in_=g["ident"][:, :], compare_op=ALU.not_equal, fill=1.0, base=0,
                             pattern=[[-1, P]], channel_multiplier=1).then_inc(s_id, 1)

        @block.vector
        def _(v):
            link = Chain(v, s_link)
            v.memset(g["ones"][:, :], 1.0)
            v.wait_ge(s_dst, 64)
            v.tensor_tensor(g["same_c"][:, :], dst[1][:, :], dst[0][:, :], ALU.is_equal).then_inc(s_mask, 1)
            link(v.tensor_tensor(far[0][:, :], dst[1][:, :], dst[0][:, :], ALU.not_equal))
            v.tensor_scalar(far[0][:, :], far[0][:, :], FAR, None, ALU.mult).then_inc(s_mask, 1)
            link(v.tensor_tensor(far[1][:, :], dst[1][:, :], dst[2][:, :], ALU.not_equal))
            v.tensor_scalar(far[1][:, :], far[1][:, :], FAR, None, ALU.mult).then_inc(s_mask, 1)
            link(v.tensor_scalar(src[:, :], src[:, :], P - 1, None, ALU.bitwise_and))
            v.tensor_copy(low[:, :], src[:, :]).then_inc(s_mask, 1)
            v.memset(g["ones3"][:, :], 1.0)
            v.wait_ge(s_bias, 16 * len(biases))
            for j in range(3):
                v.tensor_copy(part[j][:, :], bias[:, :]).then_inc(s_part, 1)
                v.wait_ge(s_part, j + 1)
                if j < 2:
                    link(v.tensor_tensor(bias[:, :], bias[:, :], part[j][:, :], ALU.subtract))


class NodeEdges:

    FILL = SLOTS * BT

    def __init__(self, ph, d, g):
        self.d, self.g = d, g
        self.dst, self.work = (ph.sb(n, [P, TILES], I32) for n in ("dst", "dwork"))
        self.low, self.high = (ph.sb(n, [P, TILES], BF16) for n in ("dlow", "dhigh"))
        self.row_i, self.row = ph.sb("row_i", [P, P], I32), ph.sb("row", [P, P], BF16)
        self.hot_low = [ph.sb(f"hotl{k}", [P, BT, P], BF16) for k in range(2)]
        self.hot_high = [ph.sb(f"hoth{k}", [P, BT, HIGH], BF16) for k in range(2)]
        self.nought, self.unit = ph.sb("nought", [P, P], BF16), ph.sb("unit", [P, P], BF16)
        self.count = ph.sb("count", [P, HIGH])
        self.upto, self.before = ph.sb("upto", [HIGH, P]), ph.sb("before", [HIGH, 1])
        self.tri = ph.sb("tri", [HIGH, HIGH])
        self.upto_i = ph.sb("upto_i", [HIGH, P], I32)
        self.a, self.b, self.c = (ph.sb(n, [P, NT]) for n in ("ta", "tb", "tc"))
        self.end_i, self.first_i, self.part_i = (ph.sb(n, [P, NT], I32) for n in ("endi", "firsti", "parti"))
        self.none = ph.sb("none", [1, 1], I32)
        self.zero = ph.sb("zeros", [P, self.FILL * D])
        self.p_count, self.p_turn = ph.ps("pH", (P, BE)), ph.ps("pG", (P, BE))
        (self.s_dst, self.s_iota, self.s_tri, self.s_zero, self.s_fill, self.s_made, self.s_hot, self.s_hist, self.s_off, self.s_back,
         self.s_tail, self.s_link, self.s_count, self.s_cum) = (ph.sem(n) for n in ("ndst", "iota", "tri", "zero", "fill", "made", "hot",
            "hist", "offd", "backd", "tail", "link", "count", "cum"))

    def pool_before(self, gp):
        gp.memset(self.zero[:, :], 0.0).then_inc(self.s_zero, 1)
        gp.iota(self.row_i[:, :], [[1, P]], base=0, channel_multiplier=0).then_inc(self.s_iota, 1)
        gp.memset(self.tri[:, :], 1.0).then_inc(self.s_tri, 1)
        gp.wait_ge(self.s_tri, 1)
        gp.affine_select(out=self.tri[:, :], in_=self.tri[:, :], compare_op=ALU.is_gt, fill=0.0, base=0,
                         pattern=[[1, HIGH]], channel_multiplier=-1).then_inc(self.s_tri, 1)

    def sync_before(self, sp):
        sp.dma_start(self.dst[:, :], self.d["dst_lane"]).then_inc(self.s_dst, 16)
        sp.wait_ge(self.s_zero, 1)

    def sync_stage(self, sp):
        seed = self.g["seed"].rearrange("(p t) f -> p t f", p=P)

        def fill(n, k, r):
            if k == 0:
                if not isinstance(r, int) or r > 0:
                    sp.wait_ge(self.s_fill, 16 * r)
                sp.dma_start(seed[:, bass.ds(r * self.FILL, self.FILL), :], self.zero[:, :].rearrange("p (t f) -> p t f", t=self.FILL)).then_inc(self.s_fill, 16)
        return fill

    def sync_after(self, sp):
        off = self.g["off"]
        by_node = lambda a: a.rearrange("(p t) a -> p (t a)", p=P)
        sp.wait_ge(self.s_off, 1)
        sp.dma_start(off[1:NP + 1, :].rearrange("(h l) a -> h (l a)", l=P), self.upto_i[:, :]).then_inc(self.s_back, 16)
        sp.dma_start(off[0:1, :], self.none[:, :]).then_inc(self.s_back, 16)
        sp.wait_ge(self.s_back, 32)
        sp.dma_start(self.end_i[:, :], by_node(off[1:NP + 1, :])).then_inc(self.s_back, 16)
        sp.dma_start(self.first_i[:, :], by_node(off[0:NP, :])).then_inc(self.s_back, 16)
        sp.wait_ge(self.s_fill, 16 * (TILES // self.FILL))

    def vector_before(self, v):
        v.memset(self.none[:, :], 0)
        v.memset(self.unit[:, :], 1.0).then_inc(self.s_made, 1)
        v.memset(self.nought[:, :], 0.0).then_inc(self.s_made, 1)
        v.wait_ge(self.s_iota, 1)
        v.tensor_copy(self.row[:, :], self.row_i[:, :]).then_inc(self.s_made, 1)
        v.wait_ge(self.s_dst, 16)
        v.tensor_scalar(self.work[:, :], self.dst[:, :], LO, None, ALU.arith_shift_right).then_inc(self.s_made, 1)
        v.tensor_scalar(self.dst[:, :], self.dst[:, :], P - 1, None, ALU.bitwise_and).then_inc(self.s_made, 1)
        v.wait_ge(self.s_made, 5)
        v.tensor_copy(self.high[:, :], self.work[:, :]).then_inc(self.s_made, 1)
        v.tensor_copy(self.low[:, :], self.dst[:, :]).then_inc(self.s_made, 1)
        v.wait_ge(self.s_made, 7)

    def vector_stage(self, v):
        def hot(n, k, r):
            room(v, self.s_hist, n, 2)
            v.tensor_tensor(self.hot_low[k % 2][:, :, :], self.row[:, :].unsqueeze(1).to_broadcast([P, BT, P]),
                            self.low[:, bass.ds(n * BT, BT)].unsqueeze(2).to_broadcast([P, BT, P]), ALU.is_equal)
            v.tensor_tensor(self.hot_high[k % 2][:, :, :], self.row[:, 0:HIGH].unsqueeze(1).to_broadcast([P, BT, HIGH]),
                            self.high[:, bass.ds(n * BT, BT)].unsqueeze(2).to_broadcast([P, BT, HIGH]), ALU.is_equal).then_inc(self.s_hot, 1)
        return hot

    def tensor_before(self, pe):
        pe.wait_ge(self.s_made, 2)
        pe.matmul(self.p_count[:, 0:HIGH], self.nought[:, :], self.nought[:, 0:HIGH], start=True, stop=False, skip_group_check=True)

    def tensor_stage(self, pe):
        def count(n, k, r):
            need(pe, self.s_hot, n)
            for t in range(BT):
                m = pe.matmul(self.p_count[:, 0:HIGH], self.hot_low[k % 2][:, t, :], self.hot_high[k % 2][:, t, :],
                              start=False, stop=False, skip_group_check=True)
            m.then_inc(self.s_hist, 1)
        return count

    def tensor_after(self, pe):
        pe.matmul(self.p_count[:, 0:HIGH], self.nought[:, :], self.nought[:, 0:HIGH], start=False, stop=True, skip_group_check=True).then_inc(self.s_tail, 1)
        pe.wait_ge(self.s_count, 1)
        pe.transpose(self.p_turn[0:HIGH, 0:P], self.count[:, :], self.g["ident"][:, :]).then_inc(self.s_tail, 1)
        pe.wait_ge(self.s_cum, 1)
        pe.wait_ge(self.s_tri, 2)
        pe.matmul(self.p_turn[0:HIGH, P:P + 1], self.tri[:, :], self.upto[:, P - 1:P], start=True, stop=True).then_inc(self.s_tail, 1)

    def vector_after(self, v):
        g, link = self.g, Chain(v, self.s_link)
        a, b, c = self.a, self.b, self.c
        v.wait_ge(self.s_tail, 1)
        v.tensor_copy(self.count[:, :], self.p_count[:, 0:HIGH]).then_inc(self.s_count, 1)
        v.wait_ge(self.s_tail, 2)
        v.tensor_tensor_scan(self.upto[:, :], self.unit[0:HIGH, :], self.p_turn[0:HIGH, 0:P], 0.0, ALU.mult, ALU.add).then_inc(self.s_cum, 1)
        v.wait_ge(self.s_tail, 3)
        link(v.tensor_copy(self.before[:, :], self.p_turn[0:HIGH, P:P + 1]))
        link(v.tensor_scalar(self.upto[:, :], self.upto[:, :], self.before[:, 0:1], None, ALU.add))
        v.tensor_copy(self.upto_i[:, :], self.upto[:, :]).then_inc(self.s_off, 1)

        def row_of(edges_i):
            link(v.tensor_scalar(self.part_i[:, :], edges_i, LO, None, ALU.arith_shift_right))
            link(v.tensor_copy(b[:, :], self.part_i[:, :]))
            link(v.tensor_scalar(self.part_i[:, :], edges_i, P - 1, None, ALU.bitwise_and))
            link(v.tensor_copy(a[:, :], self.part_i[:, :]))
            link(v.scalar_tensor_tensor(a[:, :], a[:, :], float(TILES), b[:, :], ALU.mult, ALU.add))

        v.wait_ge(self.s_back, 64)
        link(v.tensor_copy(a[:, :], self.end_i[:, :]))
        link(v.tensor_copy(b[:, :], self.first_i[:, :]))
        link(v.tensor_tensor(c[:, :], a[:, :], b[:, :], ALU.subtract))
        link(v.tensor_scalar(g["has"][:, :], c[:, :], 0.0, None, ALU.is_gt))
        link(v.tensor_scalar(c[:, :], c[:, :], 1.0, None, ALU.max))
        link(v.reciprocal(b[:, :], c[:, :]))
        link(v.tensor_tensor(g["mean"][:, :], b[:, :], g["has"][:, :], ALU.mult))
        link(v.tensor_scalar(a[:, :], a[:, :], -1.0, 0.0, ALU.add, ALU.max))
        link(v.tensor_copy(g["last_e"][:, :], a[:, :]))
        row_of(g["last_e"][:, :])
        link(v.tensor_copy(g["last"][:, :], a[:, :]))
        row_of(self.first_i[:, :])
        link(v.tensor_scalar(a[:, :], a[:, :], float(-EP), None, ALU.add))
        link(v.tensor_tensor(a[:, :], a[:, :], g["has"][:, :], ALU.mult))
        link(v.tensor_scalar(a[:, :], a[:, :], float(EP), None, ALU.add))
        link(v.tensor_copy(g["first"][:, :], a[:, :]))


def edge_buffers(ph, width):
    gath = [ph.sb(f"gath{k}", [P, BT, width]) for k in range(SLOTS)]
    idx = [ph.sb(f"idx{k}", [P, BT], I32) for k in range(SLOTS)]
    return gath, idx, ph.slot_sems("gath", SLOTS), ph.sem("idx"), ph.sem("go")


def gatherer(gp, table, gath, idx, s_gath, s_idx, s_go, s_free, s_copied=None):
    def gather(n, k, r):
        if s_copied:
            stored(gp, s_copied, k, r)
        need(gp, s_idx, n)
        room(gp, s_free, n, SLOTS)
        gp.sem_inc(s_go, 1)
        for t in range(BT):
            gp.indirect_dma_start(out=gath[k][:, t, :], out_offset=None, in_=table,
                                  in_offset=bass.IndirectOffsetOnAxis(ap=idx[k][:, t:t + 1], axis=0)).then_inc(s_gath[k], 16)
    pipeline(gp, BATCHES, SLOTS, [(0, gather)])


def indexer(v, g, idx, s_idx, s_gath):
    for k in range(SLOTS):
        v.tensor_copy(idx[k][:, :], g["src"][:, k * BT:(k + 1) * BT]).then_inc(s_idx, 1)

    def ahead(n, k, r):
        landed(v, s_gath, k, r, BT)
        v.tensor_copy(idx[k][:, :], g["src"][:, bass.ds((n + SLOTS) * BT, BT)]).then_inc(s_idx, 1)
    return ahead


def start_of(acc, n, k):
    return 0.0 if isinstance(n, int) and n == 0 else acc[(k - 1) % len(acc)][:, BE - 1:BE]


def edges_sum(nc, d, g):
    with Phase(nc, "L0") as ph:
        gath, idx, s_gath, s_idx, s_go = edge_buffers(ph, D)
        mask = [ph.sb(f"mask{k}", [P, BE], BF16) for k in range(SLOTS)]
        acc = [ph.sb(f"acc{k}", [P, BE]) for k in range(SLOTS)]
        back = [ph.sb(f"back{k}", [P, BT, D]) for k in range(SLOTS)]
        pT = [ph.ps(f"pT{k}") for k in range(2)]
        pB = [ph.ps(f"pB{k}") for k in range(2)]
        s_turn, s_scan, s_ret, s_back = (ph.sem(n) for n in ("turn", "scan", "ret", "back"))
        s_mask, s_out = ph.slot_sems("mask", SLOTS), ph.slot_sems("out", SLOTS)
        run = g["run"].rearrange("(p t) f -> p t f", p=P)
        beside = NodeEdges(ph, d, g)
        block = ph.block()

        @block.sync
        def _(sp):
            beside.sync_before(sp)
            pipeline(sp, BATCHES, SLOTS, [(0, mask_load(sp, g["same"], mask, s_mask, s_scan)), (0, beside.sync_stage(sp))])
            beside.sync_after(sp)

        @block.gpsimd
        def _(gp):
            beside.pool_before(gp)
            gatherer(gp, d["x"], gath, idx, s_gath, s_idx, s_go, s_turn)

        @block.tensor
        def _(pe):
            def turn(n, k, r):
                landed(pe, s_gath, k, r, BT)
                room(pe, s_scan, n, 2)
                for t in range(BT):
                    m = pe.transpose(pT[k % 2][:, cols(t)], gath[k][:, t, :], g["ident"][:, :])
                m.then_inc(s_turn, 1)
            beside.tensor_before(pe)
            pipeline(pe, BATCHES, SLOTS, [(0, turn), (1, turn_back(pe, g, acc, pB, s_scan, s_back, s_ret)), (0, beside.tensor_stage(pe))])
            beside.tensor_after(pe)

        @block.vector
        def _(v):
            ahead = indexer(v, g, idx, s_idx, s_gath)
            beside.vector_before(v)
            pipeline(v, BATCHES, SLOTS, [(0, running_sum(v, pT, mask, acc, s_turn, s_mask, s_ret, s_scan)), (0, ahead),
                                         (0, beside.vector_stage(v))])
            beside.vector_after(v)

        @block.scalar
        def _(act):
            pipeline(act, BATCHES, SLOTS, [(2, copy_rows(act, back, pB, s_ret, s_back, s_out)), (2, store_rows(act, run, back, s_back, s_out))])
            all_stored(act, s_out)


def turn_back(pe, g, acc, pB, s_acc, s_back, s_ret):
    def ret(n, k, r):
        need(pe, s_acc, n)
        room(pe, s_back, n, 2)
        for t in range(BT):
            m = pe.transpose(pB[k % 2][:, cols(t)], acc[k][:, cols(t)], g["ident"][:, :])
        m.then_inc(s_ret, 1)
    return ret


def running_sum(v, pT, mask, acc, s_turn, s_mask, s_ret, s_scan):
    def scan(n, k, r):
        need(v, s_turn, n)
        landed(v, s_mask, k, r)
        room(v, s_ret, n, SLOTS)
        room(v, s_scan, n, 1)
        v.tensor_tensor_scan(acc[k][:, :], mask[k][:, :], pT[k % 2][:, :], start_of(acc, n, k), ALU.mult, ALU.add).then_inc(s_scan, 1)
    return scan


def store_rows(eng, run, back, s_back, s_out):
    def store(n, k, r):
        need(eng, s_back, n)
        eng.dma_start(run[:, bass.ds(n * BT, BT), :], back[k][:, :, :]).then_inc(s_out[k], 16)
    return store


def copy_rows(act, back, pB, s_ret, s_back, s_out):
    def copy(n, k, r):
        need(act, s_ret, n)
        stored(act, s_out, k, r)
        act.activation(rows(back[k][:, :, :]), pB[k % 2][:, :], ACT.Copy).then_inc(s_back, 1)
    return copy


def all_stored(eng, s_out):
    for k in range(SLOTS):
        eng.wait_ge(s_out[k], 16 * BATCHES // SLOTS)


def edges_conv(nc, g, ew):
    with Phase(nc, "L2") as ph:
        slot = lambda name, shape, dtype=F32: [ph.sb(f"{name}{k}", shape, dtype) for k in range(SLOTS)]
        mask, low = slot("mask", [P, BE], BF16), slot("low", [P, BE], BF16)
        sent, scaled, back = (slot(n, [P, BT, D]) for n in ("sent", "scaled", "back"))
        acc, hot_low, hot_high = slot("acc", [P, BE]), slot("hotl", [P, BE], BF16), slot("hoth", [P, BT, HIGH], BF16)
        found, scale = slot("found", [P, BT]), slot("scale", [P, BT])
        part = [ph.sb(f"part{k}", [P, BT, HIGH]) for k in range(2)]
        high = ph.sb("high", [P, TILES], BF16)
        work = ph.sb("work", [P, TILES], I32)
        lane_i, lane, row_i, row = ph.sb("lane_i", [P, 1], I32), ph.sb("lane", [P, 1]), ph.sb("row_i", [P, HIGH], I32), ph.sb("row", [P, HIGH], BF16)
        pT = [ph.ps(f"pT{k}") for k in range(2)]
        pB = [ph.ps(f"pB{k}") for k in range(2)]
        pL = [ph.ps(f"pL{k}") for k in range(2)]
        s_iota, s_prep, s_hotl, s_hoth, s_look, s_part, s_pick, s_scale, s_turn, s_scan, s_ret, s_back, s_sum = (ph.sem(n) for n in
            ("iota", "prep", "hotl", "hoth", "look", "part", "pick", "scale", "turn", "scan", "ret", "back", "sum"))
        s_mask, s_low, s_sent, s_out = (ph.slot_sems(n, SLOTS) for n in ("mask", "low", "sent", "out"))
        run = g["run"].rearrange("(p t) f -> p t f", p=P)
        table = g["sent"].rearrange("(p t) f -> p t f", p=P)
        block = ph.block()

        @block.sync
        def _(sp):
            def load(n, k, r):
                room(sp, s_scale, n, SLOTS)
                sp.dma_start(sent[k][:, :, :], table[:, bass.ds(n * BT, BT), :]).then_inc(s_sent[k], 16)
            pipeline(sp, BATCHES, SLOTS, [(0, mask_load(sp, g["low"], low, s_low, s_hotl)), (0, load),
                                          (2, mask_load(sp, g["same"], mask, s_mask, s_scan)), (8, store_rows(sp, run, back, s_back, s_out))])
            all_stored(sp, s_out)

        @block.gpsimd
        def _(gp):
            gp.iota(lane_i[:, :], [[1, 1]], base=0, channel_multiplier=1).then_inc(s_iota, 1)
            gp.iota(row_i[:, :], [[1, HIGH]], base=0, channel_multiplier=0).then_inc(s_iota, 1)

        @block.tensor
        def _(pe):
            def look(n, k, r):
                need(pe, s_hotl, n)
                room(pe, s_part, n, 2)
                for t in range(BT):
                    for j in range(3):
                        m = pe.matmul(pL[k % 2][:, t * HIGH:(t + 1) * HIGH], hot_low[k][:, cols(t)], g["dinv_low"][:, j, :],
                                      start=j == 0, stop=j == 2)
                m.then_inc(s_look, 1)

            def turn(n, k, r):
                need(pe, s_scale, n)
                room(pe, s_scan, n, 2)
                for t in range(BT):
                    m = pe.transpose(pT[k % 2][:, cols(t)], scaled[k][:, t, :], g["ident"][:, :])
                m.then_inc(s_turn, 1)
            pipeline(pe, BATCHES, SLOTS, [(0, look), (2, turn), (4, turn_back(pe, g, acc, pB, s_scan, s_back, s_ret))])

        @block.vector
        def _(v):
            v.wait_ge(s_iota, 2)
            v.tensor_copy(lane[:, :], lane_i[:, :]).then_inc(s_prep, 1)
            v.tensor_copy(row[:, :], row_i[:, :]).then_inc(s_prep, 1)
            v.tensor_scalar(work[:, :], g["src"][:, 0:TILES], LO, None, ALU.arith_shift_right).then_inc(s_prep, 1)
            v.wait_ge(s_prep, 3)
            v.tensor_copy(high[:, :], work[:, :]).then_inc(s_prep, 1)
            v.wait_ge(s_prep, 4)

            def hot(n, k, r):
                landed(v, s_low, k, r)
                room(v, s_look, n, SLOTS)
                v.tensor_scalar(hot_low[k][:, :], low[k][:, :], lane[:, 0:1], None, ALU.is_equal).then_inc(s_hotl, 1)

            def hot_of_high(n, k, r):
                room(v, s_part, n, SLOTS)
                v.tensor_tensor(hot_high[k][:, :, :], row[:, :].unsqueeze(1).to_broadcast([P, BT, HIGH]),
                                high[:, bass.ds(n * BT, BT)].unsqueeze(2).to_broadcast([P, BT, HIGH]), ALU.is_equal).then_inc(s_hoth, 1)

            def pick(n, k, r):
                need(v, s_look, n)
                need(v, s_hoth, n)
                room(v, s_sum, n, 2)
                v.tensor_tensor(rows(part[k % 2][:, :, :]), pL[k % 2][:, 0:BT * HIGH], rows(hot_high[k][:, :, :]), ALU.mult).then_inc(s_part, 1)

            def gather_up(n, k, r):
                need(v, s_part, n)
                v.tensor_reduce(found[k][:, :], part[k % 2][:, :, :], AX, ALU.add).then_inc(s_sum, 1)

            def times_weight(n, k, r):
                need(v, s_sum, n)
                room(v, s_scale, n, SLOTS)
                v.tensor_tensor(scale[k][:, :], found[k][:, :], ew[:, bass.ds(n * BT, BT)], ALU.mult).then_inc(s_pick, 1)
            pipeline(v, BATCHES, SLOTS, [(0, hot), (1, pick), (0, hot_of_high), (1, gather_up), (3, running_sum(v, pT, mask, acc, s_turn, s_mask, s_ret, s_scan)),
                                         (1, times_weight)])

        @block.scalar
        def _(act):
            def weigh(n, k, r):
                landed(act, s_sent, k, r)
                need(act, s_pick, n)
                room(act, s_turn, n, SLOTS)
                for t in range(BT):
                    a = act.activation(scaled[k][:, t, :], sent[k][:, t, :], ACT.Copy, scale=scale[k][:, t:t + 1])
                a.then_inc(s_scale, 1)
            pipeline(act, BATCHES, SLOTS, [(0, weigh), (3, copy_rows(act, back, pB, s_ret, s_back, s_out))])


def mask_load(sp, table, mask, s_mask, s_free):
    def load(n, k, r):
        room(sp, s_free, n, SLOTS)
        sp.dma_start(mask[k][:, :], table[bass.ds(n * BE, BE)].unsqueeze(0).to_broadcast([P, BE])).then_inc(s_mask[k], 16)
    return load


def edges_max(nc, d, g):
    w = g["w"]
    with Phase(nc, "L1") as ph:
        gath, idx, s_gath, s_idx, s_go = edge_buffers(ph, D)
        slot = lambda name, width=BE, dtype=F32: [ph.sb(f"{name}{k}", [P, width], dtype) for k in range(SLOTS)]
        weight = ph.sb("weight", [P, TILES])
        same, fresh = slot("same", BE, BF16), slot("fresh", BE, BF16)
        seed, sent, dest, pre, hid, acc = (slot(n) for n in ("seed", "sent", "dest", "pre", "hid", "acc"))
        back = [ph.sb(f"back{k}", [P, BT, D]) for k in range(SLOTS)]
        pA = [ph.ps(f"pA{k}") for k in range(2)]
        pS = [ph.ps(f"pS{k}") for k in range(2)]
        pM = [ph.ps(f"pM{k}") for k in range(2)]
        pB = [ph.ps(f"pB{k}") for k in range(2)]
        s_wt, s_sent, s_turn, s_turns, s_dest, s_pre, s_hid, s_msg, s_max, s_ret, s_back = (ph.sem(n) for n in
            ("wt", "sent", "turn", "turns", "dest", "pre", "hid", "msg", "max", "ret", "back"))
        s_same, s_fresh, s_seed, s_out = (ph.slot_sems(n, SLOTS) for n in ("same", "fresh", "seed", "out"))
        run = g["run"].rearrange("(p t) f -> p t f", p=P)
        seeds = g["seed"].rearrange("(p t) f -> p t f", p=P)
        block = ph.block()

        @block.sync
        def _(sp):
            sp.dma_start(weight[:, :], d["weight"]).then_inc(s_wt, 16)

            def load_seed(n, k, r):
                room(sp, s_turns, n, SLOTS)
                sp.dma_start(seed[k][:, :].rearrange("p (t f) -> p t f", t=BT), seeds[:, bass.ds(n * BT, BT), :]).then_inc(s_seed[k], 16)
            pipeline(sp, BATCHES, SLOTS, [(0, load_seed), (0, mask_load(sp, g["same"], same, s_same, s_dest)),
                                          (0, mask_load(sp, g["fresh"], fresh, s_fresh, s_max))])

        @block.gpsimd
        def _(gp):
            gatherer(gp, g["tab"], gath, idx, s_gath, s_idx, s_go, s_sent)

        @block.tensor
        def _(pe):
            def turn_seed(n, k, r):
                landed(pe, s_seed, k, r)
                room(pe, s_dest, n, 2)
                for t in range(BT):
                    m = pe.transpose(pS[k % 2][:, cols(t)], seed[k][:, cols(t)], g["ident"][:, :])
                m.then_inc(s_turns, 1)

            def turn(n, k, r):
                need(pe, s_sent, n)
                room(pe, s_pre, n, 2)
                for t in range(BT):
                    m = pe.transpose(pA[k % 2][:, cols(t)], sent[k][:, cols(t)], g["ident"][:, :])
                m.then_inc(s_turn, 1)

            def message(n, k, r):
                need(pe, s_hid, n)
                room(pe, s_max, n, 2)
                pe.matmul(pM[k % 2][:, :], w["W2"][:, :], hid[k][:, :], start=True, stop=True).then_inc(s_msg, 1)

            pipeline(pe, BATCHES, SLOTS, [(0, turn_seed), (0, turn), (1, message), (2, turn_back(pe, g, acc, pB, s_max, s_back, s_ret))])

        @block.vector
        def _(v):
            def add_weight(n, k, r):
                landed(v, s_gath, k, r, BT)
                room(v, s_turn, n, SLOTS)
                for t in range(BT):
                    a = v.scalar_tensor_tensor(sent[k][:, cols(t)], g["wide"]["W1w"][:, :], weight[:, bass.ds(n * BT + t, 1)],
                                               gath[k][:, t, :], ALU.mult, ALU.add)
                a.then_inc(s_sent, 1)

            def spread(n, k, r):
                need(v, s_turns, n)
                landed(v, s_same, k, r)
                room(v, s_dest, n, 1)
                room(v, s_pre, n, SLOTS)
                v.tensor_tensor_scan(dest[k][:, :], same[k][:, :], pS[k % 2][:, :], start_of(dest, n, k), ALU.mult, ALU.add).then_inc(s_dest, 1)

            def add_dest(n, k, r):
                need(v, s_turn, n)
                need(v, s_dest, n)
                room(v, s_hid, n, SLOTS)
                v.tensor_tensor(pre[k][:, :], pA[k % 2][:, :], dest[k][:, :], ALU.add).then_inc(s_pre, 1)

            def top(n, k, r):
                need(v, s_msg, n)
                landed(v, s_fresh, k, r)
                room(v, s_max, n, 1)
                room(v, s_ret, n, SLOTS)
                v.tensor_tensor_scan(acc[k][:, :], fresh[k][:, :], pM[k % 2][:, :], start_of(acc, n, k), ALU.add, ALU.max).then_inc(s_max, 1)
            v.wait_ge(s_wt, 16)
            ahead = indexer(v, g, idx, s_idx, s_gath)
            pipeline(v, BATCHES, SLOTS, [(0, add_weight), (0, ahead), (0, spread), (0, add_dest), (2, top)])

        @block.scalar
        def _(act):
            def relu(n, k, r):
                need(act, s_pre, n)
                room(act, s_msg, n, SLOTS)
                act.activation(hid[k][:, :], pre[k][:, :], ACT.Relu).then_inc(s_hid, 1)

            pipeline(act, BATCHES, SLOTS, [(0, relu), (3, copy_rows(act, back, pB, s_ret, s_back, s_out)),
                                           (3, store_rows(act, run, back, s_back, s_out))])
            all_stored(act, s_out)


def edges_gate(nc, g, z):
    w = g["w"]
    H = slice(0, HID)
    with Phase(nc, "L2a") as ph:
        gath, idx, s_gath, s_idx, s_go = edge_buffers(ph, W2)
        slot = lambda name, width=BE, dtype=F32, p=HID: [ph.sb(f"{name}{k}", [p, width], dtype) for k in range(SLOTS)]
        same, seed = slot("same", BE, BF16), slot("seed", BT * HID, F32, P)
        dest, pre, hid = (slot(n) for n in ("dest", "pre", "hid"))
        pA = [ph.ps(f"pA{k}") for k in range(2)]
        pS = [ph.ps(f"pS{k}") for k in range(2)]
        pZ = [ph.ps(f"pZ{k}") for k in range(2)]
        s_turn, s_turns, s_dest, s_pre, s_hid, s_dot, s_z, s_tgo = (ph.sem(n) for n in
            ("turn", "turns", "dest", "pre", "hid", "dot", "z", "tgo"))
        s_same, s_seed, s_aside = (ph.slot_sems(n, SLOTS) for n in ("same", "seed", "aside"))
        aside = g["sent"].rearrange("(p t) f -> p t f", p=P)
        seeds = g["seed"].rearrange("(p t) f -> p t f", p=P)
        block = ph.block()

        @block.sync
        def _(sp):
            def load_seed(n, k, r):
                room(sp, s_turns, n, SLOTS)
                sp.dma_start(seed[k][:, :].rearrange("p (t f) -> p t f", t=BT), seeds[:, bass.ds(n * BT, BT), 0:HID]).then_inc(s_seed[k], 16)

            def load_same(n, k, r):
                room(sp, s_dest, n, SLOTS)
                sp.dma_start(same[k][:, :], g["same"][bass.ds(n * BE, BE)].unsqueeze(0).to_broadcast([HID, BE])).then_inc(s_same[k], 16)
            pipeline(sp, BATCHES, SLOTS, [(0, load_seed), (0, load_same)])

        @block.gpsimd
        def _(gp):
            gatherer(gp, g["tab_h"], gath, idx, s_gath, s_idx, s_go, s_turn, s_aside)

        @block.tensor
        def _(pe):
            def turn(n, k, r):
                landed(pe, s_seed, k, r)
                room(pe, s_dest, n, 2)
                pe.sem_inc(s_tgo, 1)
                for t in range(BT):
                    m = pe.transpose(pS[k % 2][H, cols(t)], seed[k][:, t * HID:(t + 1) * HID], g["ident"][:, :])
                m.then_inc(s_turns, 1)
                landed(pe, s_gath, k, r, BT)
                room(pe, s_pre, n, 2)
                pe.sem_inc(s_tgo, 1)
                for t in range(BT):
                    m = pe.transpose(pA[k % 2][H, cols(t)], gath[k][:, t, H], g["ident"][:, :])
                m.then_inc(s_turn, 1)

            def dot(n, k, r):
                need(pe, s_hid, n)
                room(pe, s_z, n, 2)
                for t in range(BT):
                    m = pe.matmul(pZ[k % 2][:, t:t + 1], hid[k][:, cols(t)], w["M2"][:, :], start=True, stop=True)
                m.then_inc(s_dot, 1)
            pipeline(pe, BATCHES, SLOTS, [(0, turn), (2, dot)])

        @block.vector
        def _(v):
            def spread(n, k, r):
                need(v, s_turns, n)
                landed(v, s_same, k, r)
                room(v, s_dest, n, 1)
                room(v, s_pre, n, SLOTS)
                v.tensor_tensor_scan(dest[k][:, :], same[k][:, :], pS[k % 2][H, :], start_of(dest, n, k), ALU.mult, ALU.add).then_inc(s_dest, 1)

            def add_dest(n, k, r):
                need(v, s_turn, n)
                need(v, s_dest, n)
                room(v, s_hid, n, SLOTS)
                v.tensor_tensor(pre[k][:, :], pA[k % 2][H, :], dest[k][:, :], ALU.add).then_inc(s_pre, 1)

            def keep(n, k, r):
                need(v, s_dot, n)
                v.tensor_copy(z[:, bass.ds(n * BT, BT)], pZ[k % 2][:, 0:BT]).then_inc(s_z, 1)
            ahead = indexer(v, g, idx, s_idx, s_gath)
            pipeline(v, BATCHES, SLOTS, [(0, spread), (0, add_dest), (0, ahead), (3, keep)])

        @block.scalar
        def _(act):
            def gelu(n, k, r):
                need(act, s_pre, n)
                room(act, s_dot, n, SLOTS)
                act.activation(hid[k][:, :], pre[k][:, :], ACT.Gelu).then_inc(s_hid, 1)

            def put_aside(n, k, r):
                landed(act, s_gath, k, r, BT)
                act.dma_start(aside[:, bass.ds(n * BT, BT), :], gath[k][:, :, HID:W2]).then_inc(s_aside[k], 16)
            pipeline(act, BATCHES, SLOTS, [(0, put_aside), (0, gelu)])
            all_stored(act, s_aside)


def degrees(nc, g, ew):
    with Phase(nc, "deg") as ph:
        turns = -(-TILES // P)
        lin = [ph.sb(f"lin{k}", [P, P]) for k in range(2)]
        c = ph.sb("c", [P, TILES])
        run = ph.sb("run", [P, TILES])
        open_ = ph.sb("open", [P, TILES])
        ends = ph.sb("ends", [1, 2, P])
        carry = ph.sb("carry", [1, P + 1])
        cin = ph.sb("cin", [P, 1])
        deg = ph.sb("deg", [P, NT])
        by_high, rest = ph.sb("by_high", [HIGH, P]), ph.sb("rest", [P, HIGH])
        idx = [ph.sb(f"idx{k}", [P, BT], I32) for k in range(NSLOTS)]
        got = [ph.sb(f"got{k}", [P, BT]) for k in range(NSLOTS)]
        pT = [ph.ps(f"pT{k}") for k in range(2)]
        pE = ph.ps("pE")
        pC = ph.ps("pC")
        s_sig, s_t, s_lin, s_c, s_v, s_pe, s_run, s_ix, s_go, s_got, s_deg, s_lay = (ph.sem(n) for n in
            ("sig", "t", "lin", "c", "v", "pe", "run", "ix", "go", "got", "deg", "lay"))
        s_ld, s_gath = ph.slot_sems("ld", 2), ph.slot_sems("gath", NSLOTS)
        block = ph.block()

        @block.scalar
        def _(act):
            act.activation(ew[:, :], ew[:, :], ACT.Sigmoid, bias=g["wide"]["m2"][:, 0:1]).then_inc(s_sig, 1)
            for j in range(turns):
                width = min(P, TILES - j * P)
                need(act, s_t, j)
                if j >= 2:
                    act.wait_ge(s_ld[j % 2], 16 * (j // 2))
                act.activation(lin[j % 2][0:width, :], pT[j % 2][0:width, 0:P], ACT.Copy).then_inc(s_lin, 1)
                need(act, s_lin, j)
                act.dma_start(g["ew"].rearrange("(t l) a -> t (l a)", l=P)[j * P:j * P + width, :], lin[j % 2][0:width, :]).then_inc(s_ld[j % 2], 16)
            for k in range(2):
                act.wait_ge(s_ld[k], 16 * len(range(k, turns, 2)))
            act.dma_start(c[:, :], g["ew"].rearrange("(p i) a -> p (i a)", p=P)).then_inc(s_c, 16)
            act.wait_ge(s_run, 1)
            act.dma_start(g["ew"].rearrange("(p i) a -> p (i a)", p=P), run[:, :]).then_inc(s_c, 16)
            act.wait_ge(s_c, 32)
            act.sem_inc(s_run, 1)
            act.wait_ge(s_deg, 1)
            act.activation(deg[:, :], deg[:, :], ACT.Sqrt).then_inc(s_deg, 1)

        @block.tensor
        def _(pe):
            pe.wait_ge(s_sig, 1)
            for j in range(turns):
                width = min(P, TILES - j * P)
                room(pe, s_lin, j, 2)
                pe.transpose(pT[j % 2][0:width, 0:P], ew[:, j * P:j * P + width], g["ident"][:, :]).then_inc(s_t, 1)
            pe.wait_ge(s_v, 2)
            pe.transpose(pE[0:1, 0:P], run[:, TILES - 1:TILES], g["ident"][:, :])
            pe.transpose(pE[0:1, P:2 * P], open_[:, TILES - 1:TILES], g["ident"][:, :]).then_inc(s_pe, 1)
            pe.wait_ge(s_v, 5)
            pe.matmul(pC[:, 0:1], carry[0:1, 0:P], g["ones"][0:1, 0:1], start=True, stop=True).then_inc(s_pe, 1)
            pe.wait_ge(s_lay, 32)
            pe.transpose(pC[:, P:P + HIGH], by_high[:, :], g["ident"][0:HIGH, 0:HIGH]).then_inc(s_pe, 1)

        @block.vector
        def _(v):
            link = Chain(v, s_v)
            v.wait_ge(s_c, 16)
            link(v.tensor_tensor_scan(run[:, :], g["same_c"][:, :], c[:, :], 0.0, ALU.mult, ALU.add))
            link(v.tensor_tensor_scan(open_[:, :], g["same_c"][:, :], g["same_c"][:, :], 1.0, ALU.mult, ALU.min))
            v.wait_ge(s_pe, 1)
            link(v.memset(carry[:, :], 0.0))
            link(v.tensor_copy(ends[:, :, :].rearrange("a b c -> a (b c)"), pE[0:1, 0:2 * P]))
            link(v.tensor_tensor_scan(carry[0:1, 1:P + 1], ends[0:1, 1, :], ends[0:1, 0, :], 0.0, ALU.mult, ALU.add))
            v.wait_ge(s_pe, 2)
            link(v.tensor_copy(cin[:, :], pC[:, 0:1]))
            v.scalar_tensor_tensor(run[:, :], open_[:, :], cin[:, 0:1], run[:, :], ALU.mult, ALU.add).then_inc(s_run, 1)

            def keep(n, k, r):
                landed(v, s_gath, k, r, BT)
                v.tensor_copy(deg[:, bass.ds(n * BT, BT)], got[k][:, :]).then_inc(s_got, 1)
            pipeline(v, NB, NSLOTS, [(0, keep)])
            v.wait_ge(s_got, NB)
            link(v.tensor_tensor(deg[:, :], deg[:, :], g["has"][:, :], ALU.mult))
            v.tensor_scalar(deg[:, :], deg[:, :], 1.0, None, ALU.add).then_inc(s_deg, 1)
            v.wait_ge(s_deg, 2)
            v.reciprocal(g["dinv"][:, :], deg[:, :]).then_inc(s_deg, 1)
            v.wait_ge(s_pe, 3)
            link(v.tensor_copy(rest[:, :], pC[:, P:P + HIGH]))
            for j in range(3):
                link(v.tensor_copy(g["dinv_low"][:, j, :], rest[:, :]))
                if j < 2:
                    link(v.tensor_tensor(rest[:, :], rest[:, :], g["dinv_low"][:, j, :], ALU.subtract))

        @block.gpsimd
        def _(gp):
            gp.wait_ge(s_run, 2)

            def fetch(n, k, r):
                room(gp, s_got, n, NSLOTS)
                gp.tensor_copy(idx[k][:, :], g["last_e"][:, bass.ds(n * BT, BT)]).then_inc(s_ix, 1)
                need(gp, s_ix, n)
                gp.sem_inc(s_go, 1)
                for t in range(BT):
                    gp.indirect_dma_start(out=got[k][:, t:t + 1], out_offset=None, in_=g["ew"],
                                          in_offset=bass.IndirectOffsetOnAxis(ap=idx[k][:, t:t + 1], axis=0)).then_inc(s_gath[k], 16)
            pipeline(gp, NB, NSLOTS, [(0, fetch)])

        @block.sync
        def _(sp):
            sp.wait_ge(s_deg, 3)
            sp.dma_start(g["dinv_row"].rearrange("(p t) -> p t", p=P), g["dinv"][:, :]).then_inc(s_lay, 16)
            sp.wait_ge(s_lay, 16)
            sp.dma_start(by_high[:, :], g["dinv_row"].rearrange("(h l) -> h l", l=P)).then_inc(s_lay, 16)


def edges_attention(nc, g):
    with Phase(nc, "L3") as ph:
        gath, idx, s_gath, s_idx, s_go = edge_buffers(ph, 2 * D)
        slot = lambda name, width=BE, dtype=F32, c=2: [ph.sb(f"{name}{k}", [P, width], dtype) for k in range(c)]
        same, fresh, ends = (slot(n, BE, BF16, SLOTS) for n in ("same", "fresh", "ends"))
        seed = slot("seed", BE, F32, SLOTS)
        dest, prod, top, ref, prob, pv = (slot(n) for n in ("dest", "prod", "top", "ref", "prob", "pv"))
        factor, start = slot("factor", 1), slot("start", 2)
        sums = [ph.sb(f"sums{k}", [P, 2, BE]) for k in range(2)]
        back = [ph.sb(f"back{k}", [P, BT, W3]) for k in range(SLOTS)]
        blocks = ph.sb("blocks", [P, P])
        minus = ph.sb("minus", [P, P])
        pS, pK, pB, pD = (ph.ps(n) for n in ("pS", "pK", "pB", "pD"))
        pV = [ph.ps(f"pV{k}") for k in range(2)]
        pC = [ph.ps(f"pC{k}") for k in range(2)]
        (s_c, s_cc, s_turns, s_turnk, s_turnv, s_dest, s_prod, s_score, s_top, s_ref, s_diff, s_factor, s_prob, s_pv, s_init,
         s_num, s_den, s_ret, s_back) = (ph.sem(n) for n in ("c", "cc", "turns", "turnk", "turnv", "dest", "prod", "score", "top",
            "ref", "diff", "factor", "prob", "pv", "init", "num", "den", "ret", "back"))
        s_same, s_fresh, s_ends, s_seed, s_out = (ph.slot_sems(n, SLOTS) for n in ("same", "fresh", "ends", "seed", "out"))
        run = g["run3"].rearrange("(p t) f -> p t f", p=P)
        seeds = g["seed"].rearrange("(p t) f -> p t f", p=P)
        block = ph.block()

        @block.sync
        def _(sp):
            def load_seed(n, k, r):
                room(sp, s_turns, n, SLOTS)
                sp.dma_start(seed[k][:, :].rearrange("p (t f) -> p t f", t=BT), seeds[:, bass.ds(n * BT, BT), :]).then_inc(s_seed[k], 16)
            pipeline(sp, BATCHES, SLOTS, [(0, load_seed), (0, mask_load(sp, g["same"], same, s_same, s_num)),
                                          (0, mask_load(sp, g["fresh"], fresh, s_fresh, s_top)),
                                          (0, mask_load(sp, g["ends"], ends, s_ends, s_ref))])

        @block.gpsimd
        def _(gp):
            gatherer(gp, g["tab_kv"], gath, idx, s_gath, s_idx, s_go, s_turnv)

        @block.tensor
        def _(pe):
            def turn_seed(n, k, r):
                landed(pe, s_seed, k, r)
                room(pe, s_dest, n, 1)
                for t in range(BT):
                    m = pe.transpose(pS[:, cols(t)], seed[k][:, cols(t)], g["ident"][:, :])
                m.then_inc(s_turns, 1)

            def turn_keys(n, k, r):
                landed(pe, s_gath, k, r, BT)
                room(pe, s_prod, n, 1)
                for t in range(BT):
                    m = pe.transpose(pK[:, cols(t)], gath[k][:, t, 0:D], g["ident"][:, :])
                m.then_inc(s_turnk, 1)

            def turn_values(n, k, r):
                room(pe, s_pv, n, 2)
                for t in range(BT):
                    m = pe.transpose(pV[k % 2][:, cols(t)], gath[k][:, t, D:2 * D], g["ident"][:, :])
                m.then_inc(s_turnv, 1)

            def score(n, k, r):
                need(pe, s_prod, n)
                room(pe, s_prob, n, 2)
                pe.matmul(pC[k % 2][:, :], blocks[:, :], prod[k % 2][:, :], start=True, stop=True).then_inc(s_score, 1)

            def distance(n, k, r):
                need(pe, s_top, n)
                need(pe, s_ref, n)
                pe.matmul(pC[k % 2][:, :], minus[:, :], ref[k % 2][:, :], start=False, stop=True, skip_group_check=True).then_inc(s_diff, 1)

            def ret(n, k, r):
                need(pe, s_num, n)
                need(pe, s_den, n)
                room(pe, s_back, n, 1)
                for t in range(BT):
                    pe.transpose(pB[:, cols(t)], sums[k % 2][:, 0, cols(t)], g["ident"][:, :])
                for t in range(BT):
                    m = pe.transpose(pD[:, cols(t)], sums[k % 2][:, 1, cols(t)], g["ident"][:, :])
                m.then_inc(s_ret, 1)
            pe.wait_ge(s_cc, HEADS + 1)
            pipeline(pe, BATCHES, SLOTS, [(0, turn_seed), (2, distance), (1, score), (0, turn_keys), (2, turn_values), (4, ret)])

        @block.vector
        def _(v):
            v.memset(blocks[:, :], 0.0).then_inc(s_c, 1)
            v.tensor_scalar(minus[:, :], g["ident"][:, :], -1.0, None, ALU.mult).then_inc(s_cc, 1)
            v.wait_ge(s_c, 1)
            for h in range(HEADS):
                part = slice(h * HEAD, (h + 1) * HEAD)
                v.memset(blocks[part, part], float(HEAD) ** -0.5).then_inc(s_cc, 1)

            def spread(n, k, r):
                need(v, s_turns, n)
                landed(v, s_same, k, r)
                room(v, s_dest, n, 1)
                room(v, s_prod, n, 2)
                v.tensor_tensor_scan(dest[k % 2][:, :], same[k][:, :], pS[:, :], start_of(dest, n, k % 2), ALU.mult, ALU.add).then_inc(s_dest, 1)

            def query(n, k, r):
                need(v, s_turnk, n)
                need(v, s_dest, n)
                room(v, s_score, n, 2)
                v.tensor_tensor(prod[k % 2][:, :], pK[:, :], dest[k % 2][:, :], ALU.mult).then_inc(s_prod, 1)

            def peak(n, k, r):
                need(v, s_score, n)
                landed(v, s_fresh, k, r)
                room(v, s_top, n, 1)
                room(v, s_ref, n, 2)
                v.tensor_tensor_scan(top[k % 2][:, :], fresh[k][:, :], pC[k % 2][:, :], start_of(top, n, k % 2), ALU.add, ALU.max).then_inc(s_top, 1)

            def reference(n, k, r):
                landed(v, s_ends, k, r)
                need(v, s_top, n)
                room(v, s_diff, n, 2)
                room(v, s_factor, n, 1)
                v.tensor_tensor_scan(ref[k % 2][:, ::-1], ends[k][:, ::-1], top[k % 2][:, ::-1], FAR, ALU.add, ALU.max).then_inc(s_ref, 1)

            def weigh(n, k, r):
                need(v, s_prob, n)
                need(v, s_turnv, n)
                room(v, s_num, n, 2)
                v.tensor_tensor(pv[k % 2][:, :], pV[k % 2][:, :], prob[k % 2][:, :], ALU.mult).then_inc(s_pv, 1)

            def rescale(n, k, r):
                need(v, s_factor, n)
                room(v, s_num, n, 1)
                if isinstance(n, int) and n == 0:
                    v.memset(start[0][:, :], 0.0).then_inc(s_init, 1)
                else:
                    v.scalar_tensor_tensor(start[k % 2][:, :], factor[k % 2][:, 0:1].to_broadcast([P, 2]), 1.0,
                                           sums[(k - 1) % 2][:, :, BE - 1], ALU.min, ALU.mult).then_inc(s_init, 1)

            def total(n, k, r):
                landed(v, s_same, k, r)
                need(v, s_init, n)
                room(v, s_ret, n, 2)
                v.tensor_tensor_scan(sums[k % 2][:, 1, :], same[k][:, :], prob[k % 2][:, :], start[k % 2][:, 1:2], ALU.mult, ALU.add).then_inc(s_den, 1)
                need(v, s_pv, n)
                v.tensor_tensor_scan(sums[k % 2][:, 0, :], same[k][:, :], pv[k % 2][:, :], start[k % 2][:, 0:1], ALU.mult, ALU.add).then_inc(s_num, 1)
            ahead = indexer(v, g, idx, s_idx, s_gath)
            pipeline(v, BATCHES, SLOTS, [(1, peak), (0, spread), (2, rescale), (1, reference), (0, query), (0, ahead), (2, weigh), (2, total)])

        @block.scalar
        def _(act):
            def exps(n, k, r):
                need(act, s_ref, n)
                room(act, s_init, n, 2)
                before = ref[(k - 1) % 2][:, BE - 1:BE] if not isinstance(n, int) or n > 0 else ref[0][:, 0:1]
                act.activation(factor[k % 2][:, :], ref[k % 2][:, 0:1], ACT.Exp, bias=before, scale=-1.0).then_inc(s_factor, 1)
                need(act, s_diff, n)
                room(act, s_num, n, 2)
                act.activation(prob[k % 2][:, :], pC[k % 2][:, :], ACT.Exp).then_inc(s_prob, 1)

            def store(n, k, r):
                need(act, s_ret, n)
                stored(act, s_out, k, r)
                act.activation(back[k][:, :, 0:D], pB[:, :].rearrange("p (t f) -> p t f", t=BT), ACT.Copy)
                act.activation(back[k][:, :, D:W3], pD[:, 0:BE:HEAD].rearrange("p (t h) -> p t h", t=BT), ACT.Copy).then_inc(s_back, 1)
                need(act, s_back, n)
                act.dma_start(run[:, bass.ds(n * BT, BT), :], back[k][:, :, :]).then_inc(s_out[k], 16)
            pipeline(act, BATCHES, SLOTS, [(0, exps), (2, store)])
            all_stored(act, s_out)


def nodes(nc, g, layer, out):
    w, wide = g["w"], g["wide"]
    width = W3 if layer == 3 else D
    table = g["run3"] if layer == 3 else g["run"]
    nxt = [("W1s", None, g["tab"]), ("M1s", None, g["tab_h"]), ("Wkv", "bkv", g["tab_kv"]), None][layer]
    seed_w = [("W1d", "b1"), ("M1d", "m1"), ("Wq", "bq"), None][layer]
    last_layer = layer == 3
    tw = w[nxt[0]].shape[1] if nxt else 0
    sw = w[seed_w[0]].shape[1] if nxt else 0
    with Phase(nc, f"N{layer}") as ph:
        slot = lambda name, shape, dtype=F32: [ph.sb(f"{name}{k}", shape, dtype) for k in range(NSLOTS)]
        idx = slot("idx", [P, BT], I32)
        got = ph.sb("got", [P, NT, width])
        agg, y, xn = (slot(n, [P, BT, D]) for n in ("agg", "y", "xn"))
        xT = slot("xT", [P, BE]) if layer != 2 else None
        aT = slot("aT", [P, BE]) if layer in (0, 1) else None
        uT = slot("uT", [P, BE]) if layer == 1 else None
        if not last_layer:
            idf, xn_T, seed, tab = slot("idf", [P, BT], I32), slot("xnT", [P, BE]), slot("seed", [P, BT, D]), slot("tab", [P, BT, W2 if layer == 1 else tw])
        sq = ph.sb("sq", [P, BT, D])
        minus, var, inv, std = (ph.sb(n, [P, BT]) for n in ("minus", "var", "inv", "std"))
        if layer >= 2:
            part = ph.sb("part", [P, BT, D])
        if last_layer:
            part2 = ph.sb("part2", [P, BT, D])
            dot, beta = ph.sb("dot", [P, BT]), ph.sb("beta", [P, BT])
            inv_den = ph.sb("inv_den", [P, BT, HEADS])
            w_out, w_skip = ph.sb("w_out", [P, D]), ph.sb("w_skip", [P, D])
        pA, pU, pY, pX, pQ = (ph.ps(n) for n in ("pA", "pU", "pY", "pX", "pQ"))
        pT = [ph.ps(f"pT{j}") for j in range(2)]
        (s_ix, s_if, s_go, s_gz, s_agg, s_turn, s_aT, s_xs, s_u, s_uT, s_y, s_dot, s_beta, s_sum, s_bias, s_var, s_std, s_inv, s_xn,
         s_turnx, s_xnT, s_keep, s_tab, s_tabc, s_seedc, s_prep, s_norm, s_att, s_mix, s_zero, s_pre, s_ago) = (ph.sem(n) for n in (
            "ix", "if", "go", "gz", "agg", "turn", "aT", "xs", "u", "uT", "y", "dot", "beta", "sum", "bias", "var", "std", "inv", "xn",
            "turnx", "xnT", "keep", "tab", "tabc", "seedc", "prep", "norm", "att", "mix", "zero", "pre", "ago"))
        s_got, s_scat, s_tout = (ph.slot_sems(n, NSLOTS) for n in ("got", "scat", "tout"))
        block = ph.block()
        over = lambda a, n, m=D: a.unsqueeze(2).to_broadcast([P, n, m])
        tiled = lambda a: a.unsqueeze(1).to_broadcast([P, BT, D])
        now = lambda a, n: a[:, bass.ds(n * BT, BT)]
        now3 = lambda a, n: a[:, bass.ds(n * BT, BT), :]
        per_slot = lambda k: len(range(k, NB, NSLOTS))

        @block.gpsimd
        def _(gp):
            if not last_layer and sw < D:
                for k in range(NSLOTS):
                    gp.memset(seed[k][:, :, :], 0.0).then_inc(s_zero, 1)

            def fetch(n, k, r):
                stored(gp, s_got, k, r, BT)
                gp.tensor_copy(idx[k][:, :], now(g["last"], n)).then_inc(s_ix, 1)
                need(gp, s_ix, n)
                gp.sem_inc(s_go, 1)
                for t in range(BT):
                    gp.indirect_dma_start(out=got[:, n * BT + t, :], out_offset=None, in_=table,
                                          in_offset=bass.IndirectOffsetOnAxis(ap=idx[k][:, t:t + 1], axis=0)).then_inc(s_got[k], 16)

            def scatter(n, k, r):
                stored(gp, s_scat, k, r, BT)
                gp.tensor_copy(idf[k][:, :], now(g["first"], n)).then_inc(s_if, 1)
                need(gp, s_if, n)
                need(gp, s_seedc, n)
                gp.sem_inc(s_gz, 1)
                for t in range(BT):
                    gp.indirect_dma_start(out=g["seed"], out_offset=bass.IndirectOffsetOnAxis(ap=idf[k][:, t:t + 1], axis=0),
                                          in_=seed[k][:, t, :], in_offset=None, bounds_check=EP - 1, oob_is_err=False).then_inc(s_scat[k], 16)
            for n in range(NB):
                fetch(n, n % NSLOTS, n // NSLOTS)
            if not last_layer:
                pipeline(gp, NB, NSLOTS, [(0, scatter)])
                for k in range(NSLOTS):
                    gp.wait_ge(s_scat[k], 16 * BT * per_slot(k))

        @block.sync
        def _(sp):
            if last_layer:
                full, rest = N // NT, N % NT

                def store(n, k, r):
                    need(sp, s_xn, n)
                    sp.dma_start(now3(out[0:full * NT, :].rearrange("(p t) f -> p t f", t=NT), n), xn[k][0:full, :, :]).then_inc(s_tout[k], 16)
                pipeline(sp, NB, NSLOTS, [(0, store)])
                for k in range(NSLOTS):
                    sp.wait_ge(s_tout[k], 16 * per_slot(k))
                need(sp, s_keep, NB - 1)
                sp.dma_start(out[full * NT:N, :].unsqueeze(0), g["x"][full:full + 1, 0:rest, :]).then_inc(s_tout[0], 16)
                sp.wait_ge(s_tout[0], 16 * (per_slot(0) + 1))
            else:
                to = nxt[2].rearrange("(p t) f -> p t f", p=P)

                def store(n, k, r):
                    need(sp, s_tabc, n)
                    sp.dma_start(now3(to, n), tab[k][:, :, :]).then_inc(s_tout[k], 16)
                pipeline(sp, NB, NSLOTS, [(0, store)])
                for k in range(NSLOTS):
                    sp.wait_ge(s_tout[k], 16 * per_slot(k))

        @block.tensor
        def _(pe):
            def product(to, left, w_name, bias):
                m = pe.matmul(to, left, w[w_name][:, :], start=True, stop=bias is None)
                if bias is not None:
                    first = g["bias_at"][bias]
                    m = pe.matmul(to, g["ones3"][:, :], g["bias"][:, first:first + w[w_name].shape[1]], start=False, stop=True)
                return m

            def turn_agg(n, k, r):
                need(pe, s_agg, n)
                room(pe, s_aT, n, 1)
                for t in range(BT):
                    m = pe.transpose(pA[:, cols(t)], agg[k][:, t, :], g["ident"][:, :])
                m.then_inc(s_turn, 1)

            def hidden(n, k, r):
                need(pe, s_xs, n)
                need(pe, s_aT, n)
                room(pe, s_uT, n, 1)
                pe.matmul(pU[:, :], w["U1x"][:, :], xT[k][:, :], start=True, stop=False)
                pe.matmul(pU[:, :], w["U1a"][:, :], aT[k][:, :], start=False, stop=True).then_inc(s_u, 1)

            def result(n, k, r):
                room(pe, s_dot if last_layer else s_sum, n, 1)
                if layer == 0:
                    need(pe, s_xs, n)
                    need(pe, s_aT, n)
                    for t in range(BT):
                        pe.matmul(pY[:, cols(t)], xT[k][:, cols(t)], w["W0x"][:, :], start=True, stop=False)
                        m = pe.matmul(pY[:, cols(t)], aT[k][:, cols(t)], w["W0a"][:, :], start=False, stop=True)
                elif layer == 1:
                    need(pe, s_uT, n)
                    for t in range(BT):
                        m = product(pY[:, cols(t)], uT[k][:, cols(t)], "U2", "c2")
                else:
                    need(pe, s_xs, n)
                    for t in range(BT):
                        m = product(pY[:, cols(t)], xT[k][:, cols(t)], "Wskip", "bskip")
                m.then_inc(s_y, 1)

            def turn_new(n, k, r):
                need(pe, s_xn, n)
                room(pe, s_xnT, n, 1)
                for t in range(BT):
                    m = pe.transpose(pX[:, cols(t)], xn[k][:, t, :], g["ident"][:, :])
                m.then_inc(s_turnx, 1)

            def tables(n, k, r):
                need(pe, s_xnT, n)
                room(pe, s_tabc, n, 1)
                room(pe, s_seedc, n, 1)
                for t in range(BT):
                    bank, at = (pT[t * tw // BE], t * tw % BE)
                    product(bank[:, at:at + tw], xn_T[k][:, cols(t)], nxt[0], nxt[1])
                    if layer == 1:
                        product(pT[1][:, cols(t)], xn_T[k][:, cols(t)], "conv", None)
                    m = product(pQ[:, t * D:t * D + sw], xn_T[k][:, cols(t)], *seed_w)
                m.then_inc(s_tab, 1)
            stages = {0: [(0, turn_agg), (3, turn_new), (1, result), (4, tables)],
                      1: [(0, turn_agg), (3, turn_new), (1, result), (0, hidden), (4, tables)],
                      2: [(2, turn_new), (3, tables)],
                      3: [(0, result)]}[layer]
            pipeline(pe, NB, NSLOTS, stages)

        @block.vector
        def _(v):
            prep_link, norm_link, att_link, mix_link = (Chain(v, s, per) for s, per in (
                (s_prep, {1: 1, 2: 3}.get(layer, 0)), (s_norm, 5), (s_att, 8), (s_mix, 2)))
            pre_link = Chain(v, s_pre)
            if layer == 2:
                pre_link(v.tensor_tensor(g["mean"][:, :], g["dinv"][:, :], g["has"][:, :], ALU.mult))
            if last_layer:
                wb = lambda j: wide["beta"][:, j * D:(j + 1) * D]
                pre_link(v.tensor_tensor(w_out[:, :], wb(0), wb(2), ALU.add))
                pre_link(v.tensor_tensor(w_skip[:, :], wb(1), wb(2), ALU.subtract))

            def prep(n, k, r):
                landed(v, s_got, k, r, BT)
                prep_link.item(n)
                mine = now3(got, n)
                if layer == 0:
                    room(v, s_turn, n, NSLOTS)
                    v.tensor_tensor(agg[k][:, :, :], mine, over(now(g["mean"], n), BT), ALU.mult).then_inc(s_agg, 1)
                elif layer == 1:
                    room(v, s_turn, n, NSLOTS)
                    prep_link(v.tensor_tensor(agg[k][:, :, :], mine, tiled(wide["b2"][:, :]), ALU.add))
                    v.tensor_tensor(agg[k][:, :, :], agg[k][:, :, :], over(now(g["has"], n), BT), ALU.mult).then_inc(s_agg, 1)
                else:
                    room(v, s_sum, n, NSLOTS)
                    dinv = over(now(g["dinv"], n), BT)
                    prep_link(v.tensor_tensor(agg[k][:, :, :], mine, over(now(g["mean"], n), BT), ALU.mult))
                    prep_link(v.tensor_tensor(part[:, :, :], now3(g["xt"], n), dinv, ALU.mult))
                    prep_link(v.tensor_tensor(part[:, :, :], part[:, :, :], dinv, ALU.mult))
                    v.tensor_tensor(agg[k][:, :, :], agg[k][:, :, :], part[:, :, :], ALU.add).then_inc(s_agg, 1)

            def attend(n, k, r):
                landed(v, s_got, k, r, BT)
                att_link.item(n)
                mine = now3(got, n)
                att_link(v.tensor_scalar(inv_den[:, :, :], mine[:, :, D:W3], 1e-16, None, ALU.max))
                att_link(v.reciprocal(inv_den[:, :, :], inv_den[:, :, :]))
                att_link(v.tensor_tensor(inv_den[:, :, :], inv_den[:, :, :], over(now(g["has"], n), BT, HEADS), ALU.mult))
                room(v, s_sum, n, NSLOTS)
                for t in range(BT):
                    a = v.tensor_tensor(agg[k][:, t, :].rearrange("p (h c) -> p h c", h=HEADS),
                                        got[:, bass.ds(n * BT + t, 1), 0:D].rearrange("p a (h c) -> p (a h) c", h=HEADS),
                                        over(inv_den[:, t, :], HEADS, HEAD), ALU.mult)
                att_link(a)
                need(v, s_y, n)
                skip = pY[:, :].rearrange("p (t f) -> p t f", t=BT)
                att_link(v.tensor_tensor(part[:, :, :], agg[k][:, :, :], skip, ALU.subtract))
                att_link(v.tensor_tensor(part2[:, :, :], skip, tiled(w_skip[:, :]), ALU.mult))
                att_link(v.tensor_tensor(sq[:, :, :], agg[k][:, :, :], tiled(w_out[:, :]), ALU.mult))
                att_link(v.tensor_tensor(part2[:, :, :], part2[:, :, :], sq[:, :, :], ALU.add))
                v.tensor_reduce(dot[:, :], part2[:, :, :], AX, ALU.add).then_inc(s_dot, 1)

            def mix(n, k, r):
                need(v, s_beta, n)
                mix_link.item(n)
                mix_link(v.tensor_tensor(part[:, :, :], part[:, :, :], over(beta[:, :], BT), ALU.mult))
                mix_link(v.tensor_tensor(agg[k][:, :, :], agg[k][:, :, :], part[:, :, :], ALU.subtract))

            def centre(n, k, r):
                room(v, s_xn, n, NSLOTS)
                if layer < 2:
                    need(v, s_y, n)
                    other = pY[:, :].rearrange("p (t f) -> p t f", t=BT)
                else:
                    other = agg[k][:, :, :]
                    if layer == 2:
                        need(v, s_agg, n)
                v.tensor_tensor(y[k][:, :, :], other, now3(g["x"], n), ALU.add).then_inc(s_sum, 1)
                need(v, s_sum, n)
                if layer == 2:
                    v.tensor_tensor(y[k][:, :, :], y[k][:, :, :], tiled(wide["conv_b"][:, :]), ALU.add).then_inc(s_bias, 1)
                    need(v, s_bias, n)
                norm_link.item(n)
                norm_link(v.tensor_reduce(minus[:, :], y[k][:, :, :], AX, ALU.add))
                norm_link(v.tensor_scalar(minus[:, :], minus[:, :], -1.0 / D, None, ALU.mult))
                norm_link(v.tensor_tensor(y[k][:, :, :], y[k][:, :, :], over(minus[:, :], BT), ALU.add))
                norm_link(v.tensor_tensor(sq[:, :, :], y[k][:, :, :], y[k][:, :, :], ALU.mult))
                norm_link(v.tensor_reduce(var[:, :], sq[:, :, :], AX, ALU.add))
                v.tensor_scalar(var[:, :], var[:, :], 1.0 / D, EPS, ALU.mult, ALU.add).then_inc(s_var, 1)

            def scale(n, k, r):
                need(v, s_std, n)
                v.reciprocal(inv[:, :], std[:, :]).then_inc(s_inv, 1)
                need(v, s_inv, n)
                if last_layer:
                    stored(v, s_tout, k, r)
                else:
                    room(v, s_turnx, n, NSLOTS)
                room(v, s_keep, n, NSLOTS)
                v.tensor_tensor(xn[k][:, :, :], y[k][:, :, :], over(inv[:, :], BT), ALU.mult).then_inc(s_xn, 1)
            pipeline(v, NB, NSLOTS, {
                0: [(0, prep), (2, centre), (2, scale)],
                1: [(0, prep), (2, centre), (2, scale)],
                2: [(1, centre), (0, prep), (1, scale)],
                3: [(2, mix), (2, centre), (1, attend), (2, scale)]}[layer])

        @block.scalar
        def _(act):
            def load_xT(n, k, r):
                room(act, s_u if layer == 1 else s_y, n, NSLOTS)
                act.activation(xT[k][:, :], g["xT"][:, bass.ds(n * BE, BE)], ACT.Copy).then_inc(s_xs, 1)

            def copy_agg(n, k, r):
                need(act, s_turn, n)
                room(act, s_u if layer == 1 else s_y, n, NSLOTS)
                act.activation(aT[k][:, :], pA[:, :], ACT.Copy).then_inc(s_aT, 1)

            def relu(n, k, r):
                need(act, s_u, n)
                room(act, s_y, n, NSLOTS)
                act.activation(uT[k][:, :], pU[:, :], ACT.Relu, bias=g["c1"][:, 0:1]).then_inc(s_uT, 1)

            def gate(n, k, r):
                need(act, s_dot, n)
                act.activation(beta[:, :], dot[:, :], ACT.Sigmoid).then_inc(s_beta, 1)

            def root(n, k, r):
                need(act, s_var, n)
                act.activation(std[:, :], var[:, :], ACT.Sqrt).then_inc(s_std, 1)

            def keep(n, k, r):
                need(act, s_xn, n)
                act.sem_inc(s_ago, 1)
                act.activation(now3(g["x"], n), xn[k][:, :, :], ACT.Copy).then_inc(s_keep, 1)

            def copy_new(n, k, r):
                need(act, s_turnx, n)
                room(act, s_tab, n, NSLOTS)
                act.activation(xn_T[k][:, :], pX[:, :], ACT.Copy).then_inc(s_xnT, 1)

            def keep_T(n, k, r):
                need(act, s_xnT, n)
                act.sem_inc(s_ago, 1)
                act.activation(g["xT"][:, bass.ds(n * BE, BE)], xn_T[k][:, :], ACT.Copy)

            def copy_tables(n, k, r):
                need(act, s_tab, n)
                stored(act, s_tout, k, r)
                half = BE // tw if tw > D else BT
                for j in range(BT // half):
                    a = act.activation(tab[k][:, j * half:(j + 1) * half, 0:tw], pT[j][:, 0:half * tw].rearrange("p (t f) -> p t f", f=tw), ACT.Copy)
                if layer == 1:
                    act.activation(tab[k][:, :, HID:W2], pT[1][:, :].rearrange("p (t f) -> p t f", t=BT), ACT.Copy)
                    a = act.activation(now3(g["xt"], n), pT[1][:, :].rearrange("p (t f) -> p t f", t=BT), ACT.Copy)
                a.then_inc(s_tabc, 1)
                stored(act, s_scat, k, r, BT)
                act.activation(seed[k][:, :, 0:sw], pQ[:, :].rearrange("p (t f) -> p t f", t=BT)[:, :, 0:sw], ACT.Copy).then_inc(s_seedc, 1)
            if not last_layer and sw < D:
                act.wait_ge(s_zero, NSLOTS)
            pipeline(act, NB, NSLOTS, {
                0: [(0, load_xT), (5, copy_tables), (0, copy_agg), (3, copy_new), (2, root), (2, keep), (3, keep_T)],
                1: [(0, load_xT), (5, copy_tables), (0, copy_agg), (3, copy_new), (2, root), (0, relu), (2, keep), (3, keep_T)],
                2: [(4, copy_tables), (2, copy_new), (1, root), (1, keep), (2, keep_T)],
                3: [(0, load_xT), (2, root), (1, gate), (2, keep)]}[layer])


_WEIGHTS = ["L0_gnn_weight", "L1_gnn_W1", "L1_gnn_b1", "L1_gnn_W2", "L1_gnn_b2", "L1_gnn_U1", "L1_gnn_c1", "L1_gnn_U2", "L1_gnn_c2",
            "L2_gnn_mlp_w1", "L2_gnn_mlp_b1", "L2_gnn_mlp_w2", "L2_gnn_mlp_b2", "L2_gnn_conv_w", "L2_gnn_conv_b",
            "L3_gnn_Wq", "L3_gnn_bq", "L3_gnn_Wk", "L3_gnn_bk", "L3_gnn_Wv", "L3_gnn_bv", "L3_gnn_Wskip", "L3_gnn_bskip", "L3_gnn_Wbeta"]


def kernel(**inputs):
    import numpy as _np
    import concourse.bacc as _bacc
    from concourse import mybir as _mybir
    from concourse.bass_utils import run_bass_kernel_spmd as _run

    nc = _bacc.Bacc("TRN2", target_bir_lowering=False, num_devices=1)
    x = _np.zeros((NP, D), _np.float32)
    x[:N] = inputs["x"]
    src = _np.zeros((EP + SLOTS * BE,), _np.int32)
    src[:E] = inputs["src"]
    dst = _np.full((EP + 2,), N, _np.int32)
    dst[0] = -1
    dst[1:E + 1] = inputs["dst"]
    dst[EP + 1] = N + 1
    weight = _np.zeros((EP,), _np.float32)
    weight[:E] = inputs["edge_weight"]
    arrays = {
        "x": x,
        "src": _np.ascontiguousarray(src.reshape(-1, P).T),
        "src_row": src[:EP],
        "dst": dst,
        "dst_lane": _np.ascontiguousarray(dst[1:EP + 1].reshape(TILES, P).T),
        "weight": _np.ascontiguousarray(weight.reshape(TILES, P).T),
    }
    for name in _WEIGHTS:
        arrays[name] = _np.ascontiguousarray(inputs[name])
    d = {n: nc.dram_tensor("in_" + n, a.shape, _mybir.dt.from_np(a.dtype), kind="ExternalInput").ap() for n, a in arrays.items()}
    out = nc.dram_tensor("out_0", (N, D), F32, kind="ExternalOutput").ap()
    build(nc, d, out)
    r = _run(nc, [{"in_" + n: a for n, a in arrays.items()}], core_ids=[0])
    return r.results[0]["out_0"]
```
